# Optimizing a Trainium2 kernel written in Bass

```python
import numpy as np
import jax
import jax.numpy as jnp

def _softmax(x, axis=-1):
    return jax.nn.softmax(x, axis=axis)

def _gelu(x):
    return jax.nn.gelu(x, approximate=True)

def _silu(x):
    return jax.nn.silu(x)

def _sigmoid(x):
    return jax.nn.sigmoid(x)

def _layernorm(x, axis=-1, eps=1e-05):
    m = jnp.mean(x, axis=axis, keepdims=True)
    v = jnp.var(x, axis=axis, keepdims=True)
    return (x - m) / jnp.sqrt(v + eps)

def _scatter_add(tgt, idx, src, axis=0):
    return tgt.at[idx].add(src)

def _segment_sum(src, seg, n):
    return jax.ops.segment_sum(src, seg, n)
kernel_name = 'mk_xattn_seq_d4_seqx_r4_b4bd35'

def setup_inputs(seed: int=0):
    np.random.seed(seed)
    _w = jnp.asarray

    def _rec_inputs():
        import jax
        import jax.numpy as jnp
        _rk = jax.random.key(seed)
        x = 7.22e-05 + 1 * jax.random.normal(jax.random.fold_in(_rk, 1), (4, 512, 512), jnp.float32)
        _lenS = 512 - jax.random.randint(jax.random.fold_in(_rk, 7), (4,), 0, max(1, 512 // 4) + 1, jnp.int32)
        _lenS2 = 512 - jax.random.randint(jax.random.fold_in(_rk, 8), (4,), 0, max(1, 512 // 4) + 1, jnp.int32)
        _ctx_2048P = jax.random.normal(jax.random.fold_in(_rk, 11), (4, 16, 512), jnp.float32)
        _ctx_2048c = jax.random.dirichlet(jax.random.fold_in(_rk, 511), 0.3 * jnp.ones((16,), jnp.float32), (4, 512))
        _ctx_2048t = jnp.einsum('bsk,bkd->bsd', _ctx_2048c, _ctx_2048P)
        _ctx_2048t = _ctx_2048t * jax.lax.rsqrt(jnp.mean(jnp.square(_ctx_2048t)) + 1e-12) * 0.953939
        ctx_2048 = 4.13588e-05 + 0.999923 * (_ctx_2048t + 0.3 * jax.random.normal(jax.random.fold_in(_rk, 611), (4, 512, 512), jnp.float32))
        _validS = jnp.arange(512)[None, :] < _lenS[:, None]
        _validS2 = jnp.arange(512)[None, :] < _lenS2[:, None]
        _causal = jnp.tril(jnp.ones((512, 512), dtype=bool))
        mask_Bx1xSxS2_ff0 = jnp.where(jnp.ones((4, 1, 512, 512), dtype=bool), 0.0, -1000000000.0).astype(jnp.float32)
        mask_BxS2_ik0 = jnp.where(jnp.broadcast_to(_validS2[:, :], (4, 512)), 0, 1).astype(jnp.int32)
        return (x, ctx_2048, mask_Bx1xSxS2_ff0, mask_BxS2_ik0)
    x, ctx_2048, mask_Bx1xSxS2_ff0, mask_BxS2_ik0 = _rec_inputs()

    def _L0_xattn_setup():
        import jax, jax.numpy as jnp
        import numpy as np
        H = 512
        NH = 32
        KVH = 8
        HD = H // NH
        GROUPS = NH // KVH
        EPS = 1e-06
        B, L, S = (4, 256, 256)

        def _gqa_forward(hidden_state, encoder_hidden_state, encoder_attention_mask, Wq, bq, Wk, bk, Wv, bv, Wo, bo, gamma, beta):
            b, l, _ = hidden_state.shape
            s = encoder_hidden_state.shape[1]
            q = hidden_state @ Wq + bq
            k = encoder_hidden_state @ Wk + bk
            v = encoder_hidden_state @ Wv + bv
            q = q.reshape(b, l, KVH, GROUPS, HD).transpose(0, 2, 3, 1, 4)
            k = k.reshape(b, s, KVH, HD).transpose(0, 2, 1, 3)
            v = v.reshape(b, s, KVH, HD).transpose(0, 2, 1, 3)
            scale = 1.0 / jnp.sqrt(jnp.asarray(HD, q.dtype))
            scores = jnp.einsum('bkgld,bksd->bkgls', q, k) * scale
            scores = scores + encoder_attention_mask[:, :, None, :, :]
            attn = jax.nn.softmax(scores, axis=-1)
            out = jnp.einsum('bkgls,bksd->bkgld', attn, v)
            out = out.transpose(0, 3, 1, 2, 4).reshape(b, l, H)
            out = out @ Wo + bo
            x = out + hidden_state
            mu = jnp.mean(x, axis=-1, keepdims=True)
            var = jnp.var(x, axis=-1, keepdims=True)
            return (x - mu) * jax.lax.rsqrt(var + EPS) * gamma + beta
        key = jax.random.key(seed)
        ks = jax.random.split(key, 12)
        sd = 0.02
        return {'hidden_state': jax.random.normal(ks[0], (B, L, H), jnp.float32), 'encoder_hidden_state': jax.random.normal(ks[1], (B, S, H), jnp.float32), 'encoder_attention_mask': jnp.zeros((B, 1, L, S), jnp.float32), 'Wq': jax.random.normal(ks[2], (H, H), jnp.float32) * sd, 'bq': jnp.zeros((H,), jnp.float32), 'Wk': jax.random.normal(ks[3], (H, KVH * HD), jnp.float32) * sd, 'bk': jnp.zeros((KVH * HD,), jnp.float32), 'Wv': jax.random.normal(ks[4], (H, KVH * HD), jnp.float32) * sd, 'bv': jnp.zeros((KVH * HD,), jnp.float32), 'Wo': jax.random.normal(ks[5], (H, H), jnp.float32) * sd, 'bo': jnp.zeros((H,), jnp.float32), 'gamma': jnp.ones((H,), jnp.float32), 'beta': jnp.zeros((H,), jnp.float32)}
    _L0_xattn_all = _L0_xattn_setup()
    _L0_xattn_in = {k: v for k, v in _L0_xattn_all.items() if k in ('Wq', 'bq', 'Wk', 'bk', 'Wv', 'bv', 'Wo', 'bo', 'gamma', 'beta')}
    del _L0_xattn_all

    def _L1_xattn_setup():
        import jax, jax.numpy as jnp
        import numpy as np
        N_HEAD = 32
        EPS = 1e-05

        def _ln(x, w, b):
            m = jnp.mean(x, axis=-1, keepdims=True)
            v = jnp.mean((x - m) ** 2, axis=-1, keepdims=True)
            return (x - m) * jax.lax.rsqrt(v + EPS) * w + b

        def _forward(x, state, i, ln1_w, ln1_b, ln2_w, ln2_b, maa_x, maa_w, maa_k, maa_v, maa_r, maa_g, maa_w1, maa_w2, time_decay, decay_w1, decay_w2, faaaa, Wr, Wk, Wv, Wg, Wo, gn_w, gn_b, fmaa_k, fmaa_r, fWk, fWr, fWv):
            B, L, C = x.shape
            H = N_HEAD
            S = C // H
            i0 = (2 + S) * i
            xa = _ln(x, ln1_w, ln1_b)
            sx = jnp.concatenate([state[:, i0 + 1][:, None], xa[:, :-1]], axis=1) - xa
            xxx = xa + sx * maa_x
            t = jnp.tanh(xxx @ maa_w1).reshape(B, L, 5, -1)
            m = jnp.einsum('blfd,fdc->blfc', t, maa_w2)
            mw, mk, mv, mr, mg = (m[:, :, j] for j in range(5))
            xw = xa + sx * (maa_w + mw)
            xk = xa + sx * (maa_k + mk)
            xv = xa + sx * (maa_v + mv)
            xr = xa + sx * (maa_r + mr)
            xg = xa + sx * (maa_g + mg)
            w = time_decay + jnp.tanh(xw @ decay_w1) @ decay_w2
            w = jnp.exp(-jnp.exp(w)).reshape(B, L, H, S)
            r = (xr @ Wr.T).reshape(B, L, H, S)
            k = (xk @ Wk.T).reshape(B, L, H, S)
            v = (xv @ Wv.T).reshape(B, L, H, S)
            g = jax.nn.silu(xg @ Wg.T)
            s0 = state[:, i0 + 2:i0 + 2 + S].reshape(B, H, S, S)

            def step(s, inp):
                k_l, v_l, w_l, r_l = inp
                a = k_l[..., :, None] * v_l[..., None, :]
                out = jnp.einsum('bhs,bhst->bht', r_l, faaaa * a + s)
                s_new = a + w_l[..., None] * s
                return (s_new, out)
            seq = tuple((z.transpose(1, 0, 2, 3) for z in (k, v, w, r)))
            _, outs = jax.lax.scan(step, s0, seq)
            y = outs.transpose(1, 0, 2, 3)
            gm = jnp.mean(y, axis=-1, keepdims=True)
            gv = jnp.mean((y - gm) ** 2, axis=-1, keepdims=True)
            y = ((y - gm) * jax.lax.rsqrt(gv + EPS)).reshape(B, L, C) * gn_w + gn_b
            x = x + y * g @ Wo.T
            xc = _ln(x, ln2_w, ln2_b)
            sxc = jnp.concatenate([state[:, i0][:, None], xc[:, :-1]], axis=1) - xc
            xk2 = xc + sxc * fmaa_k
            xr2 = xc + sxc * fmaa_r
            rr = jax.nn.sigmoid(xr2 @ fWr.T)
            kk = jnp.square(jax.nn.relu(xk2 @ fWk.T))
            x = x + rr * (kk @ fWv.T)
            return x
        key = jax.random.key(seed)
        B, L, C, H = (8, 128, 512, N_HEAD)
        S = C // H
        DM, DD = (32, 64)
        ks = jax.random.split(key, 32)
        n = lambda k, shp, s=1.0: jax.random.normal(k, shp, dtype=jnp.float32) * s
        u = lambda k, shp: jax.random.uniform(k, shp, dtype=jnp.float32)
        inp = {'x': n(ks[0], (B, L, C)), 'state': n(ks[1], (B, 2 + S, C), 0.1), 'i': 0, 'ln1_w': jnp.ones((C,), jnp.float32), 'ln1_b': jnp.zeros((C,), jnp.float32), 'ln2_w': jnp.ones((C,), jnp.float32), 'ln2_b': jnp.zeros((C,), jnp.float32), 'maa_x': u(ks[2], (C,)), 'maa_w': u(ks[3], (C,)), 'maa_k': u(ks[4], (C,)), 'maa_v': u(ks[5], (C,)), 'maa_r': u(ks[6], (C,)), 'maa_g': u(ks[7], (C,)), 'maa_w1': n(ks[8], (C, 5 * DM), 0.02), 'maa_w2': n(ks[9], (5, DM, C), 0.02), 'time_decay': n(ks[10], (C,), 0.5), 'decay_w1': n(ks[11], (C, DD), 0.02), 'decay_w2': n(ks[12], (DD, C), 0.02), 'faaaa': n(ks[13], (H, S, 1), 0.1), 'Wr': n(ks[14], (C, C), 0.02), 'Wk': n(ks[15], (C, C), 0.02), 'Wv': n(ks[16], (C, C), 0.02), 'Wg': n(ks[17], (C, C), 0.02), 'Wo': n(ks[18], (C, C), 0.02), 'gn_w': jnp.ones((C,), jnp.float32), 'gn_b': jnp.zeros((C,), jnp.float32), 'fmaa_k': u(ks[19], (C,)), 'fmaa_r': u(ks[20], (C,)), 'fWk': n(ks[21], (C, C), 0.02), 'fWr': n(ks[22], (C, C), 0.02), 'fWv': n(ks[23], (C, C), 0.02)}
        return inp
    _L1_xattn_all = _L1_xattn_setup()
    _L1_xattn_in = {k: v for k, v in _L1_xattn_all.items() if k in ('ln1_w', 'ln1_b', 'ln2_w', 'ln2_b', 'maa_x', 'maa_w', 'maa_k', 'maa_v', 'maa_r', 'maa_g', 'maa_w1', 'maa_w2', 'time_decay', 'decay_w1', 'decay_w2', 'faaaa', 'Wr', 'Wk', 'Wv', 'Wg', 'Wo', 'gn_w', 'gn_b', 'fmaa_k', 'fmaa_r', 'fWk', 'fWr', 'fWv')}
    del _L1_xattn_all

    def _L2_xattn_setup():
        import jax, jax.numpy as jnp
        import numpy as np
        B, L, E, H = (4, 128, 512, 32)
        S = E // H
        EXTRA_MAA, EXTRA_DECAY = (32, 64)
        EPS = 1e-05

        def _ln(x, w, b):
            m = jnp.mean(x, axis=-1, keepdims=True)
            v = jnp.mean((x - m) ** 2, axis=-1, keepdims=True)
            return (x - m) * jax.lax.rsqrt(v + EPS) * w + b

        def _token_shift(xn, prev_row):
            first = (prev_row - xn[:, 0])[:, None]
            rest = xn[:, :-1] - xn[:, 1:]
            return jnp.concatenate([first, rest], axis=1)
        key = jax.random.key(seed)
        ks = jax.random.split(key, 24)
        rn = lambda k, shp, s=1.0: jax.random.normal(k, shp, dtype=jnp.float32) * s
        return dict(x=rn(ks[0], (B, L, E)), state=rn(ks[1], (B, 2 + S, E), 0.1), ln1_w=jnp.ones((E,), jnp.float32), ln1_b=jnp.zeros((E,), jnp.float32), ln2_w=jnp.ones((E,), jnp.float32), ln2_b=jnp.zeros((E,), jnp.float32), maa_x=rn(ks[2], (E,), 0.02), maa_w1=rn(ks[3], (E, 5 * EXTRA_MAA), 0.02), maa_w2=rn(ks[4], (5, EXTRA_MAA, E), 0.02), maa_stack=rn(ks[5], (5, E), 0.02), time_decay=rn(ks[6], (E,), 0.5), decay_w1=rn(ks[7], (E, EXTRA_DECAY), 0.02), decay_w2=rn(ks[8], (EXTRA_DECAY, E), 0.02), faaaa=rn(ks[9], (H, S), 0.1), Wr=rn(ks[10], (E, E), 0.02), Wk=rn(ks[11], (E, E), 0.02), Wv=rn(ks[12], (E, E), 0.02), Wg=rn(ks[13], (E, E), 0.02), Wo=rn(ks[14], (E, E), 0.02), gn_w=jnp.ones((E,), jnp.float32), gn_b=jnp.zeros((E,), jnp.float32), ffn_maa_k=rn(ks[15], (E,), 0.02), ffn_maa_r=rn(ks[16], (E,), 0.02), ffn_Wk=rn(ks[17], (E, E), 0.02), ffn_Wr=rn(ks[18], (E, E), 0.02), ffn_Wv=rn(ks[19], (E, E), 0.02), i=0)
    _L2_xattn_all = _L2_xattn_setup()
    _L2_xattn_in = {k: v for k, v in _L2_xattn_all.items() if k in ('ln1_w', 'ln1_b', 'ln2_w', 'ln2_b', 'maa_x', 'maa_w1', 'maa_w2', 'maa_stack', 'time_decay', 'decay_w1', 'decay_w2', 'faaaa', 'Wr', 'Wk', 'Wv', 'Wg', 'Wo', 'gn_w', 'gn_b', 'ffn_maa_k', 'ffn_maa_r', 'ffn_Wk', 'ffn_Wr', 'ffn_Wv')}
    del _L2_xattn_all

    def _L3_xattn_setup():
        import jax, jax.numpy as jnp
        import numpy as np
        B, P, K, H, NH = (4, 512, 64, 512, 16)
        DH = H // NH
        EPS = 1e-06

        def rmsnorm(x, w):
            var = jnp.mean(jnp.square(x), axis=-1, keepdims=True)
            return x * jax.lax.rsqrt(var + EPS) * w
        key = jax.random.key(seed)
        ks = jax.random.split(key, 12)
        s = 0.02
        return {'x': jax.random.normal(ks[0], (B, P, H), jnp.float32), 'latents': jax.random.normal(ks[1], (B, K, H), jnp.float32), 'attention_mask': jax.random.randint(ks[2], (B, P), 0, 2, jnp.int32), 'q_w': s * jax.random.normal(ks[3], (H, H), jnp.float32), 'q_b': jnp.zeros((H,), jnp.float32), 'kv_w': s * jax.random.normal(ks[4], (H, 2 * H), jnp.float32), 'kv_b': jnp.zeros((2 * H,), jnp.float32), 'out_w': s * jax.random.normal(ks[5], (H, H), jnp.float32), 'out_b': jnp.zeros((H,), jnp.float32), 'postnorm_w': jnp.ones((H,), jnp.float32), 'mlp_w1': s * jax.random.normal(ks[6], (H, 4 * H), jnp.float32), 'mlp_b1': jnp.zeros((4 * H,), jnp.float32), 'mlp_w2': s * jax.random.normal(ks[7], (4 * H, H), jnp.float32), 'mlp_b2': jnp.zeros((H,), jnp.float32)}
    _L3_xattn_all = _L3_xattn_setup()
    _L3_xattn_in = {k: v for k, v in _L3_xattn_all.items() if k in ('q_w', 'q_b', 'kv_w', 'kv_b', 'out_w', 'out_b', 'postnorm_w', 'mlp_w1', 'mlp_b1', 'mlp_w2', 'mlp_b2')}
    del _L3_xattn_all
    return {'x': x, 'ctx_2048': ctx_2048, 'mask_Bx1xSxS2_ff0': mask_Bx1xSxS2_ff0, 'mask_BxS2_ik0': mask_BxS2_ik0, 'L0_xattn_Wq': _L0_xattn_in['Wq'], 'L0_xattn_bq': _L0_xattn_in['bq'], 'L0_xattn_Wk': _L0_xattn_in['Wk'], 'L0_xattn_bk': _L0_xattn_in['bk'], 'L0_xattn_Wv': _L0_xattn_in['Wv'], 'L0_xattn_bv': _L0_xattn_in['bv'], 'L0_xattn_Wo': _L0_xattn_in['Wo'], 'L0_xattn_bo': _L0_xattn_in['bo'], 'L0_xattn_gamma': _L0_xattn_in['gamma'], 'L0_xattn_beta': _L0_xattn_in['beta'], 'L1_xattn_ln1_w': _L1_xattn_in['ln1_w'], 'L1_xattn_ln1_b': _L1_xattn_in['ln1_b'], 'L1_xattn_ln2_w': _L1_xattn_in['ln2_w'], 'L1_xattn_ln2_b': _L1_xattn_in['ln2_b'], 'L1_xattn_maa_x': _L1_xattn_in['maa_x'], 'L1_xattn_maa_w': _L1_xattn_in['maa_w'], 'L1_xattn_maa_k': _L1_xattn_in['maa_k'], 'L1_xattn_maa_v': _L1_xattn_in['maa_v'], 'L1_xattn_maa_r': _L1_xattn_in['maa_r'], 'L1_xattn_maa_g': _L1_xattn_in['maa_g'], 'L1_xattn_maa_w1': _L1_xattn_in['maa_w1'], 'L1_xattn_maa_w2': _L1_xattn_in['maa_w2'], 'L1_xattn_time_decay': _L1_xattn_in['time_decay'], 'L1_xattn_decay_w1': _L1_xattn_in['decay_w1'], 'L1_xattn_decay_w2': _L1_xattn_in['decay_w2'], 'L1_xattn_faaaa': _L1_xattn_in['faaaa'], 'L1_xattn_Wr': _L1_xattn_in['Wr'], 'L1_xattn_Wk': _L1_xattn_in['Wk'], 'L1_xattn_Wv': _L1_xattn_in['Wv'], 'L1_xattn_Wg': _L1_xattn_in['Wg'], 'L1_xattn_Wo': _L1_xattn_in['Wo'], 'L1_xattn_gn_w': _L1_xattn_in['gn_w'], 'L1_xattn_gn_b': _L1_xattn_in['gn_b'], 'L1_xattn_fmaa_k': _L1_xattn_in['fmaa_k'], 'L1_xattn_fmaa_r': _L1_xattn_in['fmaa_r'], 'L1_xattn_fWk': _L1_xattn_in['fWk'], 'L1_xattn_fWr': _L1_xattn_in['fWr'], 'L1_xattn_fWv': _L1_xattn_in['fWv'], 'L2_xattn_ln1_w': _L2_xattn_in['ln1_w'], 'L2_xattn_ln1_b': _L2_xattn_in['ln1_b'], 'L2_xattn_ln2_w': _L2_xattn_in['ln2_w'], 'L2_xattn_ln2_b': _L2_xattn_in['ln2_b'], 'L2_xattn_maa_x': _L2_xattn_in['maa_x'], 'L2_xattn_maa_w1': _L2_xattn_in['maa_w1'], 'L2_xattn_maa_w2': _L2_xattn_in['maa_w2'], 'L2_xattn_maa_stack': _L2_xattn_in['maa_stack'], 'L2_xattn_time_decay': _L2_xattn_in['time_decay'], 'L2_xattn_decay_w1': _L2_xattn_in['decay_w1'], 'L2_xattn_decay_w2': _L2_xattn_in['decay_w2'], 'L2_xattn_faaaa': _L2_xattn_in['faaaa'], 'L2_xattn_Wr': _L2_xattn_in['Wr'], 'L2_xattn_Wk': _L2_xattn_in['Wk'], 'L2_xattn_Wv': _L2_xattn_in['Wv'], 'L2_xattn_Wg': _L2_xattn_in['Wg'], 'L2_xattn_Wo': _L2_xattn_in['Wo'], 'L2_xattn_gn_w': _L2_xattn_in['gn_w'], 'L2_xattn_gn_b': _L2_xattn_in['gn_b'], 'L2_xattn_ffn_maa_k': _L2_xattn_in['ffn_maa_k'], 'L2_xattn_ffn_maa_r': _L2_xattn_in['ffn_maa_r'], 'L2_xattn_ffn_Wk': _L2_xattn_in['ffn_Wk'], 'L2_xattn_ffn_Wr': _L2_xattn_in['ffn_Wr'], 'L2_xattn_ffn_Wv': _L2_xattn_in['ffn_Wv'], 'L3_xattn_q_w': _L3_xattn_in['q_w'], 'L3_xattn_q_b': _L3_xattn_in['q_b'], 'L3_xattn_kv_w': _L3_xattn_in['kv_w'], 'L3_xattn_kv_b': _L3_xattn_in['kv_b'], 'L3_xattn_out_w': _L3_xattn_in['out_w'], 'L3_xattn_out_b': _L3_xattn_in['out_b'], 'L3_xattn_postnorm_w': _L3_xattn_in['postnorm_w'], 'L3_xattn_mlp_w1': _L3_xattn_in['mlp_w1'], 'L3_xattn_mlp_b1': _L3_xattn_in['mlp_b1'], 'L3_xattn_mlp_w2': _L3_xattn_in['mlp_w2'], 'L3_xattn_mlp_b2': _L3_xattn_in['mlp_b2']}

def reference(x, ctx_2048, mask_Bx1xSxS2_ff0, mask_BxS2_ik0, L0_xattn_Wq, L0_xattn_bq, L0_xattn_Wk, L0_xattn_bk, L0_xattn_Wv, L0_xattn_bv, L0_xattn_Wo, L0_xattn_bo, L0_xattn_gamma, L0_xattn_beta, L1_xattn_ln1_w, L1_xattn_ln1_b, L1_xattn_ln2_w, L1_xattn_ln2_b, L1_xattn_maa_x, L1_xattn_maa_w, L1_xattn_maa_k, L1_xattn_maa_v, L1_xattn_maa_r, L1_xattn_maa_g, L1_xattn_maa_w1, L1_xattn_maa_w2, L1_xattn_time_decay, L1_xattn_decay_w1, L1_xattn_decay_w2, L1_xattn_faaaa, L1_xattn_Wr, L1_xattn_Wk, L1_xattn_Wv, L1_xattn_Wg, L1_xattn_Wo, L1_xattn_gn_w, L1_xattn_gn_b, L1_xattn_fmaa_k, L1_xattn_fmaa_r, L1_xattn_fWk, L1_xattn_fWr, L1_xattn_fWv, L2_xattn_ln1_w, L2_xattn_ln1_b, L2_xattn_ln2_w, L2_xattn_ln2_b, L2_xattn_maa_x, L2_xattn_maa_w1, L2_xattn_maa_w2, L2_xattn_maa_stack, L2_xattn_time_decay, L2_xattn_decay_w1, L2_xattn_decay_w2, L2_xattn_faaaa, L2_xattn_Wr, L2_xattn_Wk, L2_xattn_Wv, L2_xattn_Wg, L2_xattn_Wo, L2_xattn_gn_w, L2_xattn_gn_b, L2_xattn_ffn_maa_k, L2_xattn_ffn_maa_r, L2_xattn_ffn_Wk, L2_xattn_ffn_Wr, L2_xattn_ffn_Wv, L3_xattn_q_w, L3_xattn_q_b, L3_xattn_kv_w, L3_xattn_kv_b, L3_xattn_out_w, L3_xattn_out_b, L3_xattn_postnorm_w, L3_xattn_mlp_w1, L3_xattn_mlp_b1, L3_xattn_mlp_w2, L3_xattn_mlp_b2):
    import jax
    import jax.numpy as jnp

    def _L0_xattn_ref(hidden_state, encoder_hidden_state, encoder_attention_mask, Wq, bq, Wk, bk, Wv, bv, Wo, bo, gamma, beta):
        import jax, jax.numpy as jnp
        import numpy as np
        H = 512
        NH = 32
        KVH = 8
        HD = H // NH
        GROUPS = NH // KVH
        EPS = 1e-06
        B, L, S = (4, 256, 256)

        def _gqa_forward(hidden_state, encoder_hidden_state, encoder_attention_mask, Wq, bq, Wk, bk, Wv, bv, Wo, bo, gamma, beta):
            b, l, _ = hidden_state.shape
            s = encoder_hidden_state.shape[1]
            q = hidden_state @ Wq + bq
            k = encoder_hidden_state @ Wk + bk
            v = encoder_hidden_state @ Wv + bv
            q = q.reshape(b, l, KVH, GROUPS, HD).transpose(0, 2, 3, 1, 4)
            k = k.reshape(b, s, KVH, HD).transpose(0, 2, 1, 3)
            v = v.reshape(b, s, KVH, HD).transpose(0, 2, 1, 3)
            scale = 1.0 / jnp.sqrt(jnp.asarray(HD, q.dtype))
            scores = jnp.einsum('bkgld,bksd->bkgls', q, k) * scale
            scores = scores + encoder_attention_mask[:, :, None, :, :]
            attn = jax.nn.softmax(scores, axis=-1)
            out = jnp.einsum('bkgls,bksd->bkgld', attn, v)
            out = out.transpose(0, 3, 1, 2, 4).reshape(b, l, H)
            out = out @ Wo + bo
            x = out + hidden_state
            mu = jnp.mean(x, axis=-1, keepdims=True)
            var = jnp.var(x, axis=-1, keepdims=True)
            return (x - mu) * jax.lax.rsqrt(var + EPS) * gamma + beta
        return _gqa_forward(hidden_state, encoder_hidden_state, encoder_attention_mask, Wq, bq, Wk, bk, Wv, bv, Wo, bo, gamma, beta)

    def _L1_xattn_ref(x, state, i, ln1_w, ln1_b, ln2_w, ln2_b, maa_x, maa_w, maa_k, maa_v, maa_r, maa_g, maa_w1, maa_w2, time_decay, decay_w1, decay_w2, faaaa, Wr, Wk, Wv, Wg, Wo, gn_w, gn_b, fmaa_k, fmaa_r, fWk, fWr, fWv):
        import jax, jax.numpy as jnp
        import numpy as np
        N_HEAD = 32
        EPS = 1e-05

        def _ln(x, w, b):
            m = jnp.mean(x, axis=-1, keepdims=True)
            v = jnp.mean((x - m) ** 2, axis=-1, keepdims=True)
            return (x - m) * jax.lax.rsqrt(v + EPS) * w + b

        def _forward(x, state, i, ln1_w, ln1_b, ln2_w, ln2_b, maa_x, maa_w, maa_k, maa_v, maa_r, maa_g, maa_w1, maa_w2, time_decay, decay_w1, decay_w2, faaaa, Wr, Wk, Wv, Wg, Wo, gn_w, gn_b, fmaa_k, fmaa_r, fWk, fWr, fWv):
            B, L, C = x.shape
            H = N_HEAD
            S = C // H
            i0 = (2 + S) * i
            xa = _ln(x, ln1_w, ln1_b)
            sx = jnp.concatenate([state[:, i0 + 1][:, None], xa[:, :-1]], axis=1) - xa
            xxx = xa + sx * maa_x
            t = jnp.tanh(xxx @ maa_w1).reshape(B, L, 5, -1)
            m = jnp.einsum('blfd,fdc->blfc', t, maa_w2)
            mw, mk, mv, mr, mg = (m[:, :, j] for j in range(5))
            xw = xa + sx * (maa_w + mw)
            xk = xa + sx * (maa_k + mk)
            xv = xa + sx * (maa_v + mv)
            xr = xa + sx * (maa_r + mr)
            xg = xa + sx * (maa_g + mg)
            w = time_decay + jnp.tanh(xw @ decay_w1) @ decay_w2
            w = jnp.exp(-jnp.exp(w)).reshape(B, L, H, S)
            r = (xr @ Wr.T).reshape(B, L, H, S)
            k = (xk @ Wk.T).reshape(B, L, H, S)
            v = (xv @ Wv.T).reshape(B, L, H, S)
            g = jax.nn.silu(xg @ Wg.T)
            s0 = state[:, i0 + 2:i0 + 2 + S].reshape(B, H, S, S)

            def step(s, inp):
                k_l, v_l, w_l, r_l = inp
                a = k_l[..., :, None] * v_l[..., None, :]
                out = jnp.einsum('bhs,bhst->bht', r_l, faaaa * a + s)
                s_new = a + w_l[..., None] * s
                return (s_new, out)
            seq = tuple((z.transpose(1, 0, 2, 3) for z in (k, v, w, r)))
            _, outs = jax.lax.scan(step, s0, seq)
            y = outs.transpose(1, 0, 2, 3)
            gm = jnp.mean(y, axis=-1, keepdims=True)
            gv = jnp.mean((y - gm) ** 2, axis=-1, keepdims=True)
            y = ((y - gm) * jax.lax.rsqrt(gv + EPS)).reshape(B, L, C) * gn_w + gn_b
            x = x + y * g @ Wo.T
            xc = _ln(x, ln2_w, ln2_b)
            sxc = jnp.concatenate([state[:, i0][:, None], xc[:, :-1]], axis=1) - xc
            xk2 = xc + sxc * fmaa_k
            xr2 = xc + sxc * fmaa_r
            rr = jax.nn.sigmoid(xr2 @ fWr.T)
            kk = jnp.square(jax.nn.relu(xk2 @ fWk.T))
            x = x + rr * (kk @ fWv.T)
            return x
        return _forward(x, state, i, ln1_w, ln1_b, ln2_w, ln2_b, maa_x, maa_w, maa_k, maa_v, maa_r, maa_g, maa_w1, maa_w2, time_decay, decay_w1, decay_w2, faaaa, Wr, Wk, Wv, Wg, Wo, gn_w, gn_b, fmaa_k, fmaa_r, fWk, fWr, fWv)

    def _L2_xattn_ref(x, state, ln1_w, ln1_b, ln2_w, ln2_b, maa_x, maa_w1, maa_w2, maa_stack, time_decay, decay_w1, decay_w2, faaaa, Wr, Wk, Wv, Wg, Wo, gn_w, gn_b, ffn_maa_k, ffn_maa_r, ffn_Wk, ffn_Wr, ffn_Wv, i):
        import jax, jax.numpy as jnp
        import numpy as np
        B, L, E, H = (4, 128, 512, 32)
        S = E // H
        EXTRA_MAA, EXTRA_DECAY = (32, 64)
        EPS = 1e-05

        def _ln(x, w, b):
            m = jnp.mean(x, axis=-1, keepdims=True)
            v = jnp.mean((x - m) ** 2, axis=-1, keepdims=True)
            return (x - m) * jax.lax.rsqrt(v + EPS) * w + b

        def _token_shift(xn, prev_row):
            first = (prev_row - xn[:, 0])[:, None]
            rest = xn[:, :-1] - xn[:, 1:]
            return jnp.concatenate([first, rest], axis=1)
        b, l = (x.shape[0], x.shape[1])
        i0 = (2 + S) * i + 0
        i1 = (2 + S) * i + 1
        xn = _ln(x, ln1_w, ln1_b)
        sx = _token_shift(xn, state[:, i1])
        xxx = jnp.tanh((xn + sx * maa_x) @ maa_w1).reshape(b, l, 5, 1, EXTRA_MAA)
        xxx = jnp.matmul(xxx, maa_w2).reshape(b, l, 5, E)
        x5 = xn[:, :, None] + sx[:, :, None] * (maa_stack + xxx)
        w = jnp.exp(-jnp.exp(time_decay + jnp.tanh(x5[:, :, 1] @ decay_w1) @ decay_w2))
        w = w.reshape(b, l, H, S)
        r = (x5[:, :, 3] @ Wr.T).reshape(b, l, H, S)
        k = (x5[:, :, 0] @ Wk.T).reshape(b, l, H, S)
        v = (x5[:, :, 2] @ Wv.T).reshape(b, l, H, S)
        g = jax.nn.silu(x5[:, :, 4] @ Wg.T)
        s0 = state[:, (2 + S) * i + 2:(2 + S) * (i + 1)].reshape(b, H, S, S)
        u = faaaa[None, :, :, None]

        def step(s, rkvw):
            r_t, k_t, v_t, w_t = rkvw
            a = k_t[:, :, :, None] * v_t[:, :, None, :]
            out = jnp.einsum('bhk,bhkd->bhd', r_t, u * a + s)
            return (a + w_t[:, :, :, None] * s, out)
        xs = tuple((jnp.moveaxis(t, 1, 0) for t in (r, k, v, w)))
        _, outs = jax.lax.scan(step, s0, xs)
        att = jnp.moveaxis(outs, 0, 1).reshape(b, l, E)
        a4 = att.reshape(b, l, H, S)
        m = jnp.mean(a4, axis=-1, keepdims=True)
        var = jnp.mean((a4 - m) ** 2, axis=-1, keepdims=True)
        att = ((a4 - m) * jax.lax.rsqrt(var + EPS)).reshape(b, l, E) * gn_w + gn_b
        x = x + att * g @ Wo.T
        xn2 = _ln(x, ln2_w, ln2_b)
        sx2 = _token_shift(xn2, state[:, i0])
        xk = xn2 + sx2 * ffn_maa_k
        xr = xn2 + sx2 * ffn_maa_r
        rr = jax.nn.sigmoid(xr @ ffn_Wr.T)
        kk = jnp.square(jax.nn.relu(xk @ ffn_Wk.T))
        x = x + rr * (kk @ ffn_Wv.T)
        return x

    def _L3_xattn_ref(x, latents, attention_mask, q_w, q_b, kv_w, kv_b, out_w, out_b, postnorm_w, mlp_w1, mlp_b1, mlp_w2, mlp_b2):
        import jax, jax.numpy as jnp
        import numpy as np
        B, P, K, H, NH = (4, 512, 64, 512, 16)
        DH = H // NH
        EPS = 1e-06

        def rmsnorm(x, w):
            var = jnp.mean(jnp.square(x), axis=-1, keepdims=True)
            return x * jax.lax.rsqrt(var + EPS) * w
        b, p, _ = x.shape
        k_len = latents.shape[1]
        residual = latents
        h = jnp.concatenate([x, latents], axis=1)
        q = (latents @ q_w + q_b).reshape(b, k_len, NH, DH)
        kv = (h @ kv_w + kv_b).reshape(b, p + k_len, NH, DH, 2)
        kmat, v = (kv[..., 0], kv[..., 1])
        attn = jnp.einsum('bkhd,bnhd->bhkn', q, kmat) / DH
        full_mask = jnp.concatenate([attention_mask.astype(bool), jnp.ones((b, k_len), bool)], axis=-1)
        attn = jnp.where(full_mask[:, None, None, :], attn, -jnp.inf)
        attn = jax.nn.softmax(attn.astype(jnp.float32), axis=-1).astype(q.dtype)
        attn_out = jnp.einsum('bhkn,bnhd->bkhd', attn, v).reshape(b, k_len, H)
        attn_out = attn_out @ out_w + out_b + residual
        out = rmsnorm(attn_out, postnorm_w)
        out = jax.nn.gelu(out @ mlp_w1 + mlp_b1) @ mlp_w2 + mlp_b2
        return out + residual
    x = _L0_xattn_ref(x, ctx_2048, mask_Bx1xSxS2_ff0, L0_xattn_Wq, L0_xattn_bq, L0_xattn_Wk, L0_xattn_bk, L0_xattn_Wv, L0_xattn_bv, L0_xattn_Wo, L0_xattn_bo, L0_xattn_gamma, L0_xattn_beta)
    x = _L1_xattn_ref(x, ctx_2048, 0, L1_xattn_ln1_w, L1_xattn_ln1_b, L1_xattn_ln2_w, L1_xattn_ln2_b, L1_xattn_maa_x, L1_xattn_maa_w, L1_xattn_maa_k, L1_xattn_maa_v, L1_xattn_maa_r, L1_xattn_maa_g, L1_xattn_maa_w1, L1_xattn_maa_w2, L1_xattn_time_decay, L1_xattn_decay_w1, L1_xattn_decay_w2, L1_xattn_faaaa, L1_xattn_Wr, L1_xattn_Wk, L1_xattn_Wv, L1_xattn_Wg, L1_xattn_Wo, L1_xattn_gn_w, L1_xattn_gn_b, L1_xattn_fmaa_k, L1_xattn_fmaa_r, L1_xattn_fWk, L1_xattn_fWr, L1_xattn_fWv)
    x = _L2_xattn_ref(x, ctx_2048, L2_xattn_ln1_w, L2_xattn_ln1_b, L2_xattn_ln2_w, L2_xattn_ln2_b, L2_xattn_maa_x, L2_xattn_maa_w1, L2_xattn_maa_w2, L2_xattn_maa_stack, L2_xattn_time_decay, L2_xattn_decay_w1, L2_xattn_decay_w2, L2_xattn_faaaa, L2_xattn_Wr, L2_xattn_Wk, L2_xattn_Wv, L2_xattn_Wg, L2_xattn_Wo, L2_xattn_gn_w, L2_xattn_gn_b, L2_xattn_ffn_maa_k, L2_xattn_ffn_maa_r, L2_xattn_ffn_Wk, L2_xattn_ffn_Wr, L2_xattn_ffn_Wv, 0)
    x = _L3_xattn_ref(ctx_2048, x, mask_BxS2_ik0, L3_xattn_q_w, L3_xattn_q_b, L3_xattn_kv_w, L3_xattn_kv_b, L3_xattn_out_w, L3_xattn_out_b, L3_xattn_postnorm_w, L3_xattn_mlp_w1, L3_xattn_mlp_b1, L3_xattn_mlp_w2, L3_xattn_mlp_b2)
    return x

_drawn_inputs = setup_inputs


def setup_inputs(seed=0):
    import zlib

    import numpy as np

    out = dict(_drawn_inputs(seed))
    spreads = {'L0_xattn_bq': (0.0, 0.8),
     'L0_xattn_bk': (0.0, 2.0),
     'L0_xattn_bv': (0.0, 0.1),
     'L0_xattn_bo': (0.0, 0.1),
     'L0_xattn_gamma': (1.0, 0.2),
     'L0_xattn_beta': (0.0, 0.1),
     'L1_xattn_ln1_w': (1.0, 0.2),
     'L1_xattn_ln1_b': (0.0, 0.279),
     'L1_xattn_ln2_w': (1.0, 0.6),
     'L1_xattn_ln2_b': (0.0, 0.8),
     'L1_xattn_gn_w': (1.0, 0.6),
     'L1_xattn_gn_b': (0.0, 0.8),
     'L2_xattn_ln1_w': (1.0, 0.2),
     'L2_xattn_ln1_b': (0.0, 0.294),
     'L2_xattn_ln2_w': (1.0, 0.6),
     'L2_xattn_ln2_b': (0.0, 0.8),
     'L2_xattn_gn_w': (1.0, 0.6),
     'L2_xattn_gn_b': (0.0, 0.706),
     'L3_xattn_q_b': (0.0, 0.8),
     'L3_xattn_kv_b': (0.0, 0.8),
     'L3_xattn_out_b': (0.0, 1.697),
     'L3_xattn_postnorm_w': (1.0, 0.2),
     'L3_xattn_mlp_b1': (0.0, 0.1),
     'L3_xattn_mlp_b2': (0.0, 0.1)}
    factors = {'L0_xattn_Wq': 7.37,
     'L0_xattn_Wk': 7.163,
     'L1_xattn_maa_x': 6.89,
     'L1_xattn_maa_w': 8.0,
     'L1_xattn_maa_w1': 3.504,
     'L1_xattn_maa_w2': 3.56,
     'L1_xattn_decay_w1': 8.0,
     'L1_xattn_decay_w2': 8.0,
     'L1_xattn_faaaa': 3.758,
     'L1_xattn_fmaa_k': 2.683,
     'L1_xattn_fmaa_r': 8.0,
     'L1_xattn_fWr': 7.573,
     'L2_xattn_maa_x': 8.0,
     'L2_xattn_maa_w1': 3.03,
     'L2_xattn_maa_w2': 3.046,
     'L2_xattn_maa_stack': 6.69,
     'L2_xattn_decay_w1': 8.0,
     'L2_xattn_decay_w2': 8.0,
     'L2_xattn_faaaa': 3.122,
     'L2_xattn_ffn_maa_k': 8.0,
     'L2_xattn_ffn_maa_r': 8.0,
     'L2_xattn_ffn_Wr': 4.104,
     'L3_xattn_q_w': 8.0,
     'L3_xattn_kv_w': 7.498,
     'L3_xattn_out_w': 4.151}
    for name, (base, spread) in spreads.items():
        noise = np.random.default_rng([zlib.crc32(name.encode()), seed]).standard_normal(out[name].shape)
        drawn = base * np.exp(spread * noise) if base else spread * noise
        out[name] = jnp.asarray(drawn.astype(out[name].dtype))
    for name, factor in factors.items():
        out[name] = (out[name] * factor).astype(out[name].dtype)
    return out
```

```python
import concourse.bass as bass
from concourse import mybir
from contextlib import ExitStack

F32 = mybir.dt.float32
I32 = mybir.dt.int32
ALU = mybir.AluOpType
ACT = mybir.ActivationFunctionType
AX = mybir.AxisListType

P = 128
B, L, C = 4, 512, 512
CT, LT = C // P, L // P
BANK = 512
NBANK = 8

QH, KVH = 32, 8
HD = C // QH
NL = 2
RH, RS = 32, 16
HPT = P // RS
NF, DM, DD = 5, 32, 64
DECAY, KEY, VALUE, RECEPT, GATE = range(NF)
PH = 16
PD = C // PH
NK = 2 * L
MLP = 4 * C
MT = MLP // P

MASKED = -1.0e30

(V_LN1W, V_LN1B, V_MAAX, V_MAA, V_TD, V_U, V_GNW, V_GNB, V_LN2W, V_LN2B, V_FK, V_FR, V_N) = \
    (0, 1, 2, 3, 8, 9, 10, 11, 12, 13, 14, 15, 16)
W_R, W_K, W_V, W_G, W_O, W_FK, W_FR, W_FV = range(8)


class Queue:

    def __init__(self, engine, sem):
        self.e, self.sem, self.count, self.seen = engine, sem, 0, {}

    def after(self, *events):
        for ev in events:
            if ev is None:
                continue
            sem, value = ev
            if self.seen.get(id(sem), 0) < value:
                self.e.wait_ge(sem, value)
                self.seen[id(sem)] = value
        return self.e

    def did(self, instruction):
        instruction.then_inc(self.sem, 1)
        self.count += 1
        return (self.sem, self.count)

    def last(self):
        return (self.sem, self.count) if self.count else None

    def reset(self):
        self.count, self.seen = 0, {}


class Ring:

    def __init__(self, bufs):
        self.bufs, self.free, self.at = list(bufs), [None] * len(bufs), -1

    def take(self):
        self.at = (self.at + 1) % len(self.bufs)
        return self.at, self.bufs[self.at], self.free[self.at]


def program(nc, t):
    top = ExitStack()
    with top:
        def sem(name):
            return top.enter_context(nc.semaphore(name))

        PE = Queue(nc.tensor, sem("pe_done"))
        DVE = Queue(nc.vector, sem("dve_done"))
        ACE = Queue(nc.scalar, sem("act_done"))
        POOL = Queue(nc.gpsimd, sem("pool_done"))
        SP = Queue(nc.sync, None)
        queues = (PE, DVE, ACE, POOL, SP)
        load_sems = [sem(f"load{i}") for i in range(24)]
        store_sem = sem("store")
        loads = [0]

        def load(dst, src, q=None):
            q = q or SP
            s = load_sems[loads[0]]
            loads[0] += 1
            q.e.dma_start(dst, src).then_inc(s, 16)
            return (s, 16)

        def end_of_step(stored=0):
            if stored:
                SP.e.wait_ge(store_sem, stored)
            nc.all_engine_barrier()
            for s in [q.sem for q in queues if q.sem is not None] + load_sems[:loads[0]] + ([store_sem] if stored else []):
                nc.gpsimd.sem_clear(s)
            nc.all_engine_barrier()
            loads[0] = 0
            for q in queues:
                q.reset()

        def sb(name, shape, ctx=top, dt=F32):
            return ctx.enter_context(nc.sbuf_tensor(name, shape, dt))

        psum = top.enter_context(nc.psum_tensor("psum", [P, NBANK * BANK], F32))
        bank = [psum[:, i * BANK:(i + 1) * BANK] for i in range(NBANK)]

        X = sb("x_res", [P, B, LT, C])
        ident = sb("ident", [P, P])
        headsum = sb("headsum", [P, HPT])

        ev = POOL.did(POOL.e.memset(ident[:, :], 0.0))
        POOL.after(ev)
        ev_ident = POOL.did(POOL.e.affine_select(out=ident[:, :], in_=ident[:, :], compare_op=ALU.not_equal,
                                                 fill=1.0, base=0, pattern=[[-1, P]], channel_multiplier=1))
        DVE.after(ev_ident)
        DVE.did(DVE.e.tensor_reduce(headsum[:, :], ident[:, :].rearrange("p (h i) -> p h i", i=RS),
                                    axis=AX.X, op=ALU.add))
        end_of_step()

        def transpose(out, in_):
            return PE.e.transpose(out, in_, ident[:, :])

        def rsqrt(a, scratch, add, mul=1.0):
            v, y, u = scratch
            e = DVE.did(DVE.e.tensor_scalar(v, a, mul, add, ALU.mult, ALU.add))
            DVE.after(e)
            e = DVE.did(DVE.e.tensor_single_scalar(u.bitcast(I32), v.bitcast(I32), 1, ALU.arith_shift_right))
            DVE.after(e)
            e = DVE.did(DVE.e.tensor_scalar(y.bitcast(I32), u.bitcast(I32), -1.0, float(0x5F3759DF), ALU.mult, ALU.add))
            for n in range(4):
                DVE.after(e)
                e = DVE.did(DVE.e.tensor_tensor(u, y, y, ALU.mult))
                DVE.after(e)
                e = DVE.did(DVE.e.tensor_tensor(u, u, v, ALU.mult))
                DVE.after(e)
                e = DVE.did(DVE.e.tensor_scalar(u, u, -0.5, 1.5, ALU.mult, ALU.add))
                DVE.after(e)
                e = DVE.did(DVE.e.tensor_tensor(a if n == 3 else y, y, u, ALU.mult))
            return e

        def norm_stats(tiles, ready, stats, mv, rstd, scratch, eps):
            es = []
            for i, x in enumerate(tiles):
                DVE.after(ready[i])
                es.append(DVE.did(DVE.e.bn_stats(stats[:, i, :], x)))
            for i, e in enumerate(es):
                DVE.after(e)
                e2 = DVE.did(DVE.e.bn_aggr(mv[:, i, :], stats[:, i, :]))
            DVE.after(e2)
            e = DVE.did(DVE.e.tensor_copy(rstd, mv[:, :, 1]))
            DVE.after(e)
            return rsqrt(rstd, scratch, eps)

        with ExitStack() as ctx:
            wq = sb("l0_wq", [P, CT, C], ctx)
            wk = sb("l0_wk", [P, CT, 2 * CT, P], ctx)
            wv = sb("l0_wv", [P, CT, KVH * HD], ctx)
            wo = sb("l0_wo", [P, CT, C], ctx)
            bq = sb("l0_bq", [P, CT], ctx)
            bk = sb("l0_bk", [P, 2 * CT], ctx)
            bv = sb("l0_bv", [P, KVH * HD], ctx)
            bo = sb("l0_bo", [P, C], ctx)
            gamma = sb("l0_gamma", [P, C], ctx)
            beta = sb("l0_beta", [P, C], ctx)
            xT = sb("l0_xT", [P, CT, L], ctx)
            cT = sb("l0_cT", [P, CT, L], ctx)
            xin = sb("l0_x", [P, LT, C], ctx)
            mask = sb("l0_mask", [P, LT, L], ctx)
            qT = sb("l0_qT", [P, CT, L], ctx)
            kT = sb("l0_kT", [P, 2 * CT, L], ctx)
            vt = sb("l0_v", [P, LT, KVH * HD], ctx)
            nz = sb("l0_nz", [P, 3, L], ctx)
            pr = sb("l0_p", [P, 3, L], ctx)
            pT = sb("l0_pT", [P, 3, LT, P], ctx)
            nmax = sb("l0_nmax", [P, LT * QH], ctx)
            den = sb("l0_den", [P, LT * QH], ctx)
            rden = sb("l0_rden", [P, LT * QH], ctx)
            on = sb("l0_on", [P, 2, C], ctx)
            oT = sb("l0_oT", [P, 2, CT, P], ctx)
            stats = sb("l0_stats", [P, LT, 6], ctx)
            mv = sb("l0_mv", [P, LT, 2], ctx)
            rstd = sb("l0_rstd", [P, LT], ctx)
            scr = sb("l0_scr", [P, 3, LT], ctx)

            SP.after(load(wq[:, :, :], t["l0_wq"]), load(wk[:, :, :, :], t["l0_wk"], ACE), load(wv[:, :, :], t["l0_wv"]),
                     load(wo[:, :, :], t["l0_wo"]), load(bq[:, :], t["l0_bq"], ACE), load(bk[:, :], t["l0_bk"], ACE),
                     load(bv[:, :], t["l0_bv"].partition_broadcast(P)), load(bo[:, :], t["l0_bo"].partition_broadcast(P)),
                     load(gamma[:, :], t["l0_gamma"].partition_broadcast(P)),
                     load(beta[:, :], t["l0_beta"].partition_broadcast(P)))
            end_of_step()

            with nc.Fori(0, B) as b:
                got_x = load(xT[:, :, :], t["xT"][b])
                got_c = load(cT[:, :, :], t["cT"][b], ACE)
                got_m = load(mask[:, :, :], t["mask"][b])
                got_xin = load(xin[:, :, :], t["x"][b])

                ring = Ring(bank)
                PE.after(got_x)
                for m in range(CT):
                    i, ps, free = ring.take()
                    PE.after(free)
                    for k in range(CT):
                        mm = PE.e.matmul(ps, wq[:, k, m * P:(m + 1) * P], xT[:, k, :], start=k == 0, stop=k == CT - 1)
                    DVE.after(PE.did(mm))
                    ring.free[i] = q_done = DVE.did(DVE.e.tensor_scalar(qT[:, m, :], ps, bq[:, m:m + 1], HD ** -0.5,
                                                                        ALU.add, ALU.mult))
                PE.after(got_c)
                for m in range(2 * CT):
                    i, ps, free = ring.take()
                    PE.after(free)
                    for k in range(CT):
                        mm = PE.e.matmul(ps, wk[:, k, m, :], cT[:, k, :], start=k == 0, stop=k == CT - 1)
                    ACE.after(PE.did(mm))
                    ring.free[i] = k_done = ACE.did(ACE.e.activation(kT[:, m, :], ps, ACT.Identity, bias=bk[:, m:m + 1]))
                i, ps, free = ring.take()
                PE.after(free)
                for s in range(LT):
                    for k in range(CT):
                        mm = PE.e.matmul(ps[:, s * P:(s + 1) * P], cT[:, k, s * P:(s + 1) * P], wv[:, k, :],
                                         start=k == 0, stop=k == CT - 1)
                DVE.after(PE.did(mm))
                v_done = DVE.did(DVE.e.tensor_tensor(vt[:, :, :], ps.rearrange("p (s c) -> p s c", s=LT),
                                                     bv[:, :].unsqueeze(1).broadcast_to([P, LT, KVH * HD]), ALU.add))
                POOL.after(got_xin)
                for m in range(LT):
                    xb_done = POOL.did(POOL.e.tensor_tensor(xin[:, m, :], xin[:, m, :], bo[:, :], ALU.add))
                PE.after(q_done, k_done, v_done)
                DVE.after(got_m)

                s_ring, t_ring, o_ring = Ring(bank[0:3]), Ring(bank[3:6]), Ring(bank[6:8])
                for r in (s_ring, t_ring, o_ring):
                    r.free = [v_done] * len(r.bufs)
                nz_ring, pr_ring, pT_ring = Ring(range(3)), Ring(range(3)), Ring(range(3))
                on_ring = Ring(range(2))
                item = {}
                N = LT * QH
                wo_done = [None] * LT

                def scores(n):
                    lt, h = divmod(n, QH)
                    c, r = divmod(h, HPT)
                    quad = 32 * (r // 2)
                    i, ps, free = s_ring.take()
                    PE.after(free)
                    mm = PE.did(PE.e.matmul(ps, qT[quad:quad + 32, c, lt * P:(lt + 1) * P],
                                            kT[quad:quad + 32, 2 * c + r % 2, :], start=True, stop=True))
                    a, _, freed = nz_ring.take()
                    DVE.after(mm, freed)
                    z = s_ring.free[i] = DVE.did(DVE.e.tensor_tensor_reduce(
                        out=nz[:, a, :], in0=ps, in1=mask[:, lt, :], scale=-1.0, scalar=3.0e38,
                        op0=ALU.add, op1=ALU.min, accum_out=nmax[:, n:n + 1]))
                    i, _, freed = pr_ring.take()
                    ACE.after(z, freed)
                    e = nz_ring.free[a] = ACE.did(ACE.e.activation(pr[:, i, :], nz[:, a, :], ACT.Exp, scale=-1.0,
                                                                   bias=nmax[:, n:n + 1], accum_out=den[:, n:n + 1]))
                    item[n] = (i, e)

                def turn(n):
                    i, e = item[n]
                    j, ps, free = t_ring.take()
                    PE.after(e, free)
                    for s in range(LT):
                        mm = transpose(ps[:, s * P:(s + 1) * P], pr[:, i, s * P:(s + 1) * P])
                    mm = pr_ring.free[i] = PE.did(mm)
                    k, _, freed = pT_ring.take()
                    dst = pT[:, k, :, :].rearrange("p s l -> p (s l)")
                    if n % 8 in (0, 2, 4, 5, 7):
                        DVE.after(mm, freed)
                        e = DVE.did(DVE.e.tensor_copy(dst, ps))
                    else:
                        ACE.after(mm, freed)
                        e = ACE.did(ACE.e.activation(dst, ps, ACT.Copy))
                    t_ring.free[j] = e
                    item[n] = (k, e)

                def mix(n):
                    lt, h = divmod(n, QH)
                    k, e = item.pop(n)
                    if h == 0:
                        item["o"] = o_ring.take()
                        PE.after(item["o"][2])
                    oi, ops, _ = item["o"]
                    PE.after(e)
                    g = h // (QH // KVH)
                    for s in range(LT):
                        mm = PE.e.matmul(ops[:, h * HD:(h + 1) * HD], pT[:, k, s, :], vt[:, s, g * HD:(g + 1) * HD],
                                         start=s == 0, stop=s == LT - 1)
                    pT_ring.free[k] = mm = PE.did(mm)
                    if h == QH - 1:
                        item[("lt", lt)] = (oi, ops, mm)

                def project(lt):
                    oi, ops, mm = item.pop(("lt", lt))
                    sl = slice(lt * QH, (lt + 1) * QH)
                    j, _, freed = on_ring.take()
                    DVE.after(ACE.last())
                    e = DVE.did(DVE.e.reciprocal(rden[:, sl], den[:, sl]))
                    DVE.after(e, mm, freed)
                    e = o_ring.free[oi] = DVE.did(DVE.e.tensor_tensor(
                        on[:, j, :].rearrange("p (h d) -> p h d", h=QH), ops.rearrange("p (h d) -> p h d", h=QH),
                        rden[:, sl].unsqueeze(2).broadcast_to([P, QH, HD]), ALU.mult))
                    i, ps, free = s_ring.take()
                    PE.after(e, free)
                    for c in range(CT):
                        mm = transpose(ps[:, c * P:(c + 1) * P], on[:, j, c * P:(c + 1) * P])
                    DVE.after(PE.did(mm))
                    e = s_ring.free[i] = DVE.did(DVE.e.tensor_copy(oT[:, j, :, :].rearrange("p c l -> p (c l)"), ps))
                    i, ps, free = t_ring.take()
                    PE.after(e, free)
                    for c in range(CT):
                        mm = PE.e.matmul(ps, oT[:, j, c, :], wo[:, c, :], start=c == 0, stop=c == CT - 1)
                    on_ring.free[j] = mm = PE.did(mm)
                    DVE.after(mm, xb_done)
                    t_ring.free[i] = wo_done[lt] = DVE.did(DVE.e.tensor_tensor(xin[:, lt, :], ps, xin[:, lt, :], ALU.add))

                for n in range(N + 2):
                    if n < N:
                        scores(n)
                    if 1 <= n <= N:
                        turn(n - 1)
                    if n >= 2:
                        mix(n - 2)
                        if (n - 2) % QH == QH - 1:
                            project((n - 2) // QH)

                e = norm_stats([xin[:, m, :] for m in range(LT)], wo_done, stats, mv, rstd[:, :],
                               [scr[:, i, :] for i in range(3)], 1e-6)
                DVE.after(e)
                for m in range(LT):
                    e = DVE.did(DVE.e.tensor_scalar(xin[:, m, :], xin[:, m, :], mv[:, m, 0:1], rstd[:, m:m + 1],
                                                    ALU.subtract, ALU.mult))
                    POOL.after(e)
                    e = POOL.did(POOL.e.tensor_tensor(xin[:, m, :], xin[:, m, :], gamma[:, :], ALU.mult))
                    POOL.after(e)
                    POOL.did(POOL.e.tensor_tensor(X[:, b, m, :], xin[:, m, :], beta[:, :], ALU.add))
                end_of_step()

        with ExitStack() as ctx:
            w1 = sb("rw_w1", [P, CT, NF * DM], ctx)
            w2 = sb("rw_w2", [P, C], ctx)
            w2b = sb("rw_w2b", [DM, C], ctx)
            dw1 = sb("rw_dw1", [P, CT, DD], ctx)
            dw2 = sb("rw_dw2", [DD, C], ctx)
            W = sb("rw_w", [P, 8, CT, C], ctx)
            vec = sb("rw_vec", [P, V_N, CT], ctx)
            xn = sb("rw_xn", [P, LT, C], ctx)
            xa = sb("rw_xa", [P, CT, L + 1], ctx)
            sx = sb("rw_sx", [P, CT, L], ctx)
            big = sb("rw_big", [P, 4 * (L + 1) + 4 * L], ctx)
            xf = [big[:, f * CT * L:(f + 1) * CT * L].rearrange("p (c l) -> p c l", c=CT) for f in range(2)]
            S = big[:, 0:4 * (L + 1)].rearrange("p (n l) -> p n l", n=4)
            kvb = big[:, 4 * (L + 1):4 * (L + 1) + 2 * L].rearrange("p (n l) -> p n l", n=2)
            rs = big[:, 4 * (L + 1) + 2 * L:].rearrange("p (n l) -> p n l", n=2)
            tm = sb("rw_tm", [P, L], ctx)
            tmb = sb("rw_tmb", [DM, L], ctx)
            dT = sb("rw_dT", [DD, L], ctx)
            wT = sb("rw_wT", [P, CT, L], ctx)
            kT = sb("rw_kT", [P, CT, L], ctx)
            vT = sb("rw_vT", [P, CT, L], ctx)
            rT = sb("rw_rT", [P, CT, L], ctx)
            gT = sb("rw_gT", [P, CT, L], ctx)
            prev = sb("rw_prev", [P, 2, CT], ctx)
            s0 = sb("rw_s0", [P, CT, RS], ctx)
            tmp = sb("rw_tmp", [P, 2, L], ctx)
            ruk = sb("rw_ruk", [P, LT, HPT], ctx)
            stats = sb("rw_stats", [P, LT, 6], ctx)
            mv = sb("rw_mv", [P, LT, 2], ctx)
            rstd = sb("rw_rstd", [P, LT], ctx)
            scr = sb("rw_scr", [P, 3, LT * HPT], ctx)
            gm = sb("rw_gm", [P, 2, LT * HPT], ctx)
            small = [scr[:, i, 0:LT] for i in range(3)]
            pick = sb("rw_pick", [P, RS, P], ctx)
            for j in range(RS):
                DVE.did(DVE.e.tensor_copy(
                    pick[:, j, :].rearrange("p (h i) -> p h i", i=RS),
                    ident[:, :].rearrange("p (h i) -> p h i", i=RS)[:, :, j:j + 1].broadcast_to([P, HPT, RS])))

            with nc.Fori(0, NL) as layer:
                SP.after(load(w1[:, :, :], t["rw_w1"][layer]), load(w2[:, :], t["rw_w2"][layer, 0:P, :]),
                         load(w2b[:, :], t["rw_w2"][layer, P:P + DM, :], ACE), load(dw1[:, :, :], t["rw_dw1"][layer], ACE),
                         load(dw2[:, :], t["rw_dw2"][layer]), load(vec[:, :, :], t["rw_vec"][layer], ACE),
                         *[load(W[:, i, :, :], t["rw_w"][layer, i], (SP, ACE)[i % 2]) for i in range(8)])
                end_of_step()

                with nc.Fori(0, B) as b:
                    got_s0 = load(s0[:, :, :], t["s0"][b])
                    got_prev = load(prev[:, :, :], t["prev"][b], ACE)

                    def vcol(v, c):
                        return vec[:, v, c:c + 1]

                    def shifted_norm(vw, vb, ready, xa_free):
                        e = norm_stats([X[:, b, m, :] for m in range(LT)], ready, stats, mv, rstd[:, :], small, 1e-5)
                        DVE.after(e)
                        done = [DVE.did(DVE.e.tensor_scalar(xn[:, m, :], X[:, b, m, :], mv[:, m, 0:1], rstd[:, m:m + 1],
                                                            ALU.subtract, ALU.mult)) for m in range(LT)]
                        ACE.after(xa_free)
                        out = []
                        for c in range(CT):
                            i, ps, free = ring.take()
                            PE.after(free)
                            for m in range(LT):
                                PE.after(done[m])
                                mm = transpose(ps[:, m * P:(m + 1) * P], xn[:, m, c * P:(c + 1) * P])
                            ACE.after(PE.did(mm))
                            e = ring.free[i] = ACE.did(ACE.e.activation(xa[:, c, 1:L + 1], ps, ACT.Identity,
                                                                        scale=vcol(vw, c), bias=vcol(vb, c)))
                            POOL.after(e)
                            out.append(POOL.did(POOL.e.tensor_tensor(sx[:, c, :], xa[:, c, 0:L], xa[:, c, 1:L + 1],
                                                                     ALU.subtract)))
                        return out

                    ring = Ring(bank)
                    POOL.after(got_prev)
                    POOL.after(POOL.did(POOL.e.tensor_copy(xa[:, :, 0], prev[:, 1, :])))
                    sx_done = shifted_norm(V_LN1W, V_LN1B, [None] * LT, None)

                    for c in range(CT):
                        DVE.after(sx_done[c])
                        xx_done = DVE.did(DVE.e.scalar_tensor_tensor(xf[0][:, c, :], sx[:, c, :], vcol(V_MAAX, c),
                                                                     xa[:, c, 1:L + 1], ALU.mult, ALU.add))
                    PE.after(xx_done)
                    i, ps, free = ring.take()
                    PE.after(free)
                    for k in range(CT):
                        mm = PE.e.matmul(ps, w1[:, k, 0:P], xf[0][:, k, :], start=k == 0, stop=k == CT - 1)
                    ACE.after(PE.did(mm))
                    e = ring.free[i] = ACE.did(ACE.e.activation(tm[:, :], ps, ACT.Tanh))
                    i, ps, free = ring.take()
                    PE.after(free)
                    for k in range(CT):
                        mm = PE.e.matmul(ps[0:DM, :], w1[:, k, P:P + DM], xf[0][:, k, :], start=k == 0, stop=k == CT - 1)
                    xf_free = [PE.did(mm), None]
                    ACE.after(xf_free[0])
                    e2 = ring.free[i] = ACE.did(ACE.e.activation(tmb[:, :], ps[0:DM, :], ACT.Tanh))
                    PE.after(e, e2)

                    def mixed(f, slot):
                        q = 32 * f
                        out = []
                        for c in range(CT):
                            i, ps, free = ring.take()
                            PE.after(free)
                            if f < 4:
                                mm = PE.e.matmul(ps, w2[q:q + DM, c * P:(c + 1) * P], tm[q:q + DM, :], start=True, stop=True)
                            else:
                                mm = PE.e.matmul(ps, w2b[:, c * P:(c + 1) * P], tmb[:, :], start=True, stop=True)
                            DVE.after(PE.did(mm), xf_free[slot])
                            e = ring.free[i] = DVE.did(DVE.e.scalar_tensor_tensor(
                                xf[slot][:, c, :], ps, vcol(V_MAA + f, c), sx[:, c, :], ALU.add, ALU.mult))
                            POOL.after(e)
                            out.append(POOL.did(POOL.e.tensor_tensor(xf[slot][:, c, :], xf[slot][:, c, :],
                                                                     xa[:, c, 1:L + 1], ALU.add)))
                        return out

                    def gemm_T(w, x, n_out, evac, k_ready=()):
                        for m in range(n_out):
                            i, ps, free = ring.take()
                            PE.after(free)
                            for k in range(CT):
                                if m == 0 and k_ready:
                                    PE.after(k_ready[k])
                                mm = PE.e.matmul(ps, w[:, k, m * P:(m + 1) * P], x[:, k, :], start=k == 0, stop=k == CT - 1)
                            ring.free[i] = evac(m, ps, PE.did(mm))

                    ready = mixed(DECAY, 0)
                    ready2 = mixed(KEY, 1)
                    i, ps, free = ring.take()
                    PE.after(free)
                    for k in range(CT):
                        PE.after(ready[k])
                        mm = PE.e.matmul(ps[0:DD, :], dw1[:, k, :], xf[0][:, k, :], start=k == 0, stop=k == CT - 1)
                    xf_free[0] = PE.did(mm)
                    ACE.after(xf_free[0])
                    e = ring.free[i] = ACE.did(ACE.e.activation(dT[:, :], ps[0:DD, :], ACT.Tanh))
                    PE.after(e)
                    for c in range(CT):
                        i, ps, free = ring.take()
                        PE.after(free)
                        mm = PE.did(PE.e.matmul(ps, dw2[:, c * P:(c + 1) * P], dT[:, :], start=True, stop=True))
                        ACE.after(mm)
                        e = ring.free[i] = ACE.did(ACE.e.activation(wT[:, c, :], ps, ACT.Exp, bias=vcol(V_TD, c)))
                        ACE.after(e)
                        w_done = ACE.did(ACE.e.activation(wT[:, c, :], wT[:, c, :], ACT.Exp, scale=-1.0))

                    def copy_to(dst):
                        def evac(m, ps, mm):
                            ACE.after(mm)
                            return ACE.did(ACE.e.activation(dst[:, m, :], ps, ACT.Copy))
                        return evac

                    gemm_T(W[:, W_K, :, :], xf[1], CT, copy_to(kT), ready2)
                    xf_free[1] = PE.last()
                    ready = mixed(VALUE, 0)
                    ready2 = mixed(RECEPT, 1)
                    gemm_T(W[:, W_V, :, :], xf[0], CT, copy_to(vT), ready)
                    xf_free[0] = PE.last()
                    gemm_T(W[:, W_R, :, :], xf[1], CT, copy_to(rT), ready2)
                    ready = mixed(GATE, 0)
                    krv_done = ACE.last()

                    def gate(m, ps, mm):
                        ACE.after(mm)
                        DVE.after(ACE.did(ACE.e.activation(gT[:, m, :], ps, ACT.Sigmoid)))
                        return DVE.did(DVE.e.tensor_tensor(gT[:, m, :], ps, gT[:, m, :], ALU.mult))
                    gemm_T(W[:, W_G, :, :], xf[0], CT, gate, ready)
                    g_done = DVE.last()
                    front_done = (PE.last(), POOL.last(), DVE.last(), ACE.last())

                    bc_ring, y_ring, misc = Ring(bank[0:3]), Ring(bank[3:5]), Ring(bank[5:8])
                    for r in (bc_ring, y_ring, misc):
                        r.free = [DVE.last()] * len(r.bufs)
                    S_ring, kv_ring, rs_ring, tmp_ring = Ring(range(4)), Ring(range(2)), Ring(range(2)), Ring(range(2))
                    S_ring.free = [front_done[0]] * 4
                    DVE.after(*front_done, got_s0)
                    POOL.after(*front_done)
                    ACE.after(*front_done, got_s0)
                    PE.after(*front_done)
                    item = {}
                    yg = xn
                    yg_done = [None] * CT

                    def spread(n):
                        g, j = divmod(n, RS)
                        i, ps, free = bc_ring.take()
                        PE.after(free)
                        item[n] = (i, ps, PE.did(PE.e.matmul(ps, pick[:, j, :], vT[:, g, :], start=True, stop=True)))

                    def recur(n):
                        g, j = divmod(n, RS)
                        i, ps, mm = item[n]
                        a, _, free = kv_ring.take()
                        DVE.after(mm, free)
                        e = bc_ring.free[i] = DVE.did(DVE.e.tensor_tensor(kvb[:, a, :], ps, kT[:, g, :], ALU.mult))
                        s, _, free = S_ring.take()
                        ACE.after(free)
                        e0 = ACE.did(ACE.e.activation(S[:, s, 0:1], s0[:, g, j:j + 1], ACT.Copy))
                        DVE.after(e, free)
                        e = kv_ring.free[a] = DVE.did(DVE.e.tensor_tensor_scan(
                            S[:, s, 1:L + 1], wT[:, g, :], kvb[:, a, :], s0[:, g, j:j + 1], ALU.mult, ALU.add))
                        q = POOL
                        a, _, free = rs_ring.take()
                        q.after(e, e0, free)
                        e = S_ring.free[s] = q.did(q.e.tensor_tensor(rs[:, a, :], S[:, s, 0:L], rT[:, g, :], ALU.mult))
                        item[n] = (a, e)

                    def read(n):
                        g, j = divmod(n, RS)
                        a, e = item.pop(n)
                        if j == 0:
                            item["y"] = y_ring.take()
                            PE.after(item["y"][2])
                        yi, yps, _ = item["y"]
                        PE.after(e)
                        y4 = yps.rearrange("p (m h j) -> p m h j", m=LT, h=HPT)
                        for m in range(LT):
                            mm = PE.e.matmul(y4[:, m, :, j], rs[:, a, m * P:(m + 1) * P], headsum[:, :], start=True, stop=True)
                        rs_ring.free[a] = mm = PE.did(mm)
                        if j == RS - 1:
                            item[("g", g)] = (yi, yps, mm)

                    def group(g):
                        yi, yps, y_mm = item.pop(("g", g))
                        G = LT * HPT
                        ti, _, free = tmp_ring.take()
                        ta = tmp[:, ti, :]
                        DVE.after(free)
                        e = DVE.did(DVE.e.scalar_tensor_tensor(ta, rT[:, g, :], vcol(V_U, g), kT[:, g, :], ALU.mult, ALU.mult))
                        i, ps, free = misc.take()
                        PE.after(e, free)
                        for m in range(LT):
                            mm = PE.e.matmul(ps[:, m * HPT:(m + 1) * HPT], ta[:, m * P:(m + 1) * P], headsum[:, :],
                                             start=True, stop=True)
                        DVE.after(PE.did(mm))
                        e = misc.free[i] = DVE.did(DVE.e.tensor_copy(ruk[:, :, :].rearrange("p m h -> p (m h)"), ps[:, 0:G]))
                        i, ps, free = misc.take()
                        PE.after(free)
                        for m in range(LT):
                            mm = transpose(ps[:, m * P:(m + 1) * P], vT[:, g, m * P:(m + 1) * P])
                        DVE.after(PE.did(mm), e)
                        rows = ta.rearrange("p (g j) -> p g j", g=G)
                        e = misc.free[i] = DVE.did(DVE.e.tensor_tensor(
                            rows, ps.rearrange("p (g j) -> p g j", g=G),
                            ruk[:, :, :].rearrange("p m h -> p (m h)").unsqueeze(2).broadcast_to([P, G, RS]), ALU.mult))
                        DVE.after(e, y_mm)
                        e = y_ring.free[yi] = DVE.did(DVE.e.tensor_tensor(ta, yps, ta, ALU.add))
                        DVE.after(e)
                        e = DVE.did(DVE.e.tensor_reduce(gm[:, 0, :], rows, axis=AX.X, op=ALU.add))
                        DVE.after(e)
                        e = DVE.did(DVE.e.tensor_scalar_mul(gm[:, 0, :], gm[:, 0, :], 1.0 / RS))
                        DVE.after(e)
                        e = DVE.did(DVE.e.tensor_tensor(rows, rows, gm[:, 0, :].unsqueeze(2).broadcast_to([P, G, RS]),
                                                        ALU.subtract))
                        ti2, _, free = tmp_ring.take()
                        tb = tmp[:, ti2, :]
                        ACE.after(e, free)
                        e = ACE.did(ACE.e.activation(tb, ta, ACT.Square))
                        DVE.after(e)
                        e = DVE.did(DVE.e.tensor_reduce(gm[:, 1, :], tb.rearrange("p (g j) -> p g j", g=G), axis=AX.X, op=ALU.add))
                        DVE.after(e)
                        e = rsqrt(gm[:, 1, :], [scr[:, q, :] for q in range(3)], 1e-5, 1.0 / RS)
                        DVE.after(e)
                        e = DVE.did(DVE.e.tensor_tensor(rows, rows, gm[:, 1, :].unsqueeze(2).broadcast_to([P, G, RS]), ALU.mult))
                        i, ps, free = misc.take()
                        PE.after(e, free)
                        for m in range(LT):
                            mm = transpose(ps[:, m * P:(m + 1) * P], ta[:, m * P:(m + 1) * P])
                        mm = PE.did(mm)
                        tmp_ring.free[ti] = tmp_ring.free[ti2] = mm
                        ACE.after(mm)
                        e = misc.free[i] = ACE.did(ACE.e.activation(yg[:, g, :], ps, ACT.Identity, scale=vcol(V_GNW, g),
                                                                    bias=vcol(V_GNB, g)))
                        POOL.after(e)
                        yg_done[g] = POOL.did(POOL.e.tensor_tensor(yg[:, g, :], yg[:, g, :], gT[:, g, :], ALU.mult))

                    N = CT * RS
                    spread(0)
                    spread(1)
                    for n in range(N + 1):
                        if n + 2 < N:
                            spread(n + 2)
                        if n < N:
                            recur(n)
                        if n >= 1:
                            read(n - 1)
                            if n % RS == 0:
                                group(n // RS - 1)

                    PE.after(*yg_done)
                    ring = Ring(bank)
                    ring.free = [DVE.last()] * 3 + [DVE.last()] * 2 + list(misc.free)
                    PE.after(DVE.last(), ACE.last())

                    def gemm_rows(w, x, kt, evac):
                        for m in range(LT):
                            i, ps, free = ring.take()
                            PE.after(free)
                            for k in range(kt):
                                mm = PE.e.matmul(ps, x[:, k, m * P:(m + 1) * P], w[:, k, :], start=k == 0, stop=k == kt - 1)
                            ring.free[i] = evac(m, ps, PE.did(mm))

                    x_done = [None] * LT

                    def add_x(m, ps, mm):
                        DVE.after(mm)
                        x_done[m] = DVE.did(DVE.e.tensor_tensor(X[:, b, m, :], ps, X[:, b, m, :], ALU.add))
                        return x_done[m]
                    gemm_rows(W[:, W_O, :, :], yg, CT, add_x)

                    POOL.after(POOL.did(POOL.e.tensor_copy(xa[:, :, 0], prev[:, 0, :])))
                    DVE.after(PE.last())
                    sx_done = shifted_norm(V_LN2W, V_LN2B, x_done, None)
                    for c in range(CT):
                        DVE.after(sx_done[c])
                        for v, dst in ((V_FK, xf[0]), (V_FR, xf[1])):
                            e = DVE.did(DVE.e.scalar_tensor_tensor(dst[:, c, :], sx[:, c, :], vcol(v, c), xa[:, c, 1:L + 1],
                                                                   ALU.mult, ALU.add))
                    PE.after(e)

                    def relu2(m, ps, mm):
                        ACE.after(mm)
                        e = ACE.did(ACE.e.activation(kT[:, m, :], ps, ACT.Relu))
                        POOL.after(e)
                        POOL.did(POOL.e.tensor_tensor(kT[:, m, :], kT[:, m, :], kT[:, m, :], ALU.mult))
                        return e
                    gemm_T(W[:, W_FK, :, :], xf[0], CT, relu2)
                    kk_done = POOL.last()

                    def sigmoid(m, ps, mm):
                        ACE.after(mm)
                        return ACE.did(ACE.e.activation(wT[:, m, :], ps, ACT.Sigmoid))
                    gemm_rows(W[:, W_FR, :, :], xf[1], CT, sigmoid)
                    PE.after(kk_done)

                    def add_ffn(m, ps, mm):
                        DVE.after(mm)
                        e = DVE.did(DVE.e.tensor_tensor(wT[:, m, :], ps, wT[:, m, :], ALU.mult))
                        POOL.after(e)
                        POOL.did(POOL.e.tensor_tensor(X[:, b, m, :], X[:, b, m, :], wT[:, m, :], ALU.add))
                        return e
                    DVE.after(ACE.last())
                    gemm_rows(W[:, W_FV, :, :], kT, CT, add_ffn)
                    end_of_step()

        with ExitStack() as ctx:
            wq = sb("l3_wq", [P, CT, C], ctx)
            wk = sb("l3_wk", [P, CT, C], ctx)
            wv = sb("l3_wv", [P, CT, C], ctx)
            wo = sb("l3_wo", [P, CT, C], ctx)
            m1 = sb("l3_m1", [P, CT, MLP], ctx)
            vec = sb("l3_vec", [P, 3 * CT + MT], ctx)
            bv = sb("l3_bv", [P, C], ctx)
            bo = sb("l3_bo", [P, C], ctx)
            b2 = sb("l3_b2", [P, C], ctx)
            hT = sb("l3_hT", [P, CT, NK], ctx)
            qT = sb("l3_qT", [P, CT, L], ctx)
            m2 = sb("l3_m2", [P, 4, C], ctx)
            kT = sb("l3_kT", [P, CT, NK], ctx)
            vt = sb("l3_v", [P, NK // P, C], ctx)
            mi = sb("l3_mi", [P, L], ctx, I32)
            mb = sb("l3_mb", [P, NK], ctx)
            nz = sb("l3_nz", [P, 2, NK], ctx)
            pr = sb("l3_p", [P, 2, NK], ctx)
            pT = sb("l3_pT", [P, 3, 4, P], ctx)
            nmax = sb("l3_nmax", [P, LT * PH], ctx)
            den = sb("l3_den", [P, LT * PH], ctx)
            rden = sb("l3_rden", [P, LT * PH], ctx)
            on = sb("l3_on", [P, 1, C], ctx)
            oT = sb("l3_oT", [P, 1, CT, P], ctx)
            att = sb("l3_att", [P, LT, C], ctx)
            nT = qT
            ss = sb("l3_ss", [P, LT], ctx)
            scr = sb("l3_scr", [P, 3, LT], ctx)
            h1 = [(kT, vt, hT)[m // 8][:, :, :].rearrange("p c l -> p (c l)")[:, (m % 8) * L:(m % 8 + 1) * L] for m in range(MT)]

            SP.after(load(wq[:, :, :], t["l3_wq"]), load(wk[:, :, :], t["l3_wk"], ACE), load(wv[:, :, :], t["l3_wv"]),
                     load(wo[:, :, :], t["l3_wo"], ACE), load(m1[:, :, :], t["l3_m1"]), load(vec[:, :], t["l3_vec"], ACE),
                     load(bv[:, :], t["l3_bv"].partition_broadcast(P)), load(bo[:, :], t["l3_bo"].partition_broadcast(P)),
                     load(b2[:, :], t["l3_b2"].partition_broadcast(P)))
            DVE.did(DVE.e.memset(mb[:, L:NK], 0.0))
            end_of_step()

            with nc.Fori(0, B) as b:
                got_c = load(hT[:, :, 0:L], t["cT"][b])
                got_m = load(mi[:, :], t["keymask"][b].partition_broadcast(P), ACE)
                got_m2 = load(m2[:, :, :], t["l3_m2"][0])
                ring = Ring(bank)
                for c in range(CT):
                    for m in range(LT):
                        if c == 0:
                            cp = DVE.did(DVE.e.tensor_copy(att[:, m, :], X[:, b, m, :]))
                            PE.after(cp)
                for c in range(CT):
                    i, ps, free = ring.take()
                    PE.after(free)
                    for m in range(LT):
                        mm = transpose(ps[:, m * P:(m + 1) * P], att[:, m, c * P:(c + 1) * P])
                    ACE.after(PE.did(mm))
                    ring.free[i] = l_done = ACE.did(ACE.e.activation(hT[:, c, L:NK], ps, ACT.Copy))
                DVE.after(got_m)
                e = DVE.did(DVE.e.tensor_single_scalar(mb[:, 0:L], mi[:, :], 0.0, ALU.is_equal))
                DVE.after(e)
                mb_done = DVE.did(DVE.e.tensor_scalar_mul(mb[:, 0:L], mb[:, 0:L], MASKED))
                PE.after(l_done)
                for m in range(CT):
                    i, ps, free = ring.take()
                    PE.after(free)
                    for k in range(CT):
                        mm = PE.e.matmul(ps, wq[:, k, m * P:(m + 1) * P], hT[:, k, L:NK], start=k == 0, stop=k == CT - 1)
                    DVE.after(PE.did(mm))
                    ring.free[i] = q_done = DVE.did(DVE.e.tensor_scalar(qT[:, m, :], ps, vec[:, m:m + 1], 1.0 / PD,
                                                                        ALU.add, ALU.mult))
                PE.after(got_c)
                for m in range(CT):
                    for half in range(2):
                        i, ps, free = ring.take()
                        PE.after(free)
                        for k in range(CT):
                            mm = PE.e.matmul(ps, wk[:, k, m * P:(m + 1) * P], hT[:, k, half * L:(half + 1) * L],
                                             start=k == 0, stop=k == CT - 1)
                        ACE.after(PE.did(mm))
                        ring.free[i] = k_done = ACE.did(ACE.e.activation(kT[:, m, half * L:(half + 1) * L], ps, ACT.Identity,
                                                                         bias=vec[:, CT + m:CT + m + 1]))
                for s in range(NK // P):
                    i, ps, free = ring.take()
                    PE.after(free)
                    for k in range(CT):
                        mm = PE.e.matmul(ps, hT[:, k, s * P:(s + 1) * P], wv[:, k, :], start=k == 0, stop=k == CT - 1)
                    DVE.after(PE.did(mm))
                    ring.free[i] = v_done = DVE.did(DVE.e.tensor_tensor(vt[:, s, :], ps, bv[:, :], ALU.add))
                for m in range(LT):
                    DVE.after(cp, l_done)
                    at_done = DVE.did(DVE.e.tensor_tensor(att[:, m, :], att[:, m, :], bo[:, :], ALU.add))
                PE.after(q_done, k_done, v_done)
                DVE.after(mb_done)

                s_ring = Ring([psum[:, 0:2 * BANK], psum[:, 2 * BANK:4 * BANK]])
                t_ring, o_ring = Ring(bank[4:7]), Ring(bank[7:8])
                for r in (s_ring, t_ring, o_ring):
                    r.free = [v_done] * len(r.bufs)
                nz_ring, pr_ring, pT_ring, on_ring = Ring(range(2)), Ring(range(2)), Ring(range(3)), Ring(range(1))
                item = {}
                N = LT * PH

                def scores(n):
                    lt, h = divmod(n, PH)
                    c, r = divmod(h, 4)
                    quad = 32 * r
                    i, ps, free = s_ring.take()
                    PE.after(free)
                    for half in range(2):
                        mm = PE.e.matmul(ps[:, half * L:(half + 1) * L], qT[quad:quad + 32, c, lt * P:(lt + 1) * P],
                                         kT[quad:quad + 32, c, half * L:(half + 1) * L], start=True, stop=True)
                    mm = PE.did(mm)
                    a, _, freed = nz_ring.take()
                    DVE.after(mm, freed)
                    z = s_ring.free[i] = DVE.did(DVE.e.tensor_tensor_reduce(
                        out=nz[:, a, :], in0=ps, in1=mb[:, :], scale=-1.0, scalar=3.0e38,
                        op0=ALU.add, op1=ALU.min, accum_out=nmax[:, n:n + 1]))
                    i, _, freed = pr_ring.take()
                    ACE.after(z, freed)
                    e = nz_ring.free[a] = ACE.did(ACE.e.activation(pr[:, i, :], nz[:, a, :], ACT.Exp, scale=-1.0,
                                                                   bias=nmax[:, n:n + 1], accum_out=den[:, n:n + 1]))
                    item[n] = (i, e)

                def turn(n, half):
                    i, e = item[n]
                    j, ps, free = t_ring.take()
                    PE.after(e, free)
                    for s in range(4):
                        mm = transpose(ps[:, s * P:(s + 1) * P], pr[:, i, (4 * half + s) * P:(4 * half + s + 1) * P])
                    mm = PE.did(mm)
                    if half == 1:
                        pr_ring.free[i] = mm
                    k, _, freed = pT_ring.take()
                    dst = pT[:, k, :, :].rearrange("p s l -> p (s l)")
                    if half == 0:
                        DVE.after(mm, freed)
                        e = DVE.did(DVE.e.tensor_copy(dst, ps))
                    else:
                        ACE.after(mm, freed)
                        e = ACE.did(ACE.e.activation(dst, ps, ACT.Copy))
                    t_ring.free[j] = e
                    item[(n, half)] = (k, e)

                def mix(n, half):
                    lt, h = divmod(n, PH)
                    k, e = item.pop((n, half))
                    if h == 0 and half == 0:
                        item["o"] = o_ring.take()
                        PE.after(item["o"][2])
                    oi, ops, _ = item["o"]
                    PE.after(e)
                    for s in range(4):
                        mm = PE.e.matmul(ops[:, h * PD:(h + 1) * PD], pT[:, k, s, :], vt[:, 4 * half + s, h * PD:(h + 1) * PD],
                                         start=half == 0 and s == 0, stop=half == 1 and s == 3)
                    pT_ring.free[k] = mm = PE.did(mm)
                    if h == PH - 1 and half == 1:
                        item[("lt", lt)] = (oi, ops, mm)

                def project(lt):
                    oi, ops, mm = item.pop(("lt", lt))
                    sl = slice(lt * PH, (lt + 1) * PH)
                    j, _, freed = on_ring.take()
                    DVE.after(ACE.last())
                    e = DVE.did(DVE.e.reciprocal(rden[:, sl], den[:, sl]))
                    DVE.after(e, mm, freed)
                    e = o_ring.free[oi] = DVE.did(DVE.e.tensor_tensor(
                        on[:, j, :].rearrange("p (h d) -> p h d", h=PH), ops.rearrange("p (h d) -> p h d", h=PH),
                        rden[:, sl].unsqueeze(2).broadcast_to([P, PH, PD]), ALU.mult))
                    i, ps, free = t_ring.take()
                    PE.after(e, free)
                    for c in range(CT):
                        mm = transpose(ps[:, c * P:(c + 1) * P], on[:, j, c * P:(c + 1) * P])
                    DVE.after(PE.did(mm))
                    e = t_ring.free[i] = DVE.did(DVE.e.tensor_copy(oT[:, j, :, :].rearrange("p c l -> p (c l)"), ps))
                    i, ps, free = t_ring.take()
                    PE.after(e, free)
                    for c in range(CT):
                        mm = PE.e.matmul(ps, oT[:, j, c, :], wo[:, c, :], start=c == 0, stop=c == CT - 1)
                    on_ring.free[j] = mm = PE.did(mm)
                    DVE.after(mm, at_done)
                    e = t_ring.free[i] = DVE.did(DVE.e.tensor_tensor(att[:, lt, :], ps, att[:, lt, :], ALU.add))
                    DVE.after(e)
                    ACE.after(e, freed)
                    return ACE.did(ACE.e.activation(on[:, j, :], att[:, lt, :], ACT.Square, accum_out=ss[:, lt:lt + 1])), j

                for n in range(N + 2):
                    if n < N:
                        scores(n)
                    if n >= 2:
                        mix(n - 2, 1)
                        if (n - 2) % PH == PH - 1:
                            e, j = project((n - 2) // PH)
                            on_ring.free[j] = e
                    if 1 <= n <= N:
                        turn(n - 1, 0)
                        turn(n - 1, 1)
                        mix(n - 1, 0)

                DVE.after(ACE.last())
                e = rsqrt(ss[:, :], [scr[:, i, :] for i in range(3)], 1e-6, 1.0 / C)
                DVE.after(e)
                ring = Ring(bank)
                PE.after(DVE.last(), ACE.last())
                for m in range(LT):
                    an_done = DVE.did(DVE.e.tensor_scalar_mul(att[:, m, :], att[:, m, :], ss[:, m:m + 1]))
                PE.after(an_done)
                for c in range(CT):
                    i, ps, free = ring.take()
                    PE.after(free)
                    for m in range(LT):
                        mm = transpose(ps[:, m * P:(m + 1) * P], att[:, m, c * P:(c + 1) * P])
                    DVE.after(PE.did(mm))
                    ring.free[i] = n_done = DVE.did(DVE.e.tensor_scalar_mul(nT[:, c, :], ps, vec[:, 2 * CT + c:2 * CT + c + 1]))
                DVE.after(PE.last())
                for m in range(LT):
                    r_done = DVE.did(DVE.e.tensor_tensor(att[:, m, :], X[:, b, m, :], b2[:, :], ALU.add))
                PE.after(n_done)
                h_done = []
                for m in range(MT):
                    i, ps, free = ring.take()
                    PE.after(free)
                    for k in range(CT):
                        mm = PE.e.matmul(ps, m1[:, k, m * P:(m + 1) * P], nT[:, k, :], start=k == 0, stop=k == CT - 1)
                    ACE.after(PE.did(mm))
                    ring.free[i] = e = ACE.did(ACE.e.activation(h1[m], ps, ACT.Gelu_apprx_tanh,
                                                                bias=vec[:, 3 * CT + m:3 * CT + m + 1]))
                    h_done.append(e)
                PE.after(h_done[-1], got_m2)
                for q in range(MT // 4):
                    if q:
                        SP.after(PE.last())
                        PE.after(load(m2[:, :, :], t["l3_m2"][q]))
                    for m in range(LT):
                        for k in range(4):
                            mm = PE.e.matmul(bank[m], h1[4 * q + k][:, m * P:(m + 1) * P], m2[:, k, :],
                                             start=q == 0 and k == 0, stop=q == MT // 4 - 1 and k == 3)
                    PE.did(mm)
                DVE.after(PE.last(), r_done)
                for m in range(LT):
                    e = DVE.did(DVE.e.tensor_tensor(att[:, m, :], bank[m], att[:, m, :], ALU.add))
                SP.after(e)
                SP.e.dma_start(t["out"][b], att[:, :, :]).then_inc(store_sem, 16)
                end_of_step(stored=16)


def lay_out(inputs):
    import numpy as np
    a = {k: np.asarray(v) for k, v in inputs.items()}

    def w_tiles(w):
        return w.reshape(-1, P, w.shape[1]).transpose(1, 0, 2)

    def cols(v):
        return v.reshape(-1, P).T

    def tokens(x):
        return x.reshape(B, LT, P, -1).transpose(0, 2, 1, 3)

    def chans(x):
        return x.transpose(0, 2, 1).reshape(B, CT, P, L).transpose(0, 2, 1, 3)

    x, ctx = a["x"], a["ctx_2048"]
    o = {"x": tokens(x), "xT": chans(x), "cT": chans(ctx), "mask": tokens(a["mask_Bx1xSxS2_ff0"][:, 0]),
         "keymask": a["mask_BxS2_ik0"]}
    p = "L0_xattn_"
    o["l0_wq"], o["l0_wv"], o["l0_wo"] = (w_tiles(a[p + n]) for n in ("Wq", "Wv", "Wo"))
    wk = np.zeros((C, 2 * CT, 4, 2, HD), np.float32)
    bk = np.zeros((2 * CT, 4, 2, HD), np.float32)
    for c in range(CT):
        for r in range(4):
            kh = 2 * c + r // 2
            for half in range(2):
                wk[:, 2 * c + half, r, half] = a[p + "Wk"][:, kh * HD:(kh + 1) * HD]
                bk[2 * c + half, r, half] = a[p + "bk"][kh * HD:(kh + 1) * HD]
    o["l0_wk"] = wk.reshape(CT, P, 2 * CT, P).transpose(1, 0, 2, 3)
    o["l0_bk"], o["l0_bq"] = cols(bk.reshape(-1)), cols(a[p + "bq"])
    for n in ("bv", "bo", "gamma", "beta"):
        o["l0_" + n] = a[p + n]

    both = {"w1": [], "w2": [], "dw1": [], "dw2": [], "w": [], "vec": []}
    for layer, order in ((1, (0, 1, 2, 3, 4)), (2, (1, 0, 2, 3, 4))):
        p = f"L{layer}_xattn_"
        ffn = p + ("f" if layer == 1 else "ffn_")
        if layer == 1:
            maa = [a[p + "maa_" + n] for n in "wkvrg"]
        else:
            maa = [a[p + "maa_stack"][f] for f in order]
        order = list(order)
        both["w1"].append(w_tiles(a[p + "maa_w1"].reshape(C, NF, DM)[:, order].reshape(C, NF * DM)))
        both["w2"].append(a[p + "maa_w2"][order].reshape(NF * DM, C))
        both["dw1"].append(w_tiles(a[p + "decay_w1"]))
        both["dw2"].append(a[p + "decay_w2"])
        both["w"].append(np.stack([w_tiles(a[n].T) for n in (p + "Wr", p + "Wk", p + "Wv", p + "Wg", p + "Wo",
                                                            ffn + "Wk", ffn + "Wr", ffn + "Wv")]))
        v = [a[p + "ln1_w"], a[p + "ln1_b"], a[p + "maa_x"], *maa, a[p + "time_decay"], a[p + "faaaa"].reshape(C),
             a[p + "gn_w"], a[p + "gn_b"], a[p + "ln2_w"], a[p + "ln2_b"], a[ffn + "maa_k"], a[ffn + "maa_r"]]
        both["vec"].append(np.stack([cols(u) for u in v], axis=1))
    for n, v in both.items():
        o["rw_" + n] = np.stack(v)
    o["prev"] = ctx[:, 0:2].reshape(B, 2, CT, P).transpose(0, 3, 1, 2)
    o["s0"] = ctx[:, 2:2 + RS].reshape(B, CT, P, RS).transpose(0, 2, 1, 3)

    p = "L3_xattn_"
    kv = a[p + "kv_w"].reshape(C, C, 2)
    kvb = a[p + "kv_b"].reshape(C, 2)
    o["l3_wq"], o["l3_wo"], o["l3_m1"] = (w_tiles(a[p + n]) for n in ("q_w", "out_w", "mlp_w1"))
    o["l3_wk"], o["l3_wv"] = w_tiles(kv[:, :, 0]), w_tiles(kv[:, :, 1])
    o["l3_m2"] = a[p + "mlp_w2"].reshape(MT // 4, 4, P, C).transpose(0, 2, 1, 3)
    o["l3_vec"] = np.concatenate([cols(a[p + "q_b"]), cols(kvb[:, 0]), cols(a[p + "postnorm_w"]), cols(a[p + "mlp_b1"])], axis=1)
    o["l3_bv"], o["l3_bo"], o["l3_b2"] = kvb[:, 1], a[p + "out_b"], a[p + "mlp_b2"]
    return {k: np.ascontiguousarray(v) for k, v in o.items()}


def kernel(**inputs):
    import concourse.bacc as bacc
    from concourse.bass_utils import run_bass_kernel_spmd

    nc = bacc.Bacc("TRN2", target_bir_lowering=False, num_devices=1)
    arrays = lay_out(inputs)
    t = {n: nc.dram_tensor("in_" + n, v.shape, mybir.dt.from_np(v.dtype), kind="ExternalInput").ap()
         for n, v in arrays.items()}
    t["out"] = nc.dram_tensor("out", (B, P, LT, C), F32, kind="ExternalOutput").ap()
    program(nc, t)
    r = run_bass_kernel_spmd(nc, [{"in_" + n: v for n, v in arrays.items()}], core_ids=[0])
    return r.results[0]["out"].transpose(0, 2, 1, 3).reshape(B, L, C)
```

```python
import concourse.bass as bass
from concourse import mybir
from contextlib import ExitStack

F32 = mybir.dt.float32
I32 = mybir.dt.int32
F32R = mybir.dt.float32r
BF16 = mybir.dt.bfloat16
ALU = mybir.AluOpType
ACT = mybir.ActivationFunctionType
AX = mybir.AxisListType

P = 128
B, L, C = 4, 512, 512
CT, LT = C // P, L // P
BANK = 512
NBANK = 8

QH, KVH = 32, 8
HD = C // QH
NL = 2
RH, RS = 32, 16
HPT = P // RS
NF, DM, DD = 5, 32, 64
DECAY, KEY, VALUE, RECEPT, GATE = range(NF)
PH = 16
PD = C // PH
NK = 2 * L
MLP = 4 * C
MT = MLP // P

MASKED = -1.0e30

(V_LN1W, V_LN1B, V_MAAX, V_MAA, V_TD, V_U, V_GNW, V_GNB, V_LN2W, V_LN2B, V_FK, V_FR, V_N) = \
    (0, 1, 2, 3, 8, 9, 10, 11, 12, 13, 14, 15, 16)
W_R, W_K, W_V, W_G, W_O, W_FK, W_FR, W_FV = range(8)


class Queue:

    def __init__(self, engine, sem):
        self.e, self.sem, self.count, self.seen = engine, sem, 0, {}

    def after(self, *events):
        for ev in events:
            if ev is None:
                continue
            sem, value = ev
            if self.seen.get(id(sem), 0) < value:
                self.e.wait_ge(sem, value)
                self.seen[id(sem)] = value
        return self.e

    def did(self, instruction):
        instruction.then_inc(self.sem, 1)
        self.count += 1
        return (self.sem, self.count)

    def last(self):
        return (self.sem, self.count) if self.count else None

    def reset(self):
        self.count, self.seen = 0, {}


class Ring:

    def __init__(self, bufs):
        self.bufs, self.free, self.at = list(bufs), [None] * len(bufs), -1

    def take(self):
        self.at = (self.at + 1) % len(self.bufs)
        return self.at, self.bufs[self.at], self.free[self.at]


def program(nc, t):
    top = ExitStack()
    with top:
        def sem(name):
            return top.enter_context(nc.semaphore(name))

        PE = Queue(nc.tensor, sem("pe_done"))
        DVE = Queue(nc.vector, sem("dve_done"))
        ACE = Queue(nc.scalar, sem("act_done"))
        POOL = Queue(nc.gpsimd, sem("pool_done"))
        SP = Queue(nc.sync, None)
        queues = (PE, DVE, ACE, POOL, SP)
        load_sems = [sem(f"dma{i}") for i in range(48)]
        store_sem = sem("store")
        loads = [0]

        def load(dst, src, q=None):
            q = q or SP
            s = load_sems[loads[0]]
            loads[0] += 1
            q.e.dma_start(dst, src).then_inc(s, 16)
            return (s, 16)

        def load_all(pairs, q=None, again=None):
            q = q or SP
            if again is None:
                s, n = load_sems[loads[0]], 0
                loads[0] += 1
            else:
                s, n = again
            for dst, src in pairs:
                q.e.dma_start(dst, src).then_inc(s, 16)
            return (s, n + 16 * len(pairs))

        def end_of_step(stored=0):
            if stored:
                SP.e.wait_ge(store_sem, stored)
            nc.all_engine_barrier()
            for s in [q.sem for q in queues if q.sem is not None] + load_sems[:loads[0]] + ([store_sem] if stored else []):
                nc.gpsimd.sem_clear(s)
            nc.all_engine_barrier()
            loads[0] = 0
            for q in queues:
                q.reset()

        def sb(name, shape, ctx=top, dt=F32):
            return ctx.enter_context(nc.sbuf_tensor(name, shape, dt))

        psum = top.enter_context(nc.psum_tensor("psum", [P, NBANK * BANK], F32))
        bank = [psum[:, i * BANK:(i + 1) * BANK] for i in range(NBANK)]

        xs = nc.dram_tensor("x_scratch", (B, P, LT, C), F32, kind="Internal").ap()
        q_parts = nc.dram_tensor("q_parts", (3, C, L), BF16, kind="Internal").ap()
        k0_parts = nc.dram_tensor("k0_parts", (3, KVH * HD, L), BF16, kind="Internal").ap()
        k3_parts = nc.dram_tensor("k3_parts", (3, C, NK), BF16, kind="Internal").ap()
        ident = sb("ident", [P, P])
        headsum = sb("headsum", [P, HPT])

        ev = POOL.did(POOL.e.memset(ident[:, :], 0.0))
        POOL.after(ev)
        ev_ident = POOL.did(POOL.e.affine_select(out=ident[:, :], in_=ident[:, :], compare_op=ALU.not_equal,
                                                 fill=1.0, base=0, pattern=[[-1, P]], channel_multiplier=1))
        DVE.after(ev_ident)
        DVE.did(DVE.e.tensor_reduce(headsum[:, :], ident[:, :].rearrange("p (h i) -> p h i", i=RS),
                                    axis=AX.X, op=ALU.add))
        end_of_step()

        def split3(v, v_ready, rest, parts, parts_free):
            ACE.after(v_ready, parts_free)
            e = ACE.did(ACE.e.activation(parts[0], v, ACT.Copy))
            for n in (1, 2):
                POOL.after(e, v_ready, parts_free)
                e = POOL.did(POOL.e.tensor_tensor(rest, v if n == 1 else rest, parts[n - 1], ALU.subtract))
                ACE.after(e)
                e = ACE.did(ACE.e.activation(parts[n], rest, ACT.Copy))
            return e

        def transpose(out, in_):
            return PE.e.transpose(out, in_, ident[:, :])

        def rsqrt(a, scratch, add, mul=1.0):
            v, y, u = scratch
            e = DVE.did(DVE.e.tensor_scalar(v, a, mul, add, ALU.mult, ALU.add))
            DVE.after(e)
            e = DVE.did(DVE.e.tensor_single_scalar(u.bitcast(I32), v.bitcast(I32), 1, ALU.arith_shift_right))
            DVE.after(e)
            e = DVE.did(DVE.e.tensor_scalar(y.bitcast(I32), u.bitcast(I32), -1.0, float(0x5F3759DF), ALU.mult, ALU.add))
            for n in range(4):
                DVE.after(e)
                e = DVE.did(DVE.e.tensor_tensor(u, y, y, ALU.mult))
                DVE.after(e)
                e = DVE.did(DVE.e.tensor_tensor(u, u, v, ALU.mult))
                DVE.after(e)
                e = DVE.did(DVE.e.tensor_scalar(u, u, -0.5, 1.5, ALU.mult, ALU.add))
                DVE.after(e)
                e = DVE.did(DVE.e.tensor_tensor(a if n == 3 else y, y, u, ALU.mult))
            return e

        def norm_stats(tiles, ready, stats, mv, rstd, scratch, eps):
            es = []
            for i, x in enumerate(tiles):
                DVE.after(ready[i])
                es.append(DVE.did(DVE.e.bn_stats(stats[:, i, :], x)))
            for i, e in enumerate(es):
                DVE.after(e)
                e2 = DVE.did(DVE.e.bn_aggr(mv[:, i, :], stats[:, i, :]))
            DVE.after(e2)
            e = DVE.did(DVE.e.tensor_copy(rstd, mv[:, :, 1]))
            DVE.after(e)
            return rsqrt(rstd, scratch, eps)

        with ExitStack() as ctx:
            wq = sb("l0_wq", [P, CT, C], ctx)
            wk = sb("l0_wk", [P, CT, P], ctx)
            wv = sb("l0_wv", [P, CT, P], ctx)
            wo = sb("l0_wo", [P, CT, C], ctx)
            bq = sb("l0_bq", [P, CT], ctx)
            bk = sb("l0_bk", [P, 1], ctx)
            bv = sb("l0_bv", [P, KVH * HD], ctx)
            bo = sb("l0_bo", [P, C], ctx)
            gamma = sb("l0_gamma", [P, C], ctx)
            beta = sb("l0_beta", [P, C], ctx)
            xT = sb("l0_xT", [P, CT, L], ctx)
            cT = sb("l0_cT", [P, CT, L], ctx)
            xin = sb("l0_x", [P, LT, C], ctx)
            mask = sb("l0_mask", [P, LT, L], ctx)
            qf = sb("l0_qf", [P, 2, L], ctx)
            rest = sb("l0_rest", [P, 2, L], ctx)
            parts = sb("l0_parts", [P, 2, 3, L], ctx, BF16)
            qs = sb("l0_qs", [6 * HD, QH, L], ctx, BF16)
            ks = sb("l0_ks", [6 * HD, KVH, L], ctx, BF16)
            vp = sb("l0_vp", [P, LT, KVH, 3 * HD], ctx)
            nz = sb("l0_nz", [P, 3, L], ctx)
            pr = sb("l0_p", [P, 2 * LT, L], ctx)
            pT = sb("l0_pT", [P, 3, L], ctx)
            nmax = sb("l0_nmax", [P, QH * LT], ctx)
            den = sb("l0_den", [P, QH * LT], ctx)
            rden = sb("l0_rden", [P, QH * LT], ctx)
            rdx = sb("l0_rdx", [P, LT, P], ctx)
            rdT = sb("l0_rdT", [P, L], ctx)
            oT = sb("l0_oT", [P, CT, L], ctx)
            stats = sb("l0_stats", [P, LT, 6], ctx)
            mv = sb("l0_mv", [P, LT, 2], ctx)
            rstd = sb("l0_rstd", [P, LT], ctx)
            scr = sb("l0_scr", [P, 3, LT], ctx)

            SP.after(load(wq[:, :, :], t["l0_wq"]), load(wk[:, :, :], t["l0_wk"], ACE), load(wv[:, :, :], t["l0_wv"]),
                     load(wo[:, :, :], t["l0_wo"]), load(bq[:, :], t["l0_bq"], ACE), load(bk[:, :], t["l0_bk"], ACE),
                     load(bv[:, :], t["l0_bv"].partition_broadcast(P)), load(bo[:, :], t["l0_bo"].partition_broadcast(P)),
                     load(gamma[:, :], t["l0_gamma"].partition_broadcast(P)),
                     load(beta[:, :], t["l0_beta"].partition_broadcast(P)))
            DVE.did(DVE.e.memset(vp[:, :, :, HD:2 * HD], 0.0))
            end_of_step()

            with nc.Fori(0, B) as b:
                got_x = load(xT[:, :, :], t["xT"][b])
                got_c = load(cT[:, :, :], t["cT"][b], ACE)
                got_m = load(mask[:, :, :], t["mask"][b])
                got_xin = load(xin[:, :, :], t["x"][b])

                ring = Ring(bank)
                qf_ring, part_ring = Ring(range(2)), Ring(range(2))
                PE.after(got_x, got_c)
                stored_parts = []
                for m in (CT, *range(CT)):
                    i, ps, free = ring.take()
                    PE.after(free)
                    w, x, bias, scale = (wk, cT, bk, 1.0) if m == CT else (wq, xT, bq, HD ** -0.5)
                    o = 0 if m == CT else m
                    for k in range(CT):
                        mm = PE.e.matmul(ps, w[:, k, o * P:(o + 1) * P], x[:, k, :], start=k == 0, stop=k == CT - 1)
                    a, _, free = qf_ring.take()
                    DVE.after(PE.did(mm), free)
                    e = ring.free[i] = DVE.did(DVE.e.tensor_scalar(qf[:, a, :], ps, bias[:, o:o + 1], scale, ALU.add, ALU.mult))
                    p, _, free = part_ring.take()
                    e = qf_ring.free[a] = split3(qf[:, a, :], e, rest[:, a, :], [parts[:, p, n, :] for n in range(3)], free)
                    SP.after(e)
                    dst = k0_parts if m == CT else q_parts[:, m * P:(m + 1) * P, :]
                    e = part_ring.free[p] = load(dst.rearrange("n p l -> p n l"), parts[:, p, :, :])
                    stored_parts.append(e)
                pairs = []
                SP.after(*stored_parts)
                for slot, (qn, kn) in enumerate(((0, 0), (0, 1), (0, 2), (1, 0), (1, 1), (2, 0))):
                    rows = slice(slot * HD, (slot + 1) * HD)
                    pairs.append((ks[rows, :, :], k0_parts[kn].rearrange("(h i) l -> i h l", i=HD)))
                    pairs.append((qs[rows, :, :], q_parts[qn].rearrange("(h i) l -> i h l", i=HD)))
                got_qk = load_all(pairs)
                i, ps, free = ring.take()
                PE.after(free)
                for s in range(LT):
                    for k in range(CT):
                        mm = PE.e.matmul(ps[:, s * P:(s + 1) * P], cT[:, k, s * P:(s + 1) * P], wv[:, k, :],
                                         start=k == 0, stop=k == CT - 1)
                DVE.after(PE.did(mm))
                for half in (0, 2):
                    v_done = DVE.did(DVE.e.tensor_tensor(
                        vp[:, :, :, half * HD:(half + 1) * HD], ps.rearrange("p (s h d) -> p s h d", s=LT, h=KVH),
                        bv[:, :].rearrange("p (h d) -> p h d", h=KVH).unsqueeze(1).broadcast_to([P, LT, KVH, HD]), ALU.add))
                POOL.after(got_xin)
                for m in range(LT):
                    xb_done = POOL.did(POOL.e.tensor_tensor(xin[:, m, :], xin[:, m, :], bo[:, :], ALU.add))
                PE.after(v_done, got_qk)
                DVE.after(got_m)

                s_ring, t_ring, o_ring = Ring(bank[0:3]), Ring(bank[3:6]), Ring(bank[6:8])
                for r in (s_ring, t_ring, o_ring):
                    r.free = [v_done] * len(r.bufs)
                nz_ring, pr_ring, pT_ring = Ring(range(3)), Ring(range(2 * LT)), Ring(range(3))
                item = {}
                oT_done = []
                rd_free = [None]

                def scores(h, lt):
                    n = h * LT + lt
                    i, ps, free = s_ring.take()
                    PE.after(free)
                    mm = PE.did(PE.e.matmul(ps, qs[:, h, lt * P:(lt + 1) * P], ks[:, h // (QH // KVH), :], start=True, stop=True))
                    a, _, freed = nz_ring.take()
                    DVE.after(mm, freed)
                    z = s_ring.free[i] = DVE.did(DVE.e.tensor_tensor_reduce(
                        out=nz[:, a, :], in0=ps, in1=mask[:, lt, :], scale=-1.0, scalar=3.0e38,
                        op0=ALU.add, op1=ALU.min, accum_out=nmax[:, n:n + 1]))
                    i, _, freed = pr_ring.take()
                    ACE.after(z, freed)
                    e = nz_ring.free[a] = ACE.did(ACE.e.activation(pr[:, i, :], nz[:, a, :], ACT.Exp, scale=-1.0,
                                                                   bias=nmax[:, n:n + 1], accum_out=den[:, n:n + 1]))
                    item[(h, lt)] = (i, e)

                def turn(h, s):
                    j, ps, free = t_ring.take()
                    PE.after(free)
                    for lt in range(LT):
                        i, e = item[(h, lt)]
                        PE.after(e)
                        mm = transpose(ps[:, lt * P:(lt + 1) * P], pr[:, i, s * P:(s + 1) * P])
                    mm = PE.did(mm)
                    if s == LT - 1:
                        for lt in range(LT):
                            pr_ring.free[item.pop((h, lt))[0]] = mm
                    k, _, freed = pT_ring.take()
                    if s % 2:
                        DVE.after(mm, freed)
                        e = DVE.did(DVE.e.tensor_copy(pT[:, k, :], ps))
                    else:
                        ACE.after(mm, freed)
                        e = ACE.did(ACE.e.activation(pT[:, k, :], ps, ACT.Copy))
                    t_ring.free[j] = e
                    item[("pT", h, s)] = (k, e)

                def mix(h, s):
                    k, e = item.pop(("pT", h, s))
                    c, r = divmod(h, HPT)
                    if r == 0 and s == 0:
                        item["o"] = o_ring.take()
                        PE.after(item["o"][2])
                    oi, ops, _ = item["o"]
                    PE.after(e)
                    quad, odd = 32 * (r // 2), r % 2
                    mm = PE.e.matmul(ops[quad:quad + 32, :], vp[:, s, h // (QH // KVH), odd * HD:(odd + 2) * HD], pT[:, k, :],
                                     start=odd == 0 and s == 0, stop=odd == 1 and s == LT - 1)
                    pT_ring.free[k] = mm = PE.did(mm)
                    if r == HPT - 1 and s == LT - 1:
                        normalise(c, oi, ops, mm)

                def normalise(c, oi, ops, mm):
                    sl = slice(c * HPT * LT, (c + 1) * HPT * LT)
                    DVE.after(ACE.last(), rd_free[0])
                    e = DVE.did(DVE.e.reciprocal(rden[:, sl], den[:, sl]))
                    DVE.after(e)
                    e = DVE.did(DVE.e.tensor_copy(
                        rdx[:, :, :].rearrange("p l (h d) -> p l h d", h=HPT),
                        rden[:, sl].rearrange("p (h l) -> p l h", l=LT).unsqueeze(3).broadcast_to([P, LT, HPT, HD])))
                    i, ps, free = t_ring.take()
                    PE.after(e, free)
                    for lt in range(LT):
                        m2 = PE.e.matmul(ps[:, lt * P:(lt + 1) * P], rdx[:, lt, :], ident[:, :], start=True, stop=True)
                    rd_free[0] = PE.did(m2)
                    ACE.after(rd_free[0], oT_done[-1] if oT_done else None)
                    e = t_ring.free[i] = ACE.did(ACE.e.activation(rdT[:, :], ps, ACT.Copy))
                    DVE.after(e, mm)
                    e = o_ring.free[oi] = DVE.did(DVE.e.tensor_tensor(oT[:, c, :], ops, rdT[:, :], ALU.mult))
                    oT_done.append(e)

                for h in range(QH + 1):
                    for s in range(LT):
                        if h < QH:
                            scores(h, s)
                        if h >= 1:
                            turn(h - 1, s)
                            if s:
                                mix(h - 1, s - 1)
                    if h >= 1:
                        mix(h - 1, LT - 1)

                PE.after(*oT_done)
                wo_done = []
                for lt in range(LT):
                    i, ps, free = s_ring.take()
                    PE.after(free)
                    for c in range(CT):
                        mm = PE.e.matmul(ps, oT[:, c, lt * P:(lt + 1) * P], wo[:, c, :], start=c == 0, stop=c == CT - 1)
                    DVE.after(PE.did(mm), xb_done)
                    e = s_ring.free[i] = DVE.did(DVE.e.tensor_tensor(xin[:, lt, :], ps, xin[:, lt, :], ALU.add))
                    wo_done.append(e)

                e = norm_stats([xin[:, m, :] for m in range(LT)], wo_done, stats, mv, rstd[:, :],
                               [scr[:, i, :] for i in range(3)], 1e-6)
                DVE.after(e)
                for m in range(LT):
                    e = DVE.did(DVE.e.tensor_scalar(xin[:, m, :], xin[:, m, :], mv[:, m, 0:1], rstd[:, m:m + 1],
                                                    ALU.subtract, ALU.mult))
                    POOL.after(e)
                    e = POOL.did(POOL.e.tensor_tensor(xin[:, m, :], xin[:, m, :], gamma[:, :], ALU.mult))
                    POOL.after(e)
                    e = POOL.did(POOL.e.tensor_tensor(xin[:, m, :], xin[:, m, :], beta[:, :], ALU.add))
                SP.after(e)
                SP.after(load(xs[b], xin[:, :, :]))
                end_of_step()

        with ExitStack() as ctx:
            w1 = sb("rw_w1", [P, CT, NF * DM], ctx)
            w2 = sb("rw_w2", [P, NF, C], ctx)
            dw1 = sb("rw_dw1", [P, CT, DD], ctx)
            dw2 = sb("rw_dw2", [P, C], ctx)
            W = sb("rw_w", [P, 8, CT, C], ctx)
            vec = sb("rw_vec", [P, V_N, CT], ctx)
            xw = sb("rw_x", [P, LT, C], ctx)
            xn = sb("rw_xn", [P, LT, C], ctx)
            xa = sb("rw_xa", [P, CT, L + 1], ctx)
            sx = sb("rw_sx", [P, CT, L], ctx)
            big = sb("rw_big", [P, 4 * (L + 1) + 4 * L], ctx)
            xf = [big[:, f * CT * L:(f + 1) * CT * L].rearrange("p (c l) -> p c l", c=CT) for f in range(2)]
            S = big[:, 0:4 * (L + 1)].rearrange("p (n l) -> p n l", n=4)
            kvb = big[:, 4 * (L + 1):4 * (L + 1) + 2 * L].rearrange("p (n l) -> p n l", n=2)
            rs = big[:, 4 * (L + 1) + 2 * L:].rearrange("p (n l) -> p n l", n=2)
            tm = sb("rw_tm", [P, L], ctx)
            tmb = sb("rw_tmb", [P, L], ctx)
            dT = sb("rw_dT", [P, L], ctx)
            wT = sb("rw_wT", [P, CT, L], ctx)
            kT = sb("rw_kT", [P, CT, L], ctx)
            vh = sb("rw_vh", [P, CT, L], ctx, F32R)
            vl = sb("rw_vl", [P, CT, L], ctx, F32R)
            rT = sb("rw_rT", [P, CT, L], ctx)
            gT = sb("rw_gT", [P, CT, L], ctx)
            prev = sb("rw_prev", [P, 2, CT], ctx)
            s0 = sb("rw_s0", [P, CT, RS], ctx)
            tmp = sb("rw_tmp", [P, 2, L], ctx)
            ruk = sb("rw_ruk", [P, LT, HPT], ctx)
            stats = sb("rw_stats", [P, LT, 6], ctx)
            mv = sb("rw_mv", [P, LT, 2], ctx)
            rstd = sb("rw_rstd", [P, LT], ctx)
            scr = sb("rw_scr", [P, 3, LT * HPT], ctx)
            gm = sb("rw_gm", [P, 2, LT * HPT], ctx)
            small = [scr[:, i, 0:LT] for i in range(3)]
            pick = sb("rw_pick", [P, RS, P], ctx, F32R)
            place = sb("rw_place", [P, RS, P], ctx)
            identr = sb("rw_identr", [P, P], ctx, F32R)
            DVE.did(DVE.e.tensor_copy(identr[:, :], ident[:, :]))
            e = POOL.did(POOL.e.memset(place[:, :, :], 0.0))
            DVE.after(e)
            for j in range(RS):
                DVE.did(DVE.e.tensor_copy(
                    pick[:, j, :].rearrange("p (h i) -> p h i", i=RS),
                    ident[:, :].rearrange("p (h i) -> p h i", i=RS)[:, :, j:j + 1].broadcast_to([P, HPT, RS])))
                DVE.did(DVE.e.tensor_copy(place[:, j, :].rearrange("p (h i) -> p h i", i=RS)[:, :, j], headsum[:, :]))
            DVE.did(DVE.e.memset(tmb[:, :], 0.0))
            DVE.did(DVE.e.memset(dT[:, :], 0.0))
            end_of_step()

            with nc.Fori(0, NL) as layer:
                SP.after(load(w1[:, :, :], t["rw_w1"][layer]), load(w2[:, :, :], t["rw_w2"][layer]),
                         load(dw1[:, :, :], t["rw_dw1"][layer], ACE),
                         load(dw2[:, :], t["rw_dw2"][layer]), load(vec[:, :, :], t["rw_vec"][layer], ACE),
                         *[load(W[:, i, :, :], t["rw_w"][layer, i], (SP, ACE)[i % 2]) for i in range(8)])
                end_of_step()

                with nc.Fori(0, B) as b:
                    got_x = load(xw[:, :, :], xs[b])
                    got_s0 = load(s0[:, :, :], t["s0"][b])
                    got_prev = load(prev[:, :, :], t["prev"][b], ACE)

                    def vcol(v, c):
                        return vec[:, v, c:c + 1]

                    def shifted_norm(vw, vb, ready, xa_free):
                        e = norm_stats([xw[:, m, :] for m in range(LT)], ready, stats, mv, rstd[:, :], small, 1e-5)
                        DVE.after(e)
                        done = [DVE.did(DVE.e.tensor_scalar(xn[:, m, :], xw[:, m, :], mv[:, m, 0:1], rstd[:, m:m + 1],
                                                            ALU.subtract, ALU.mult)) for m in range(LT)]
                        ACE.after(xa_free)
                        out = []
                        for c in range(CT):
                            i, ps, free = ring.take()
                            PE.after(free)
                            for m in range(LT):
                                PE.after(done[m])
                                mm = transpose(ps[:, m * P:(m + 1) * P], xn[:, m, c * P:(c + 1) * P])
                            ACE.after(PE.did(mm))
                            e = ring.free[i] = ACE.did(ACE.e.activation(xa[:, c, 1:L + 1], ps, ACT.Identity,
                                                                        scale=vcol(vw, c), bias=vcol(vb, c)))
                            POOL.after(e)
                            out.append(POOL.did(POOL.e.tensor_tensor(sx[:, c, :], xa[:, c, 0:L], xa[:, c, 1:L + 1],
                                                                     ALU.subtract)))
                        return out

                    ring = Ring(bank)
                    POOL.after(got_prev)
                    POOL.after(POOL.did(POOL.e.tensor_copy(xa[:, :, 0], prev[:, 1, :])))
                    sx_done = shifted_norm(V_LN1W, V_LN1B, [got_x] * LT, None)

                    for c in range(CT):
                        DVE.after(sx_done[c])
                        xx_done = DVE.did(DVE.e.scalar_tensor_tensor(xf[0][:, c, :], sx[:, c, :], vcol(V_MAAX, c),
                                                                     xa[:, c, 1:L + 1], ALU.mult, ALU.add))
                    PE.after(xx_done)
                    i, ps, free = ring.take()
                    PE.after(free)
                    for k in range(CT):
                        mm = PE.e.matmul(ps, w1[:, k, 0:P], xf[0][:, k, :], start=k == 0, stop=k == CT - 1)
                    ACE.after(PE.did(mm))
                    e = ring.free[i] = ACE.did(ACE.e.activation(tm[:, :], ps, ACT.Tanh))
                    i, ps, free = ring.take()
                    PE.after(free)
                    for k in range(CT):
                        mm = PE.e.matmul(ps[0:DM, :], w1[:, k, P:P + DM], xf[0][:, k, :], start=k == 0, stop=k == CT - 1)
                    xf_free = [PE.did(mm), None]
                    ACE.after(xf_free[0])
                    e2 = ring.free[i] = ACE.did(ACE.e.activation(tmb[0:DM, :], ps[0:DM, :], ACT.Tanh))
                    PE.after(e, e2)

                    def mixed(f, slot):
                        out = []
                        for c in range(CT):
                            i, ps, free = ring.take()
                            PE.after(free)
                            mm = PE.e.matmul(ps, w2[:, f, c * P:(c + 1) * P], (tm if f < 4 else tmb)[:, :], start=True, stop=True)
                            DVE.after(PE.did(mm), xf_free[slot])
                            e = ring.free[i] = DVE.did(DVE.e.scalar_tensor_tensor(
                                xf[slot][:, c, :], ps, vcol(V_MAA + f, c), sx[:, c, :], ALU.add, ALU.mult))
                            POOL.after(e)
                            out.append(POOL.did(POOL.e.tensor_tensor(xf[slot][:, c, :], xf[slot][:, c, :],
                                                                     xa[:, c, 1:L + 1], ALU.add)))
                        return out

                    def gemm_T(w, x, n_out, evac, k_ready=()):
                        for m in range(n_out):
                            i, ps, free = ring.take()
                            PE.after(free)
                            for k in range(CT):
                                if m == 0 and k_ready:
                                    PE.after(k_ready[k])
                                mm = PE.e.matmul(ps, w[:, k, m * P:(m + 1) * P], x[:, k, :], start=k == 0, stop=k == CT - 1)
                            ring.free[i] = evac(m, ps, PE.did(mm))

                    ready = mixed(DECAY, 0)
                    ready2 = mixed(KEY, 1)
                    i, ps, free = ring.take()
                    PE.after(free)
                    for k in range(CT):
                        PE.after(ready[k])
                        mm = PE.e.matmul(ps[0:DD, :], dw1[:, k, :], xf[0][:, k, :], start=k == 0, stop=k == CT - 1)
                    xf_free[0] = PE.did(mm)
                    ACE.after(xf_free[0])
                    e = ring.free[i] = ACE.did(ACE.e.activation(dT[0:DD, :], ps[0:DD, :], ACT.Tanh))
                    PE.after(e)
                    for c in range(CT):
                        i, ps, free = ring.take()
                        PE.after(free)
                        mm = PE.did(PE.e.matmul(ps, dw2[:, c * P:(c + 1) * P], dT[:, :], start=True, stop=True))
                        ACE.after(mm)
                        e = ring.free[i] = ACE.did(ACE.e.activation(wT[:, c, :], ps, ACT.Exp, bias=vcol(V_TD, c)))
                        ACE.after(e)
                        w_done = ACE.did(ACE.e.activation(wT[:, c, :], wT[:, c, :], ACT.Exp, scale=-1.0))

                    def copy_to(dst):
                        def evac(m, ps, mm):
                            ACE.after(mm)
                            return ACE.did(ACE.e.activation(dst[:, m, :], ps, ACT.Copy))
                        return evac

                    gemm_T(W[:, W_K, :, :], xf[1], CT, copy_to(kT), ready2)
                    xf_free[1] = PE.last()
                    ready = mixed(VALUE, 0)
                    ready2 = mixed(RECEPT, 1)

                    def split_v(m, ps, mm):
                        ACE.after(mm)
                        e = ACE.did(ACE.e.activation(vh[:, m, :], ps, ACT.Copy))
                        DVE.after(e)
                        return DVE.did(DVE.e.tensor_tensor(vl[:, m, :], ps, vh[:, m, :].bitcast(F32), ALU.subtract))
                    gemm_T(W[:, W_V, :, :], xf[0], CT, split_v, ready)
                    xf_free[0] = PE.last()
                    gemm_T(W[:, W_R, :, :], xf[1], CT, copy_to(rT), ready2)
                    ready = mixed(GATE, 0)
                    krv_done = ACE.last()

                    def gate(m, ps, mm):
                        ACE.after(mm)
                        DVE.after(ACE.did(ACE.e.activation(gT[:, m, :], ps, ACT.Sigmoid)))
                        return DVE.did(DVE.e.tensor_tensor(gT[:, m, :], ps, gT[:, m, :], ALU.mult))
                    gemm_T(W[:, W_G, :, :], xf[0], CT, gate, ready)
                    g_done = DVE.last()
                    front_done = (PE.last(), POOL.last(), DVE.last(), ACE.last())

                    bc_ring, y_ring, misc = Ring(bank[0:3]), Ring(bank[3:5]), Ring(bank[5:8])
                    for r in (bc_ring, y_ring, misc):
                        r.free = [DVE.last()] * len(r.bufs)
                    S_ring, kv_ring, rs_ring, tmp_ring = Ring(range(4)), Ring(range(2)), Ring(range(2)), Ring(range(2))
                    S_ring.free = [front_done[0]] * 4
                    DVE.after(*front_done, got_s0)
                    POOL.after(*front_done)
                    ACE.after(*front_done, got_s0)
                    PE.after(*front_done)
                    item = {}
                    yg = xn
                    yg_done = [None] * CT

                    def spread(n):
                        g, j = divmod(n, RS)
                        i, ps, free = bc_ring.take()
                        PE.after(free)
                        PE.e.matmul(ps, pick[:, j, :], vh[:, g, :], start=True, stop=False)
                        item[n] = (i, ps, PE.did(PE.e.matmul(ps, pick[:, j, :], vl[:, g, :], start=False, stop=True)))

                    def recur(n):
                        g, j = divmod(n, RS)
                        i, ps, mm = item[n]
                        a, _, free = kv_ring.take()
                        DVE.after(mm, free)
                        e = bc_ring.free[i] = DVE.did(DVE.e.tensor_tensor(kvb[:, a, :], ps, kT[:, g, :], ALU.mult))
                        s, _, free = S_ring.take()
                        ACE.after(free)
                        e0 = ACE.did(ACE.e.activation(S[:, s, 0:1], s0[:, g, j:j + 1], ACT.Copy))
                        DVE.after(e, free)
                        e = kv_ring.free[a] = DVE.did(DVE.e.tensor_tensor_scan(
                            S[:, s, 1:L + 1], wT[:, g, :], kvb[:, a, :], s0[:, g, j:j + 1], ALU.mult, ALU.add))
                        q = POOL
                        a, _, free = rs_ring.take()
                        q.after(e, e0, free)
                        e = S_ring.free[s] = q.did(q.e.tensor_tensor(rs[:, a, :], S[:, s, 0:L], rT[:, g, :], ALU.mult))
                        item[n] = (a, e)

                    def read(n):
                        g, j = divmod(n, RS)
                        a, e = item.pop(n)
                        if j == 0:
                            item["y"] = y_ring.take()
                            PE.after(item["y"][2])
                        yi, yps, _ = item["y"]
                        PE.after(e)
                        mm = PE.e.matmul(yps, place[:, j, :], rs[:, a, :], start=j == 0, stop=j == RS - 1)
                        rs_ring.free[a] = mm = PE.did(mm)
                        if j == RS - 1:
                            item[("g", g)] = (yi, yps, mm)

                    def group(g):
                        yi, yps, y_mm = item.pop(("g", g))
                        G = LT * HPT
                        ti, _, free = tmp_ring.take()
                        ta = tmp[:, ti, :]
                        DVE.after(free)
                        e = DVE.did(DVE.e.scalar_tensor_tensor(ta, rT[:, g, :], vcol(V_U, g), kT[:, g, :], ALU.mult, ALU.mult))
                        i, ps, free = misc.take()
                        PE.after(e, free)
                        for m in range(LT):
                            mm = PE.e.matmul(ps[:, m * HPT:(m + 1) * HPT], ta[:, m * P:(m + 1) * P], headsum[:, :],
                                             start=True, stop=True)
                        DVE.after(PE.did(mm))
                        e = misc.free[i] = DVE.did(DVE.e.tensor_copy(ruk[:, :, :].rearrange("p m h -> p (m h)"), ps[:, 0:G]))
                        i, ps, free = misc.take()
                        PE.after(free)
                        for m in range(LT):
                            for v in (vh, vl):
                                mm = PE.e.matmul(ps[:, m * P:(m + 1) * P], v[:, g, m * P:(m + 1) * P], identr[:, :],
                                                 start=v is vh, stop=v is vl)
                        DVE.after(PE.did(mm), e)
                        rows = ta.rearrange("p (g j) -> p g j", g=G)
                        e = misc.free[i] = DVE.did(DVE.e.tensor_tensor(
                            rows, ps.rearrange("p (g j) -> p g j", g=G),
                            ruk[:, :, :].rearrange("p m h -> p (m h)").unsqueeze(2).broadcast_to([P, G, RS]), ALU.mult))
                        ti2, _, free = tmp_ring.take()
                        tb = tmp[:, ti2, :]
                        ACE.after(y_mm, free)
                        ey = y_ring.free[yi] = ACE.did(ACE.e.activation(tb, yps, ACT.Copy))
                        i, ps, free = misc.take()
                        PE.after(ey, free)
                        for m in range(LT):
                            mm = transpose(ps[:, m * P:(m + 1) * P], tb[:, m * P:(m + 1) * P])
                        mm = PE.did(mm)
                        DVE.after(e, mm)
                        e = misc.free[i] = DVE.did(DVE.e.tensor_tensor(ta, ps, ta, ALU.add))
                        DVE.after(e)
                        e = DVE.did(DVE.e.tensor_reduce(gm[:, 0, :], rows, axis=AX.X, op=ALU.add))
                        DVE.after(e)
                        e = DVE.did(DVE.e.tensor_scalar_mul(gm[:, 0, :], gm[:, 0, :], 1.0 / RS))
                        DVE.after(e)
                        e = DVE.did(DVE.e.tensor_tensor(rows, rows, gm[:, 0, :].unsqueeze(2).broadcast_to([P, G, RS]),
                                                        ALU.subtract))
                        ACE.after(e, mm)
                        e = ACE.did(ACE.e.activation(tb, ta, ACT.Square))
                        DVE.after(e)
                        e = DVE.did(DVE.e.tensor_reduce(gm[:, 1, :], tb.rearrange("p (g j) -> p g j", g=G), axis=AX.X, op=ALU.add))
                        DVE.after(e)
                        e = rsqrt(gm[:, 1, :], [scr[:, q, :] for q in range(3)], 1e-5, 1.0 / RS)
                        DVE.after(e)
                        e = DVE.did(DVE.e.tensor_tensor(rows, rows, gm[:, 1, :].unsqueeze(2).broadcast_to([P, G, RS]), ALU.mult))
                        i, ps, free = misc.take()
                        PE.after(e, free)
                        for m in range(LT):
                            mm = transpose(ps[:, m * P:(m + 1) * P], ta[:, m * P:(m + 1) * P])
                        mm = PE.did(mm)
                        tmp_ring.free[ti] = tmp_ring.free[ti2] = mm
                        ACE.after(mm)
                        e = misc.free[i] = ACE.did(ACE.e.activation(yg[:, g, :], ps, ACT.Identity, scale=vcol(V_GNW, g),
                                                                    bias=vcol(V_GNB, g)))
                        POOL.after(e)
                        yg_done[g] = POOL.did(POOL.e.tensor_tensor(yg[:, g, :], yg[:, g, :], gT[:, g, :], ALU.mult))

                    N = CT * RS
                    spread(0)
                    spread(1)
                    for n in range(N + 1):
                        if n + 2 < N:
                            spread(n + 2)
                        if n < N:
                            recur(n)
                        if n >= 1:
                            read(n - 1)
                            if n % RS == 0:
                                group(n // RS - 1)

                    PE.after(*yg_done)
                    ring = Ring(bank)
                    ring.free = [DVE.last()] * 3 + [DVE.last()] * 2 + list(misc.free)
                    PE.after(DVE.last(), ACE.last())

                    def gemm_rows(w, x, kt, evac):
                        for m in range(LT):
                            i, ps, free = ring.take()
                            PE.after(free)
                            for k in range(kt):
                                mm = PE.e.matmul(ps, x[:, k, m * P:(m + 1) * P], w[:, k, :], start=k == 0, stop=k == kt - 1)
                            ring.free[i] = evac(m, ps, PE.did(mm))

                    x_done = [None] * LT

                    def add_x(m, ps, mm):
                        DVE.after(mm)
                        x_done[m] = DVE.did(DVE.e.tensor_tensor(xw[:, m, :], ps, xw[:, m, :], ALU.add))
                        return x_done[m]
                    gemm_rows(W[:, W_O, :, :], yg, CT, add_x)

                    POOL.after(POOL.did(POOL.e.tensor_copy(xa[:, :, 0], prev[:, 0, :])))
                    DVE.after(PE.last())
                    sx_done = shifted_norm(V_LN2W, V_LN2B, x_done, None)
                    for c in range(CT):
                        DVE.after(sx_done[c])
                        for v, dst in ((V_FK, xf[0]), (V_FR, xf[1])):
                            e = DVE.did(DVE.e.scalar_tensor_tensor(dst[:, c, :], sx[:, c, :], vcol(v, c), xa[:, c, 1:L + 1],
                                                                   ALU.mult, ALU.add))
                    PE.after(e)

                    def relu2(m, ps, mm):
                        ACE.after(mm)
                        e = ACE.did(ACE.e.activation(kT[:, m, :], ps, ACT.Relu))
                        POOL.after(e)
                        POOL.did(POOL.e.tensor_tensor(kT[:, m, :], kT[:, m, :], kT[:, m, :], ALU.mult))
                        return e
                    gemm_T(W[:, W_FK, :, :], xf[0], CT, relu2)
                    kk_done = POOL.last()

                    def sigmoid(m, ps, mm):
                        ACE.after(mm)
                        return ACE.did(ACE.e.activation(wT[:, m, :], ps, ACT.Sigmoid))
                    gemm_rows(W[:, W_FR, :, :], xf[1], CT, sigmoid)
                    PE.after(kk_done)

                    def add_ffn(m, ps, mm):
                        DVE.after(mm)
                        e = DVE.did(DVE.e.tensor_tensor(wT[:, m, :], ps, wT[:, m, :], ALU.mult))
                        POOL.after(e)
                        POOL.did(POOL.e.tensor_tensor(xw[:, m, :], xw[:, m, :], wT[:, m, :], ALU.add))
                        return e
                    DVE.after(ACE.last())
                    gemm_rows(W[:, W_FV, :, :], kT, CT, add_ffn)
                    SP.after(POOL.last())
                    SP.after(load(xs[b], xw[:, :, :]))
                    end_of_step()

        with ExitStack() as ctx:
            wq = sb("l3_wq", [P, CT, C], ctx)
            wk = sb("l3_wk", [P, CT, C], ctx)
            wv = sb("l3_wv", [P, CT, C], ctx)
            wo = sb("l3_wo", [P, CT, C], ctx)
            m1 = sb("l3_m1", [P, CT, MLP], ctx)
            vec = sb("l3_vec", [P, 3 * CT + MT], ctx)
            bv = sb("l3_bv", [P, C], ctx)
            bo = sb("l3_bo", [P, C], ctx)
            b2 = sb("l3_b2", [P, C], ctx)
            hT = sb("l3_hT", [P, CT, NK], ctx)
            vt = sb("l3_v", [P, NK // P, C], ctx)
            qf = sb("l3_qf", [P, 2, L], ctx)
            rest = sb("l3_rest", [P, 2, L], ctx)
            parts = sb("l3_parts", [P, 2, 3, L], ctx, BF16)
            mi = sb("l3_mi", [P, L], ctx, I32)
            mb = sb("l3_mb", [P, NK], ctx)
            SR = 3
            stack = sb("l3_stack", [P, SR, 2, L + NK], ctx, BF16)
            nz = sb("l3_nz", [P, 2, NK], ctx)
            pr = sb("l3_p", [P, 2 * LT, NK], ctx)
            pT = sb("l3_pT", [P, 3, L], ctx)
            nmax = sb("l3_nmax", [P, LT * PH], ctx)
            den = sb("l3_den", [P, LT * PH], ctx)
            rden = sb("l3_rden", [P, LT * PH], ctx)
            rdx = sb("l3_rdx", [P, LT, P], ctx)
            rdT = sb("l3_rdT", [P, L], ctx)
            oT = sb("l3_oT", [P, CT, L], ctx)
            att = sb("l3_att", [P, LT, C], ctx)
            nT = oT
            st_flat = stack[:, :, :, :].rearrange("p a b c -> p (a b c)").bitcast(F32)
            m2s = [st_flat[:, a * 2 * C:(a + 1) * 2 * C].rearrange("p (k c) -> p k c", k=2) for a in range(2)]
            ss = sb("l3_ss", [P, LT], ctx)
            scr = sb("l3_scr", [P, 3, LT], ctx)
            h1 = [pr[:, m // 2, (m % 2) * L:(m % 2 + 1) * L] for m in range(MT)]

            SP.after(load(wq[:, :, :], t["l3_wq"]), load(wk[:, :, :], t["l3_wk"], ACE), load(wv[:, :, :], t["l3_wv"]),
                     load(wo[:, :, :], t["l3_wo"], ACE), load(m1[:, :, :], t["l3_m1"]), load(vec[:, :], t["l3_vec"], ACE),
                     load(bv[:, :], t["l3_bv"].partition_broadcast(P)), load(bo[:, :], t["l3_bo"].partition_broadcast(P)),
                     load(b2[:, :], t["l3_b2"].partition_broadcast(P)))
            DVE.did(DVE.e.memset(mb[:, L:NK], 0.0))
            end_of_step()

            with nc.Fori(0, B) as b:
                got_c = load(hT[:, :, 0:L], t["cT"][b])
                got_m = load(mi[:, :], t["keymask"][b].partition_broadcast(P), ACE)
                got_x = load(att[:, :, :], xs[b])
                ring = Ring(bank)
                PE.after(got_x)
                for c in range(CT):
                    i, ps, free = ring.take()
                    PE.after(free)
                    for m in range(LT):
                        mm = transpose(ps[:, m * P:(m + 1) * P], att[:, m, c * P:(c + 1) * P])
                    ACE.after(PE.did(mm))
                    ring.free[i] = l_done = ACE.did(ACE.e.activation(hT[:, c, L:NK], ps, ACT.Copy))
                DVE.after(got_m)
                e = DVE.did(DVE.e.tensor_single_scalar(mb[:, 0:L], mi[:, :], 0.0, ALU.is_equal))
                DVE.after(e)
                mb_done = DVE.did(DVE.e.tensor_scalar_mul(mb[:, 0:L], mb[:, 0:L], MASKED))
                qf_ring, part_ring = Ring(range(2)), Ring(range(2))
                PE.after(l_done, got_c)
                stored_parts = []
                for m in range(CT):
                    for half in (0, 1, None):
                        i, ps, free = ring.take()
                        PE.after(free)
                        w, o = (wq, L) if half is None else (wk, half * L)
                        for k in range(CT):
                            mm = PE.e.matmul(ps, w[:, k, m * P:(m + 1) * P], hT[:, k, o:o + L], start=k == 0, stop=k == CT - 1)
                        a, _, free = qf_ring.take()
                        DVE.after(PE.did(mm), free)
                        if half is None:
                            e = DVE.did(DVE.e.tensor_scalar(qf[:, a, :], ps, vec[:, m:m + 1], 1.0 / PD, ALU.add, ALU.mult))
                            dst = q_parts[:, m * P:(m + 1) * P, :]
                        else:
                            e = DVE.did(DVE.e.tensor_scalar_add(qf[:, a, :], ps, vec[:, CT + m:CT + m + 1]))
                            dst = k3_parts[:, m * P:(m + 1) * P, half * L:(half + 1) * L]
                        ring.free[i] = e
                        p, _, free = part_ring.take()
                        e = qf_ring.free[a] = split3(qf[:, a, :], e, rest[:, a, :], [parts[:, p, n, :] for n in range(3)], free)
                        SP.after(e)
                        part_ring.free[p] = load(dst.rearrange("n p l -> p n l"), parts[:, p, :, :])
                        stored_parts.append(part_ring.free[p])
                st_ring = Ring(range(SR))
                st_last = [None] * SR

                def fetch(h):
                    i, _, free = st_ring.take()
                    m = h // 4
                    SP.after(free, *stored_parts[3 * m:3 * m + 3])
                    d = slice(h * PD, (h + 1) * PD)
                    pairs = []
                    for st, (qn, kn) in enumerate((((0, 0, 0), (0, 1, 2)), ((1, 1, 2), (0, 1, 0)))):
                        for slot in range(3):
                            rows = slice(slot * PD, (slot + 1) * PD)
                            pairs.append((stack[rows, i, st, 0:L], q_parts[qn[slot], d, :]))
                            pairs.append((stack[rows, i, st, L:], k3_parts[kn[slot], d, :]))
                    st_last[i] = load_all(pairs, again=st_last[i])
                    item[("st", h)] = (i, st_last[i])
                item = {}
                for s in range(NK // P):
                    i, ps, free = ring.take()
                    PE.after(free)
                    for k in range(CT):
                        mm = PE.e.matmul(ps, hT[:, k, s * P:(s + 1) * P], wv[:, k, :], start=k == 0, stop=k == CT - 1)
                    DVE.after(PE.did(mm))
                    ring.free[i] = v_done = DVE.did(DVE.e.tensor_tensor(vt[:, s, :], ps, bv[:, :], ALU.add))
                for m in range(LT):
                    DVE.after(l_done)
                    at_done = DVE.did(DVE.e.tensor_tensor(att[:, m, :], att[:, m, :], bo[:, :], ALU.add))
                PE.after(v_done)
                DVE.after(mb_done)

                s_ring = Ring([psum[:, 0:2 * BANK], psum[:, 2 * BANK:4 * BANK]])
                t_ring, o_ring = Ring(bank[4:7]), Ring(bank[7:8])
                for r in (s_ring, t_ring, o_ring):
                    r.free = [v_done] * len(r.bufs)
                nz_ring, pr_ring, pT_ring = Ring(range(2)), Ring(range(2 * LT)), Ring(range(3))
                oT_done = []
                rd_free = [None]
                KT = NK // P

                def scores(h, lt):
                    n = h * LT + lt
                    si, got = item[("st", h)]
                    i, ps, free = s_ring.take()
                    PE.after(free, got)
                    for half in range(2):
                        for st in range(2):
                            mm = PE.e.matmul(ps[:, half * L:(half + 1) * L], stack[0:3 * PD, si, st, lt * P:(lt + 1) * P],
                                             stack[0:3 * PD, si, st, L + half * L:L + (half + 1) * L],
                                             start=st == 0, stop=st == 1)
                    mm = PE.did(mm)
                    if lt == LT - 1:
                        st_ring.free[si] = mm
                    a, _, freed = nz_ring.take()
                    DVE.after(mm, freed)
                    z = s_ring.free[i] = DVE.did(DVE.e.tensor_tensor_reduce(
                        out=nz[:, a, :], in0=ps, in1=mb[:, :], scale=-1.0, scalar=3.0e38,
                        op0=ALU.add, op1=ALU.min, accum_out=nmax[:, n:n + 1]))
                    i, _, freed = pr_ring.take()
                    ACE.after(z, freed)
                    e = nz_ring.free[a] = ACE.did(ACE.e.activation(pr[:, i, :], nz[:, a, :], ACT.Exp, scale=-1.0,
                                                                   bias=nmax[:, n:n + 1], accum_out=den[:, n:n + 1]))
                    item[(h, lt)] = (i, e)

                def turn(h, s):
                    j, ps, free = t_ring.take()
                    PE.after(free)
                    for lt in range(LT):
                        i, e = item[(h, lt)]
                        PE.after(e)
                        mm = transpose(ps[:, lt * P:(lt + 1) * P], pr[:, i, s * P:(s + 1) * P])
                    mm = PE.did(mm)
                    if s == KT - 1:
                        for lt in range(LT):
                            pr_ring.free[item.pop((h, lt))[0]] = mm
                    k, _, freed = pT_ring.take()
                    if s % 2:
                        DVE.after(mm, freed)
                        e = DVE.did(DVE.e.tensor_copy(pT[:, k, :], ps))
                    else:
                        ACE.after(mm, freed)
                        e = ACE.did(ACE.e.activation(pT[:, k, :], ps, ACT.Copy))
                    t_ring.free[j] = e
                    item[("pT", h, s)] = (k, e)

                def mix(h, s):
                    k, e = item.pop(("pT", h, s))
                    c, r = divmod(h, 4)
                    if r == 0 and s == 0:
                        item["o"] = o_ring.take()
                        PE.after(item["o"][2])
                    oi, ops, _ = item["o"]
                    PE.after(e)
                    mm = PE.e.matmul(ops[PD * r:PD * (r + 1), :], vt[:, s, h * PD:(h + 1) * PD], pT[:, k, :],
                                     start=s == 0, stop=s == KT - 1)
                    pT_ring.free[k] = mm = PE.did(mm)
                    if r == 3 and s == KT - 1:
                        normalise(c, oi, ops, mm)

                def normalise(c, oi, ops, mm):
                    sl = slice(c * 4 * LT, (c + 1) * 4 * LT)
                    DVE.after(ACE.last(), rd_free[0])
                    e = DVE.did(DVE.e.reciprocal(rden[:, sl], den[:, sl]))
                    DVE.after(e)
                    e = DVE.did(DVE.e.tensor_copy(
                        rdx[:, :, :].rearrange("p l (h d) -> p l h d", h=4),
                        rden[:, sl].rearrange("p (h l) -> p l h", l=LT).unsqueeze(3).broadcast_to([P, LT, 4, PD])))
                    i, ps, free = t_ring.take()
                    PE.after(e, free)
                    for lt in range(LT):
                        m2_ = PE.e.matmul(ps[:, lt * P:(lt + 1) * P], rdx[:, lt, :], ident[:, :], start=True, stop=True)
                    rd_free[0] = PE.did(m2_)
                    ACE.after(rd_free[0], oT_done[-1] if oT_done else None)
                    e = t_ring.free[i] = ACE.did(ACE.e.activation(rdT[:, :], ps, ACT.Copy))
                    DVE.after(e, mm)
                    e = o_ring.free[oi] = DVE.did(DVE.e.tensor_tensor(oT[:, c, :], ops, rdT[:, :], ALU.mult))
                    oT_done.append(e)

                fetch(0)
                fetch(1)
                for h in range(PH + 1):
                    if h + 2 < PH:
                        fetch(h + 2)
                    for s in range(KT):
                        if h < PH and s % 2 == 0:
                            scores(h, s // 2)
                        if h >= 1:
                            turn(h - 1, s)
                            if s:
                                mix(h - 1, s - 1)
                    if h >= 1:
                        mix(h - 1, KT - 1)

                PE.after(*oT_done)
                for lt in range(LT):
                    i, ps, free = t_ring.take()
                    PE.after(free)
                    for c in range(CT):
                        mm = PE.e.matmul(ps, oT[:, c, lt * P:(lt + 1) * P], wo[:, c, :], start=c == 0, stop=c == CT - 1)
                    DVE.after(PE.did(mm), at_done)
                    e = t_ring.free[i] = DVE.did(DVE.e.tensor_tensor(att[:, lt, :], ps, att[:, lt, :], ALU.add))
                    ACE.after(e)
                    ACE.after(ACE.did(ACE.e.activation(qf[:, 0, :], att[:, lt, :], ACT.Square, accum_out=ss[:, lt:lt + 1])))

                DVE.after(ACE.last())
                e = rsqrt(ss[:, :], [scr[:, i, :] for i in range(3)], 1e-6, 1.0 / C)
                DVE.after(e)
                ring = Ring(bank)
                PE.after(DVE.last(), ACE.last())
                for m in range(LT):
                    an_done = DVE.did(DVE.e.tensor_scalar_mul(att[:, m, :], att[:, m, :], ss[:, m:m + 1]))
                PE.after(an_done)
                for c in range(CT):
                    i, ps, free = ring.take()
                    PE.after(free)
                    for m in range(LT):
                        mm = transpose(ps[:, m * P:(m + 1) * P], att[:, m, c * P:(c + 1) * P])
                    DVE.after(PE.did(mm))
                    ring.free[i] = n_done = DVE.did(DVE.e.tensor_scalar_mul(nT[:, c, :], ps, vec[:, 2 * CT + c:2 * CT + c + 1]))
                SP.after(PE.last())
                got_x = load(att[:, :, :], xs[b])
                DVE.after(got_x)
                for m in range(LT):
                    r_done = DVE.did(DVE.e.tensor_tensor(att[:, m, :], att[:, m, :], b2[:, :], ALU.add))
                PE.after(n_done)
                h_done = []
                for m in range(MT):
                    i, ps, free = ring.take()
                    PE.after(free)
                    for k in range(CT):
                        mm = PE.e.matmul(ps, m1[:, k, m * P:(m + 1) * P], nT[:, k, :], start=k == 0, stop=k == CT - 1)
                    ACE.after(PE.did(mm))
                    ring.free[i] = e = ACE.did(ACE.e.activation(h1[m], ps, ACT.Gelu_apprx_tanh,
                                                                bias=vec[:, 3 * CT + m:3 * CT + m + 1]))
                    h_done.append(e)
                m2_free, m2_last = [None, None], [None, None]
                SP.after(*oT_done)
                for q in range(MT // 2):
                    a = q % 2
                    SP.after(m2_free[a])
                    m2_last[a] = load_all([(m2s[a], t["l3_m2"][q])], again=m2_last[a])
                    PE.after(m2_last[a], h_done[2 * q + 1])
                    if q == 0:
                        PE.after(*h_done[-8:])
                    for m in range(LT):
                        for k in range(2):
                            mm = PE.e.matmul(bank[m], h1[2 * q + k][:, m * P:(m + 1) * P], m2s[a][:, k, :],
                                             start=q == 0 and k == 0, stop=q == MT // 2 - 1 and k == 1)
                    m2_free[a] = PE.did(mm)
                DVE.after(PE.last(), r_done)
                for m in range(LT):
                    e = DVE.did(DVE.e.tensor_tensor(att[:, m, :], bank[m], att[:, m, :], ALU.add))
                SP.after(e)
                SP.e.dma_start(t["out"][b], att[:, :, :]).then_inc(store_sem, 16)
                end_of_step(stored=16)


def lay_out(inputs):
    import numpy as np
    a = {k: np.asarray(v) for k, v in inputs.items()}

    def w_tiles(w):
        return w.reshape(-1, P, w.shape[1]).transpose(1, 0, 2)

    def cols(v):
        return v.reshape(-1, P).T

    def tokens(x):
        return x.reshape(B, LT, P, -1).transpose(0, 2, 1, 3)

    def chans(x):
        return x.transpose(0, 2, 1).reshape(B, CT, P, L).transpose(0, 2, 1, 3)

    x, ctx = a["x"], a["ctx_2048"]
    o = {"x": tokens(x), "xT": chans(x), "cT": chans(ctx), "mask": tokens(a["mask_Bx1xSxS2_ff0"][:, 0]),
         "keymask": a["mask_BxS2_ik0"]}
    p = "L0_xattn_"
    o["l0_wq"], o["l0_wv"], o["l0_wo"] = (w_tiles(a[p + n]) for n in ("Wq", "Wv", "Wo"))
    o["l0_wk"], o["l0_bk"], o["l0_bq"] = w_tiles(a[p + "Wk"]), cols(a[p + "bk"]), cols(a[p + "bq"])
    for n in ("bv", "bo", "gamma", "beta"):
        o["l0_" + n] = a[p + n]

    both = {"w1": [], "w2": [], "dw1": [], "dw2": [], "w": [], "vec": []}
    for layer, order in ((1, (0, 1, 2, 3, 4)), (2, (1, 0, 2, 3, 4))):
        p = f"L{layer}_xattn_"
        ffn = p + ("f" if layer == 1 else "ffn_")
        if layer == 1:
            maa = [a[p + "maa_" + n] for n in "wkvrg"]
        else:
            maa = [a[p + "maa_stack"][f] for f in order]
        order = list(order)
        both["w1"].append(w_tiles(a[p + "maa_w1"].reshape(C, NF, DM)[:, order].reshape(C, NF * DM)))
        w2 = np.zeros((P, NF, C), np.float32)
        for f in range(NF):
            w2[DM * f % P:DM * f % P + DM, f] = a[p + "maa_w2"][order[f]]
        both["w2"].append(w2)
        both["dw1"].append(w_tiles(a[p + "decay_w1"]))
        both["dw2"].append(np.concatenate([a[p + "decay_w2"], np.zeros((P - DD, C), np.float32)]))
        both["w"].append(np.stack([w_tiles(a[n].T) for n in (p + "Wr", p + "Wk", p + "Wv", p + "Wg", p + "Wo",
                                                            ffn + "Wk", ffn + "Wr", ffn + "Wv")]))
        v = [a[p + "ln1_w"], a[p + "ln1_b"], a[p + "maa_x"], *maa, a[p + "time_decay"], a[p + "faaaa"].reshape(C),
             a[p + "gn_w"], a[p + "gn_b"], a[p + "ln2_w"], a[p + "ln2_b"], a[ffn + "maa_k"], a[ffn + "maa_r"]]
        both["vec"].append(np.stack([cols(u) for u in v], axis=1))
    for n, v in both.items():
        o["rw_" + n] = np.stack(v)
    o["prev"] = ctx[:, 0:2].reshape(B, 2, CT, P).transpose(0, 3, 1, 2)
    o["s0"] = ctx[:, 2:2 + RS].reshape(B, CT, P, RS).transpose(0, 2, 1, 3)

    p = "L3_xattn_"
    kv = a[p + "kv_w"].reshape(C, C, 2)
    kvb = a[p + "kv_b"].reshape(C, 2)
    o["l3_wq"], o["l3_wo"], o["l3_m1"] = (w_tiles(a[p + n]) for n in ("q_w", "out_w", "mlp_w1"))
    o["l3_wk"], o["l3_wv"] = w_tiles(kv[:, :, 0]), w_tiles(kv[:, :, 1])
    o["l3_m2"] = a[p + "mlp_w2"].reshape(MT // 2, 2, P, C).transpose(0, 2, 1, 3)
    o["l3_vec"] = np.concatenate([cols(a[p + "q_b"]), cols(kvb[:, 0]), cols(a[p + "postnorm_w"]), cols(a[p + "mlp_b1"])], axis=1)
    o["l3_bv"], o["l3_bo"], o["l3_b2"] = kvb[:, 1], a[p + "out_b"], a[p + "mlp_b2"]
    return {k: np.ascontiguousarray(v) for k, v in o.items()}


def kernel(**inputs):
    import concourse.bacc as bacc
    from concourse.bass_utils import run_bass_kernel_spmd

    nc = bacc.Bacc("TRN2", target_bir_lowering=False, num_devices=1)
    arrays = lay_out(inputs)
    t = {n: nc.dram_tensor("in_" + n, v.shape, mybir.dt.from_np(v.dtype), kind="ExternalInput").ap()
         for n, v in arrays.items()}
    t["out"] = nc.dram_tensor("out", (B, P, LT, C), F32, kind="ExternalOutput").ap()
    program(nc, t)
    r = run_bass_kernel_spmd(nc, [{"in_" + n: v for n, v in arrays.items()}], core_ids=[0])
    return r.results[0]["out"].transpose(0, 2, 1, 3).reshape(B, L, C)
```

```python
import concourse.bass as bass
from concourse import mybir
from contextlib import ExitStack

F32 = mybir.dt.float32
I32 = mybir.dt.int32
F32R = mybir.dt.float32r
BF16 = mybir.dt.bfloat16
ALU = mybir.AluOpType
ACT = mybir.ActivationFunctionType
AX = mybir.AxisListType

P = 128
B, L, C = 4, 512, 512
CT, LT = C // P, L // P
BANK = 512
NBANK = 8
LAG0, LAG3 = 3, 2

QH, KVH = 32, 8
HD = C // QH
NL = 2
RH, RS = 32, 16
HPT = P // RS
NF, DM, DD = 5, 32, 64
DECAY, KEY, VALUE, RECEPT, GATE = range(NF)
PH = 16
PD = C // PH
NK = 2 * L
MLP = 4 * C
MT = MLP // P

Q_SLOTS, K_SLOTS = (0, 0, 0, 1, 1, 2), (0, 1, 2, 0, 1, 0)

MASKED = -1.0e30

(V_LN1W, V_LN1B, V_MAAX, V_MAA, V_TD, V_U, V_GNW, V_GNB, V_LN2W, V_LN2B, V_FK, V_FR, V_N) = \
    (0, 1, 2, 3, 8, 9, 10, 11, 12, 13, 14, 15, 16)
W_R, W_K, W_V, W_G, W_O, W_FK, W_FR, W_FV = range(8)


class Queue:

    def __init__(self, engine, sem):
        self.e, self.sem, self.count, self.seen = engine, sem, 0, {}

    def after(self, *events):
        for ev in events:
            if ev is None:
                continue
            sem, value = ev
            if self.seen.get(id(sem), 0) < value:
                self.e.wait_ge(sem, value)
                self.seen[id(sem)] = value
        return self.e

    def did(self, instruction):
        instruction.then_inc(self.sem, 1)
        self.count += 1
        return (self.sem, self.count)

    def last(self):
        return (self.sem, self.count) if self.count else None

    def reset(self):
        self.count, self.seen = 0, {}


class Ring:

    def __init__(self, bufs):
        self.bufs, self.free, self.at = list(bufs), [None] * len(bufs), -1

    def take(self):
        self.at = (self.at + 1) % len(self.bufs)
        return self.at, self.bufs[self.at], self.free[self.at]


def program(nc, t):
    top = ExitStack()
    with top:
        def sem(name):
            return top.enter_context(nc.semaphore(name))

        PE = Queue(nc.tensor, sem("pe_done"))
        DVE = Queue(nc.vector, sem("dve_done"))
        ACE = Queue(nc.scalar, sem("act_done"))
        POOL = Queue(nc.gpsimd, sem("pool_done"))
        SP = Queue(nc.sync, None)
        queues = (PE, DVE, ACE, POOL, SP)
        load_sems = [sem(f"dma{i}") for i in range(48)]
        store_sem = sem("store")
        loads = [0]

        def load(dst, src, q=None):
            q = q or SP
            s = load_sems[loads[0]]
            loads[0] += 1
            q.e.dma_start(dst, src).then_inc(s, 16)
            return (s, 16)

        def load_all(pairs, q=None, again=None):
            q = q or SP
            if again is None:
                s, n = load_sems[loads[0]], 0
                loads[0] += 1
            else:
                s, n = again
            for dst, src in pairs:
                q.e.dma_start(dst, src).then_inc(s, 16)
            return (s, n + 16 * len(pairs))

        def end_of_step(stored=0):
            if stored:
                SP.e.wait_ge(store_sem, stored)
            nc.all_engine_barrier()
            for s in [q.sem for q in queues if q.sem is not None] + load_sems[:loads[0]] + ([store_sem] if stored else []):
                nc.gpsimd.sem_clear(s)
            nc.all_engine_barrier()
            loads[0] = 0
            for q in queues:
                q.reset()

        def sb(name, shape, ctx=top, dt=F32):
            return ctx.enter_context(nc.sbuf_tensor(name, shape, dt))

        psum = top.enter_context(nc.psum_tensor("psum", [P, NBANK * BANK], F32))
        bank = [psum[:, i * BANK:(i + 1) * BANK] for i in range(NBANK)]

        xs = nc.dram_tensor("x_scratch", (B, P, LT, C), F32, kind="Internal").ap()
        q_parts = nc.dram_tensor("q_parts", (3, C, L), BF16, kind="Internal").ap()
        k0_parts = nc.dram_tensor("k0_parts", (3, KVH * HD, L), BF16, kind="Internal").ap()
        k3_parts = nc.dram_tensor("k3_parts", (3, C, NK), BF16, kind="Internal").ap()
        ident = sb("ident", [P, P])
        headsum = sb("headsum", [P, HPT])

        ev = POOL.did(POOL.e.memset(ident[:, :], 0.0))
        POOL.after(ev)
        ev_ident = POOL.did(POOL.e.affine_select(out=ident[:, :], in_=ident[:, :], compare_op=ALU.not_equal,
                                                 fill=1.0, base=0, pattern=[[-1, P]], channel_multiplier=1))
        DVE.after(ev_ident)
        DVE.did(DVE.e.tensor_reduce(headsum[:, :], ident[:, :].rearrange("p (h i) -> p h i", i=RS),
                                    axis=AX.X, op=ALU.add))
        end_of_step()

        def split3(v, v_ready, rest, parts, parts_free):
            ACE.after(v_ready, parts_free)
            e = ACE.did(ACE.e.activation(parts[0], v, ACT.Copy))
            for n in (1, 2):
                POOL.after(e, v_ready, parts_free)
                e = POOL.did(POOL.e.tensor_tensor(rest, v if n == 1 else rest, parts[n - 1], ALU.subtract))
                ACE.after(e)
                e = ACE.did(ACE.e.activation(parts[n], rest, ACT.Copy))
            return e

        def transpose(out, in_):
            return PE.e.transpose(out, in_, ident[:, :])

        def rsqrt(a, scratch, add, mul=1.0):
            v, y, u = scratch
            e = DVE.did(DVE.e.tensor_scalar(v, a, mul, add, ALU.mult, ALU.add))
            DVE.after(e)
            e = DVE.did(DVE.e.tensor_single_scalar(u.bitcast(I32), v.bitcast(I32), 1, ALU.arith_shift_right))
            DVE.after(e)
            e = DVE.did(DVE.e.tensor_scalar(y.bitcast(I32), u.bitcast(I32), -1.0, float(0x5F3759DF), ALU.mult, ALU.add))
            for n in range(3):
                yield "step"
                DVE.after(e)
                e = DVE.did(DVE.e.scalar_tensor_tensor(u, y, -0.5, y, ALU.mult, ALU.mult))
                DVE.after(e)
                e = DVE.did(DVE.e.tensor_tensor(u, u, v, ALU.mult))
                DVE.after(e)
                e = DVE.did(DVE.e.scalar_tensor_tensor(a if n == 2 else y, u, 1.5, y, ALU.add, ALU.mult))
            return e

        def norm_stats(tiles, ready, stats, mv, rstd, scratch, eps):
            es = []
            for i, x in enumerate(tiles):
                DVE.after(ready[i])
                es.append(DVE.did(DVE.e.bn_stats(stats[:, i, :], x)))
                if i % 2:
                    yield "step"
            for i, e in enumerate(es):
                DVE.after(e)
                e2 = DVE.did(DVE.e.bn_aggr(mv[:, i, :], stats[:, i, :]))
            DVE.after(e2)
            e = DVE.did(DVE.e.tensor_copy(rstd, mv[:, :, 1]))
            DVE.after(e)
            return (yield from rsqrt(rstd, scratch, eps))

        def at_once(steps):
            while True:
                try:
                    next(steps)
                except StopIteration as end:
                    return end.value

        def together(*generators):
            results, going = [None] * len(generators), set(range(len(generators)))
            while going:
                for g in sorted(going):
                    try:
                        next(generators[g])
                    except StopIteration as end:
                        results[g] = end.value
                        going.discard(g)
                if going:
                    yield
            return results

        with ExitStack() as ctx:
            wq = sb("l0_wq", [P, CT, C], ctx)
            wk = sb("l0_wk", [P, CT, P], ctx)
            wv = sb("l0_wv", [P, CT, P], ctx)
            wo = sb("l0_wo", [P, CT, C], ctx)
            bq = sb("l0_bq", [P, CT], ctx)
            bk = sb("l0_bk", [P, 1], ctx)
            bv = sb("l0_bv", [P, KVH * HD], ctx)
            bo = sb("l0_bo", [P, C], ctx)
            gamma = sb("l0_gamma", [P, C], ctx)
            beta = sb("l0_beta", [P, C], ctx)
            xT = sb("l0_xT", [P, CT, L], ctx)
            cT = sb("l0_cT", [P, CT, L], ctx)
            xin = sb("l0_x", [P, LT, C], ctx)
            mask = sb("l0_mask", [P, LT, L], ctx)
            qf = sb("l0_qf", [P, 2, L], ctx)
            rest = sb("l0_rest", [P, 2, L], ctx)
            parts = sb("l0_parts", [P, 2, 3, L], ctx, BF16)
            qs = sb("l0_qs", [6 * HD, QH, L], ctx, BF16)
            ks = sb("l0_ks", [6 * HD, KVH, L], ctx, BF16)
            vp = sb("l0_vp", [P, LT, KVH, 3 * HD], ctx)
            nz = sb("l0_nz", [P, 3, L], ctx)
            pr = sb("l0_p", [P, 2 * LT, L], ctx)
            pT = sb("l0_pT", [P, LAG0 + 2, L], ctx)
            nmax = sb("l0_nmax", [P, QH * LT], ctx)
            den = sb("l0_den", [P, QH * LT], ctx)
            rden = sb("l0_rden", [P, QH * LT], ctx)
            rdx = sb("l0_rdx", [P, LT, P], ctx)
            rdT = sb("l0_rdT", [P, L], ctx)
            oT = sb("l0_oT", [P, CT, L], ctx)
            stats = sb("l0_stats", [P, LT, 6], ctx)
            mv = sb("l0_mv", [P, LT, 2], ctx)
            rstd = sb("l0_rstd", [P, LT], ctx)
            scr = sb("l0_scr", [P, 3, LT], ctx)

            SP.after(load(wq[:, :, :], t["l0_wq"]), load(wk[:, :, :], t["l0_wk"], ACE), load(wv[:, :, :], t["l0_wv"]),
                     load(wo[:, :, :], t["l0_wo"]), load(bq[:, :], t["l0_bq"], ACE), load(bk[:, :], t["l0_bk"], ACE),
                     load(bv[:, :], t["l0_bv"].partition_broadcast(P)), load(bo[:, :], t["l0_bo"].partition_broadcast(P)),
                     load(gamma[:, :], t["l0_gamma"].partition_broadcast(P)),
                     load(beta[:, :], t["l0_beta"].partition_broadcast(P)),
                     load(xT[:, :, :], t["xT"][0]), load(cT[:, :, :], t["cT"][0], ACE), load(mask[:, :, :], t["mask"][0]))
            DVE.did(DVE.e.memset(vp[:, :, :, HD:2 * HD], 0.0))
            end_of_step()

            with nc.Fori(0, B) as b:
                following = (b + 1) % B
                got_xin = load(xin[:, :, :], t["x"][b])

                ring = Ring(bank)
                qf_ring, part_ring = Ring(range(2)), Ring(range(2))
                got_q, got_k = [], None
                for m in (CT, *range(CT)):
                    i, ps, free = ring.take()
                    PE.after(free)
                    w, x, bias, scale = (wk, cT, bk, 1.0) if m == CT else (wq, xT, bq, HD ** -0.5)
                    o = 0 if m == CT else m
                    for k in range(CT):
                        mm = PE.e.matmul(ps, w[:, k, o * P:(o + 1) * P], x[:, k, :], start=k == 0, stop=k == CT - 1)
                    a, _, free = qf_ring.take()
                    DVE.after(PE.did(mm), free)
                    e = ring.free[i] = DVE.did(DVE.e.tensor_scalar(qf[:, a, :], ps, bias[:, o:o + 1], scale, ALU.add, ALU.mult))
                    p, _, free = part_ring.take()
                    e = qf_ring.free[a] = split3(qf[:, a, :], e, rest[:, a, :], [parts[:, p, n, :] for n in range(3)], free)
                    SP.after(e)
                    dst = k0_parts if m == CT else q_parts[:, m * P:(m + 1) * P, :]
                    e = part_ring.free[p] = load(dst.rearrange("n p l -> p n l"), parts[:, p, :, :])
                    SP.after(e)
                    stack, heads = (ks, slice(0, KVH)) if m == CT else (qs, slice(m * HPT, (m + 1) * HPT))
                    got = load_all([(stack[slot * HD:(slot + 1) * HD, heads, :],
                                     dst[n].rearrange("(h i) l -> i h l", i=HD))
                                    for slot, n in enumerate(K_SLOTS if m == CT else Q_SLOTS)])
                    if m == CT:
                        got_k = got
                    else:
                        got_q.append(got)
                SP.after(PE.last())
                got_next = [load(xT[:, :, :], t["xT"][following])]
                i, ps, free = ring.take()
                PE.after(free)
                for s in range(LT):
                    for k in range(CT):
                        mm = PE.e.matmul(ps[:, s * P:(s + 1) * P], cT[:, k, s * P:(s + 1) * P], wv[:, k, :],
                                         start=k == 0, stop=k == CT - 1)
                DVE.after(PE.did(mm))
                for half in (0, 2):
                    v_done = DVE.did(DVE.e.tensor_tensor(
                        vp[:, :, :, half * HD:(half + 1) * HD], ps.rearrange("p (s h d) -> p s h d", s=LT, h=KVH),
                        bv[:, :].rearrange("p (h d) -> p h d", h=KVH).unsqueeze(1).broadcast_to([P, LT, KVH, HD]), ALU.add))
                POOL.after(got_xin)
                for m in range(LT):
                    xb_done = POOL.did(POOL.e.tensor_tensor(xin[:, m, :], xin[:, m, :], bo[:, :], ALU.add))
                SP.after(PE.last())
                got_next.append(load(cT[:, :, :], t["cT"][following]))
                PE.after(v_done, got_k)

                s_ring, t_ring, o_ring = Ring(bank[0:3]), Ring(bank[3:6]), Ring(bank[6:8])
                for r in (s_ring, t_ring, o_ring):
                    r.free = [v_done] * len(r.bufs)
                nz_ring, pr_ring, pT_ring = Ring(range(3)), Ring(range(2 * LT)), Ring(range(LAG0 + 2))
                item = {}
                oT_done = []
                rd_free = [None]

                def scores(h, lt):
                    n = h * LT + lt
                    i, ps, free = s_ring.take()
                    PE.after(free, got_q[h // HPT])
                    mm = PE.did(PE.e.matmul(ps, qs[:, h, lt * P:(lt + 1) * P], ks[:, h // (QH // KVH), :], start=True, stop=True))
                    a, _, freed = nz_ring.take()
                    DVE.after(mm, freed)
                    z = s_ring.free[i] = DVE.did(DVE.e.tensor_tensor_reduce(
                        out=nz[:, a, :], in0=ps, in1=mask[:, lt, :], scale=-1.0, scalar=3.0e38,
                        op0=ALU.add, op1=ALU.min, accum_out=nmax[:, n:n + 1]))
                    i, _, freed = pr_ring.take()
                    ACE.after(z, freed)
                    e = nz_ring.free[a] = ACE.did(ACE.e.activation(pr[:, i, :], nz[:, a, :], ACT.Exp, scale=-1.0,
                                                                   bias=nmax[:, n:n + 1], accum_out=den[:, n:n + 1]))
                    item[(h, lt)] = (i, e)

                def turn(h, s):
                    j, ps, free = t_ring.take()
                    PE.after(free)
                    for lt in range(LT):
                        i, e = item[(h, lt)]
                        PE.after(e)
                        mm = transpose(ps[:, lt * P:(lt + 1) * P], pr[:, i, s * P:(s + 1) * P])
                    mm = PE.did(mm)
                    if s == LT - 1:
                        for lt in range(LT):
                            i, e = item.pop((h, lt))
                            pr_ring.free[i] = mm
                        if h % HPT == HPT - 1:
                            spread_sums(h // HPT, e)
                    k, _, freed = pT_ring.take()
                    if s % 2:
                        DVE.after(mm, freed)
                        e = DVE.did(DVE.e.tensor_copy(pT[:, k, :], ps))
                    else:
                        ACE.after(mm, freed)
                        e = ACE.did(ACE.e.activation(pT[:, k, :], ps, ACT.Copy))
                    t_ring.free[j] = e
                    item[("pT", h, s)] = (k, e)

                def mix(h, s):
                    k, e = item.pop(("pT", h, s))
                    c, r = divmod(h, HPT)
                    if r == 0 and s == 0:
                        item["o"] = o_ring.take()
                        PE.after(item["o"][2])
                    oi, ops, _ = item["o"]
                    PE.after(e)
                    quad, odd = 32 * (r // 2), r % 2
                    mm = PE.e.matmul(ops[quad:quad + 32, :], vp[:, s, h // (QH // KVH), odd * HD:(odd + 2) * HD], pT[:, k, :],
                                     start=odd == 0 and s == 0, stop=odd == 1 and s == LT - 1)
                    pT_ring.free[k] = mm = PE.did(mm)
                    if r == HPT - 1 and s == LT - 1:
                        normalise(c, oi, ops, mm)

                def spread_sums(c, summed):
                    sl = slice(c * HPT * LT, (c + 1) * HPT * LT)
                    DVE.after(summed, rd_free[0])
                    e = DVE.did(DVE.e.reciprocal(rden[:, sl], den[:, sl]))
                    DVE.after(e)
                    e = DVE.did(DVE.e.tensor_copy(
                        rdx[:, :, :].rearrange("p l (h d) -> p l h d", h=HPT),
                        rden[:, sl].rearrange("p (h l) -> p l h", l=LT).unsqueeze(3).broadcast_to([P, LT, HPT, HD])))
                    item["rdx"] = e

                def normalise(c, oi, ops, mm):
                    i, ps, free = t_ring.take()
                    PE.after(item["rdx"], free)
                    for lt in range(LT):
                        m2 = PE.e.matmul(ps[:, lt * P:(lt + 1) * P], rdx[:, lt, :], ident[:, :], start=True, stop=True)
                    rd_free[0] = PE.did(m2)
                    ACE.after(rd_free[0], oT_done[-1] if oT_done else None)
                    e = t_ring.free[i] = ACE.did(ACE.e.activation(rdT[:, :], ps, ACT.Copy))
                    DVE.after(e, mm)
                    e = o_ring.free[oi] = DVE.did(DVE.e.tensor_tensor(oT[:, c, :], ops, rdT[:, :], ALU.mult))
                    oT_done.append(e)

                for step in range((QH + 1) * LT + 1 + LAG0):
                    turn_at, mix_at = step - LT - 1, step - LT - 1 - LAG0
                    if 0 <= turn_at < QH * LT:
                        turn(*divmod(turn_at, LT))
                    if step < QH * LT:
                        scores(*divmod(step, LT))
                    if mix_at >= 0:
                        mix(*divmod(mix_at, LT))

                SP.after(DVE.last())
                got_next.append(load(mask[:, :, :], t["mask"][following]))
                PE.after(*oT_done)
                wo_done = []
                for lt in range(LT):
                    i, ps, free = s_ring.take()
                    PE.after(free)
                    for c in range(CT):
                        mm = PE.e.matmul(ps, oT[:, c, lt * P:(lt + 1) * P], wo[:, c, :], start=c == 0, stop=c == CT - 1)
                    DVE.after(PE.did(mm), xb_done)
                    e = s_ring.free[i] = DVE.did(DVE.e.tensor_tensor(xin[:, lt, :], ps, xin[:, lt, :], ALU.add))
                    wo_done.append(e)

                e = at_once(norm_stats([xin[:, m, :] for m in range(LT)], wo_done, stats, mv, rstd[:, :],
                                       [scr[:, i, :] for i in range(3)], 1e-6))
                DVE.after(e)
                for m in range(LT):
                    e = DVE.did(DVE.e.tensor_scalar(xin[:, m, :], xin[:, m, :], mv[:, m, 0:1], rstd[:, m:m + 1],
                                                    ALU.subtract, ALU.mult))
                    DVE.after(e)
                    e = DVE.did(DVE.e.tensor_tensor(xin[:, m, :], xin[:, m, :], gamma[:, :], ALU.mult))
                    POOL.after(e)
                    e = POOL.did(POOL.e.tensor_tensor(xin[:, m, :], xin[:, m, :], beta[:, :], ALU.add))
                    SP.after(e)
                    got_next.append(load(xs[b, :, m, :], xin[:, m, :]))
                SP.after(*got_next)
                end_of_step()

        with ExitStack() as ctx:
            w1 = sb("rw_w1", [P, CT, NF * DM], ctx)
            w2 = sb("rw_w2", [P, NF, C], ctx)
            dw1 = sb("rw_dw1", [P, CT, DD], ctx)
            dw2 = sb("rw_dw2", [P, C], ctx)
            W = sb("rw_w", [P, 2, CT, C], ctx)
            xw = sb("rw_x", [P, LT, C], ctx)
            xa = sb("rw_xa", [P, CT, L + 1], ctx)
            sx = sb("rw_sx", [P, CT, L], ctx)
            xf = [sb(f"rw_xf{i}", [P, CT, L], ctx) for i in range(2)]
            xn = xf[1]
            tm = sb("rw_tm", [P, L], ctx)
            tmb = sb("rw_tmb", [P, L], ctx)
            dT = sb("rw_dT", [P, L], ctx)
            S = sb("rw_S", [P, 2, L + 1], ctx)
            kvb = sb("rw_kv", [P, 1, L], ctx)
            rh = sb("rw_rh", [P, 3, L], ctx, F32R)
            rl = sb("rw_rl", [P, 3, L], ctx, F32R)
            tmp = sb("rw_tmp", [P, 2, L], ctx)
            ruk = sb("rw_ruk", [P, LT, HPT], ctx)
            stats = sb("rw_stats", [P, LT, 6], ctx)
            mv = sb("rw_mv", [P, LT, 2], ctx)
            rstd = sb("rw_rstd", [P, LT], ctx)
            small = [sb(f"rw_small{i}", [P, LT], ctx)[:, :] for i in range(3)]
            scr = sb("rw_scr", [P, 3, LT * HPT], ctx)
            gm = sb("rw_gm", [P, 2, LT * HPT], ctx)
            pick = sb("rw_pick", [P, RS, P], ctx, F32R)
            places = sb("rw_places", [P, RS + P], ctx, F32R)

            def place(j):
                return places[:, RS - j:RS - j + P]

            identr = sb("rw_identr", [P, P], ctx, F32R)

            def item_buffers(i):
                return dict(
                    vec=sb(f"rw_vec{i}", [P, V_N, CT], ctx),
                    prev=sb(f"rw_prev{i}", [P, 2, CT], ctx),
                    s0=sb(f"rw_s0{i}", [P, CT, RS], ctx),
                    decay=sb(f"rw_decay{i}", [P, CT, L], ctx),
                    key=sb(f"rw_key{i}", [P, CT, L], ctx),
                    recept=sb(f"rw_recept{i}", [P, CT, L], ctx),
                    gate=sb(f"rw_gate{i}", [P, CT, L], ctx),
                    vh=sb(f"rw_vh{i}", [P, CT, L], ctx, F32R),
                    vl=sb(f"rw_vl{i}", [P, CT, L], ctx, F32R))

            def vector(side, which, c):
                return side["vec"][:, which, c:c + 1]

            sides = [item_buffers(0), item_buffers(1)]

            DVE.did(DVE.e.tensor_copy(identr[:, :], ident[:, :]))
            e = POOL.did(POOL.e.memset(S[:, 0, 0:RS + P], 0.0))
            DVE.after(e)
            DVE.after(DVE.did(DVE.e.tensor_copy(places[:, :], S[:, 0, 0:RS + P])))
            DVE.did(DVE.e.tensor_copy(places[:, RS:].rearrange("p (h i) -> p h i", i=RS)[:, :, 0], headsum[:, :]))
            for j in range(RS):
                DVE.did(DVE.e.tensor_copy(
                    pick[:, j, :].rearrange("p (h i) -> p h i", i=RS),
                    ident[:, :].rearrange("p (h i) -> p h i", i=RS)[:, :, j:j + 1].broadcast_to([P, HPT, RS])))
            DVE.did(DVE.e.memset(tmb[:, :], 0.0))
            DVE.did(DVE.e.memset(dT[:, :], 0.0))
            end_of_step()

            class Stream:

                def __init__(self, order):
                    self.order, self.free, self.last, self.sent, self.used = order, [None, None], list(w_last), 0, 0
                    self.send()
                    self.send()

                def send(self):
                    if self.sent < len(self.order):
                        i = self.sent % 2
                        SP.after(self.free[i])
                        self.last[i] = w_last[i] = load_all([(W[:, i, :, :], t["rw_w"][self.order[self.sent]])], again=self.last[i])
                        self.sent += 1

                def take(self):
                    i = self.used % 2
                    self.used += 1
                    PE.after(self.last[i])
                    return i, W[:, i, :, :]

                def give_back(self, i):
                    self.free[i] = PE.last()
                    self.send()

            w_last = [None, None]
            fixed = {}

            def load_to(name, dst, src, q=None):
                fixed[name] = load_all([(dst, src)], q, again=fixed.get(name))
                return fixed[name]

            def shifted_norm(x, side, ring, vw, vb, row, ready):
                e = yield from norm_stats([x[:, m, :] for m in range(LT)], ready, stats, mv, rstd[:, :], small, 1e-5)
                DVE.after(e)
                done = [DVE.did(DVE.e.tensor_scalar(xn[:, m, :], x[:, m, :], mv[:, m, 0:1], rstd[:, m:m + 1],
                                                    ALU.subtract, ALU.mult)) for m in range(LT)]
                POOL.after(POOL.did(POOL.e.tensor_copy(xa[:, :, 0], side["prev"][:, row, :])))
                yield "step"
                yield "step"
                out = []
                for c in range(CT):
                    i, ps, free = ring.take()
                    PE.after(free)
                    for m in range(LT):
                        PE.after(done[m])
                        mm = transpose(ps[:, m * P:(m + 1) * P], xn[:, m, c * P:(c + 1) * P])
                    ACE.after(PE.did(mm))
                    e = ring.free[i] = ACE.did(ACE.e.activation(xa[:, c, 1:L + 1], ps, ACT.Identity,
                                                                scale=vector(side, vw, c), bias=vector(side, vb, c)))
                    POOL.after(e)
                    out.append(POOL.did(POOL.e.tensor_tensor(sx[:, c, :], xa[:, c, 0:L], xa[:, c, 1:L + 1], ALU.subtract)))
                    yield
                yield "step"
                return out

            def gemm_T(ring, w, x, evac, ready=()):
                for m in range(CT):
                    i, ps, free = ring.take()
                    PE.after(free)
                    for k in range(CT):
                        if m == 0 and ready:
                            PE.after(ready[k])
                        mm = PE.e.matmul(ps, w[:, k, m * P:(m + 1) * P], x[:, k, :], start=k == 0, stop=k == CT - 1)
                    ring.free[i] = evac(m, ps, PE.did(mm))
                    yield

            def gemm_rows(ring, w, x, evac, ready=()):
                for m in range(LT):
                    i, ps, free = ring.take()
                    PE.after(free)
                    for k in range(CT):
                        if m == 0 and ready:
                            PE.after(ready[k])
                        mm = PE.e.matmul(ps, x[:, k, m * P:(m + 1) * P], w[:, k, :], start=k == 0, stop=k == CT - 1)
                    ring.free[i] = evac(m, ps, PE.did(mm))
                    yield

            def load_front(n, side):
                b, layer = n % B, n // B
                SP.after(PE.last(), DVE.last(), POOL.last(), ACE.last())
                return (load_to("xn", xn[:, :, :], xs[b]),
                        load_to("w1", w1[:, :, :], t["rw_w1"][layer]), load_to("w2", w2[:, :, :], t["rw_w2"][layer]),
                        load_to("dw1", dw1[:, :, :], t["rw_dw1"][layer]), load_to("dw2", dw2[:, :], t["rw_dw2"][layer]),
                        load_to(("prev", id(side)), side["prev"][:, :, :], t["prev"][b]),
                        load_to(("vec", id(side)), side["vec"][:, :, :], t["rw_vec"][layer]),
                        load_to(("s0", id(side)), side["s0"][:, :, :], t["s0"][b]))

            def front(side, ring, stream, loaded):
                got_x, got_w1, got_w2, got_dw1, got_dw2, *got_side = loaded
                for q in (DVE, POOL, ACE):
                    q.after(*got_side)
                sx_done = yield from shifted_norm(xn, side, ring, V_LN1W, V_LN1B, 1, [got_x] * LT)

                for c in range(CT):
                    DVE.after(sx_done[c])
                    xx_done = DVE.did(DVE.e.scalar_tensor_tensor(xf[0][:, c, :], sx[:, c, :], vector(side, V_MAAX, c),
                                                                 xa[:, c, 1:L + 1], ALU.mult, ALU.add))
                yield "step"
                PE.after(xx_done, got_w1)
                i, ps, free = ring.take()
                PE.after(free)
                for k in range(CT):
                    mm = PE.e.matmul(ps, w1[:, k, 0:P], xf[0][:, k, :], start=k == 0, stop=k == CT - 1)
                ACE.after(PE.did(mm))
                e = ring.free[i] = ACE.did(ACE.e.activation(tm[:, :], ps, ACT.Tanh))
                yield
                i, ps, free = ring.take()
                PE.after(free)
                for k in range(CT):
                    mm = PE.e.matmul(ps[0:DM, :], w1[:, k, P:P + DM], xf[0][:, k, :], start=k == 0, stop=k == CT - 1)
                xf_free = [PE.did(mm), None]
                ACE.after(xf_free[0])
                e2 = ring.free[i] = ACE.did(ACE.e.activation(tmb[0:DM, :], ps[0:DM, :], ACT.Tanh))
                yield "step"
                PE.after(e, e2, got_w2)

                def mixed(f, slot):
                    out = []
                    for c in range(CT):
                        i, ps, free = ring.take()
                        PE.after(free)
                        mm = PE.e.matmul(ps, w2[:, f, c * P:(c + 1) * P], (tm if f < 4 else tmb)[:, :], start=True, stop=True)
                        DVE.after(PE.did(mm), xf_free[slot])
                        e = ring.free[i] = DVE.did(DVE.e.scalar_tensor_tensor(
                            xf[slot][:, c, :], ps, vector(side, V_MAA + f, c), sx[:, c, :], ALU.add, ALU.mult))
                        POOL.after(e)
                        out.append(POOL.did(POOL.e.tensor_tensor(xf[slot][:, c, :], xf[slot][:, c, :],
                                                                 xa[:, c, 1:L + 1], ALU.add)))
                        yield
                    return out

                ready = yield from mixed(DECAY, 0)

                def decay_rank():
                    i, ps, free = ring.take()
                    PE.after(free, got_dw1)
                    for k in range(CT):
                        PE.after(ready[k])
                        mm = PE.e.matmul(ps[0:DD, :], dw1[:, k, :], xf[0][:, k, :], start=k == 0, stop=k == CT - 1)
                    xf_free[0] = PE.did(mm)
                    ACE.after(xf_free[0])
                    e = ring.free[i] = ACE.did(ACE.e.activation(dT[0:DD, :], ps[0:DD, :], ACT.Tanh))
                    yield
                    return e

                ready_key, dT_done = yield from together(mixed(KEY, 1), decay_rank())
                PE.after(dT_done, got_dw2)
                for c in range(CT):
                    i, ps, free = ring.take()
                    PE.after(free)
                    mm = PE.did(PE.e.matmul(ps, dw2[:, c * P:(c + 1) * P], dT[:, :], start=True, stop=True))
                    ACE.after(mm)
                    e = ring.free[i] = ACE.did(ACE.e.activation(side["decay"][:, c, :], ps, ACT.Exp, bias=vector(side, V_TD, c)))
                    ACE.after(e)
                    ACE.did(ACE.e.activation(side["decay"][:, c, :], side["decay"][:, c, :], ACT.Exp, scale=-1.0))
                    if c % 2:
                        yield

                def copy_to(dst):
                    def evac(m, ps, mm):
                        ACE.after(mm)
                        return ACE.did(ACE.e.activation(dst[:, m, :], ps, ACT.Copy))
                    return evac

                def split_v(m, ps, mm):
                    ACE.after(mm)
                    e = ACE.did(ACE.e.activation(side["vh"][:, m, :], ps, ACT.Copy))
                    DVE.after(e)
                    return DVE.did(DVE.e.tensor_tensor(side["vl"][:, m, :], ps, side["vh"][:, m, :].bitcast(F32), ALU.subtract))
                def gate(m, ps, mm):
                    ACE.after(mm)
                    DVE.after(ACE.did(ACE.e.activation(side["gate"][:, m, :], ps, ACT.Sigmoid)))
                    return DVE.did(DVE.e.tensor_tensor(side["gate"][:, m, :], ps, side["gate"][:, m, :], ALU.mult))
                i, w = stream.take()
                ready_value, _ = yield from together(mixed(VALUE, 0), gemm_T(ring, w, xf[1], copy_to(side["key"]), ready_key))
                stream.give_back(i)
                xf_free[1] = PE.last()
                i, w = stream.take()
                ready_recept, _ = yield from together(mixed(RECEPT, 1), gemm_T(ring, w, xf[0], split_v, ready_value))
                stream.give_back(i)
                xf_free[0] = PE.last()
                i, w = stream.take()
                ready_gate, _ = yield from together(mixed(GATE, 0), gemm_T(ring, w, xf[1], copy_to(side["recept"]), ready_recept))
                stream.give_back(i)
                i, w = stream.take()
                yield from gemm_T(ring, w, xf[0], gate, ready_gate)
                stream.give_back(i)

            def back(n, side, ring, stream, mixes_used):
                b = n % B
                SP.after(DVE.last(), POOL.last())
                got_x = load_to("x", xw[:, :, :], xs[b])
                x_done = [None] * LT

                def add_x(m, ps, mm):
                    DVE.after(mm, got_x)
                    x_done[m] = DVE.did(DVE.e.tensor_tensor(xw[:, m, :], ps, xw[:, m, :], ALU.add))
                    return x_done[m]
                yield "step"
                i, w = stream.take()
                yield from gemm_rows(ring, w, side["recept"], add_x)
                stream.give_back(i)
                sx_done = yield from shifted_norm(xw, side, ring, V_LN2W, V_LN2B, 0, x_done)
                DVE.after(PE.last())
                for c in range(CT):
                    DVE.after(sx_done[c])
                    for v, dst in ((V_FK, xf[0]), (V_FR, xf[1])):
                        e = DVE.did(DVE.e.scalar_tensor_tensor(dst[:, c, :], sx[:, c, :], vector(side, v, c), xa[:, c, 1:L + 1],
                                                               ALU.mult, ALU.add))
                yield "step"
                PE.after(e)

                def relu2(m, ps, mm):
                    ACE.after(mm)
                    e = ACE.did(ACE.e.activation(side["key"][:, m, :], ps, ACT.Relu))
                    POOL.after(e)
                    POOL.did(POOL.e.tensor_tensor(side["key"][:, m, :], side["key"][:, m, :], side["key"][:, m, :], ALU.mult))
                    return e
                i, w = stream.take()
                yield from gemm_T(ring, w, xf[0], relu2)
                stream.give_back(i)
                kk_done = POOL.last()

                def sigmoid(m, ps, mm):
                    ACE.after(mm)
                    return ACE.did(ACE.e.activation(side["decay"][:, m, :], ps, ACT.Sigmoid))
                i, w = stream.take()
                yield from gemm_rows(ring, w, xf[1], sigmoid)
                stream.give_back(i)
                mixes_used()
                PE.after(kk_done)
                DVE.after(ACE.last())

                def add_ffn(m, ps, mm):
                    DVE.after(mm)
                    e = DVE.did(DVE.e.tensor_tensor(side["decay"][:, m, :], ps, side["decay"][:, m, :], ALU.mult))
                    POOL.after(e)
                    POOL.did(POOL.e.tensor_tensor(xw[:, m, :], xw[:, m, :], side["decay"][:, m, :], ALU.add))
                    return e
                i, w = stream.take()
                yield from gemm_rows(ring, w, side["key"], add_ffn)
                stream.give_back(i)
                SP.after(POOL.last())
                fixed["store"] = load_all([(xs[b], xw[:, :, :])], again=fixed.get("store"))
                SP.after(fixed["store"])

            def recurrence(side, work, units):
                bc_ring, y_ring, misc = Ring(bank[0:3]), Ring(bank[3:4]), Ring(bank[4:5])
                S_ring, kv_ring, read_ring = Ring(range(2)), Ring(range(1)), Ring(range(3))
                item, groups = {}, []

                def spread(n):
                    g, j = divmod(n, RS)
                    i, ps, free = bc_ring.take()
                    PE.after(free)
                    PE.e.matmul(ps, pick[:, j, :], side["vh"][:, g, :], start=True, stop=False)
                    item[n] = (i, ps, PE.did(PE.e.matmul(ps, pick[:, j, :], side["vl"][:, g, :], start=False, stop=True)))

                def recur(n):
                    g, j = divmod(n, RS)
                    i, ps, mm = item[n]
                    a, _, free = kv_ring.take()
                    DVE.after(mm, free)
                    e = bc_ring.free[i] = DVE.did(DVE.e.tensor_tensor(kvb[:, a, :], ps, side["key"][:, g, :], ALU.mult))
                    s, _, free = S_ring.take()
                    ACE.after(free)
                    e0 = ACE.did(ACE.e.activation(S[:, s, 0:1], side["s0"][:, g, j:j + 1], ACT.Copy))
                    DVE.after(e, free)
                    e = kv_ring.free[a] = DVE.did(DVE.e.tensor_tensor_scan(
                        S[:, s, 1:L + 1], side["decay"][:, g, :], kvb[:, a, :], side["s0"][:, g, j:j + 1], ALU.mult, ALU.add))
                    POOL.after(e, e0)
                    item[n] = (s, POOL.did(POOL.e.tensor_tensor(S[:, s, 0:L], S[:, s, 0:L], side["recept"][:, g, :], ALU.mult)))

                def round_read(n):
                    s, e = item[n]
                    a, _, free = read_ring.take()
                    ACE.after(e, free)
                    item[n] = (s, a, ACE.did(ACE.e.activation(rh[:, a, :], S[:, s, 0:L], ACT.Copy)))

                def rest_of_read(n):
                    s, a, e = item[n]
                    DVE.after(e)
                    e = S_ring.free[s] = DVE.did(DVE.e.tensor_tensor(rl[:, a, :], S[:, s, 0:L], rh[:, a, :].bitcast(F32),
                                                                     ALU.subtract))
                    item[n] = (a, e)

                def read(n):
                    g, j = divmod(n, RS)
                    a, e = item.pop(n)
                    if j == 0:
                        item["y"] = y_ring.take()
                        PE.after(item["y"][2])
                    yi, yps, _ = item["y"]
                    PE.after(e)
                    PE.e.matmul(yps, place(j), rh[:, a, :], start=j == 0, stop=False)
                    mm = PE.e.matmul(yps, place(j), rl[:, a, :], start=False, stop=j == RS - 1)
                    read_ring.free[a] = mm = PE.did(mm)
                    if j == RS - 1:
                        groups.append(group(g, yi, yps, mm))

                def group(g, yi, yps, y_mm):
                    G = LT * HPT
                    ta, tb = tmp[:, 0, :], tmp[:, 1, :]
                    rows = ta.rearrange("p (g j) -> p g j", g=G)
                    per_row = lambda x: x.unsqueeze(2).broadcast_to([P, G, RS])
                    ruk_flat = ruk[:, :, :].rearrange("p m h -> p (m h)")
                    DVE.after(PE.last())
                    e = DVE.did(DVE.e.scalar_tensor_tensor(ta, side["recept"][:, g, :], vector(side, V_U, g), side["key"][:, g, :],
                                                           ALU.mult, ALU.mult))
                    ACE.after(y_mm)
                    ey = y_ring.free[yi] = ACE.did(ACE.e.activation(tb, yps, ACT.Copy))
                    yield
                    i, ps, free = misc.take()
                    PE.after(e, free)
                    for m in range(LT):
                        mm = PE.e.matmul(ps[:, m * HPT:(m + 1) * HPT], ta[:, m * P:(m + 1) * P], headsum[:, :],
                                         start=True, stop=True)
                    DVE.after(PE.did(mm))
                    e = misc.free[i] = DVE.did(DVE.e.tensor_copy(ruk_flat, ps[:, 0:G]))
                    yield
                    i, ps, free = misc.take()
                    PE.after(free)
                    for m in range(LT):
                        for v in (side["vh"], side["vl"]):
                            mm = PE.e.matmul(ps[:, m * P:(m + 1) * P], v[:, g, m * P:(m + 1) * P], identr[:, :],
                                             start=v is side["vh"], stop=v is side["vl"])
                    DVE.after(PE.did(mm), e)
                    e = misc.free[i] = DVE.did(DVE.e.tensor_tensor(rows, ps.rearrange("p (g j) -> p g j", g=G),
                                                                   per_row(ruk_flat), ALU.mult))
                    yield
                    i, ps, free = misc.take()
                    PE.after(ey, free)
                    for m in range(LT):
                        mm = transpose(ps[:, m * P:(m + 1) * P], tb[:, m * P:(m + 1) * P])
                    mm = PE.did(mm)
                    DVE.after(e, mm)
                    e = misc.free[i] = DVE.did(DVE.e.tensor_tensor(ta, ps, ta, ALU.add))
                    yield
                    DVE.after(e)
                    e = DVE.did(DVE.e.tensor_reduce(gm[:, 0, :], rows, axis=AX.X, op=ALU.add))
                    DVE.after(e)
                    e = DVE.did(DVE.e.tensor_scalar_mul(gm[:, 0, :], gm[:, 0, :], 1.0 / RS))
                    DVE.after(e)
                    e = DVE.did(DVE.e.tensor_tensor(rows, rows, per_row(gm[:, 0, :]), ALU.subtract))
                    ACE.after(e, mm)
                    e = ACE.did(ACE.e.activation(tb, ta, ACT.Square))
                    yield
                    DVE.after(e)
                    e = DVE.did(DVE.e.tensor_reduce(gm[:, 1, :], tb.rearrange("p (g j) -> p g j", g=G), axis=AX.X, op=ALU.add))
                    DVE.after(e)
                    e = yield from rsqrt(gm[:, 1, :], [scr[:, q, :] for q in range(3)], 1e-5, 1.0 / RS)
                    DVE.after(e)
                    e = DVE.did(DVE.e.tensor_tensor(rows, rows, per_row(gm[:, 1, :]), ALU.mult))
                    yield
                    yield
                    i, ps, free = misc.take()
                    PE.after(e, free)
                    for m in range(LT):
                        mm = transpose(ps[:, m * P:(m + 1) * P], ta[:, m * P:(m + 1) * P])
                    ACE.after(PE.did(mm))
                    yg = side["recept"][:, g, :]
                    e = misc.free[i] = ACE.did(ACE.e.activation(yg, ps, ACT.Identity, scale=vector(side, V_GNW, g),
                                                                bias=vector(side, V_GNB, g)))
                    POOL.after(e)
                    POOL.did(POOL.e.tensor_tensor(yg, yg, side["gate"][:, g, :], ALU.mult))

                N = CT * RS
                credit, going = 0.0, work is not None
                spread(0)
                n = 0
                while n < N + 3 or groups or going:
                    if n + 1 < N:
                        spread(n + 1)
                    if 2 <= n <= N + 1:
                        rest_of_read(n - 2)
                    if n < N:
                        recur(n)
                    if 1 <= n <= N:
                        round_read(n - 1)
                    for _ in range(1 if n < N else 2):
                        groups[:] = [g for g in groups if next(g, "end") != "end"]
                    credit += units / N if n < N else 1.0 if n < N + 3 or groups else 10.0
                    while going and credit >= 1.0:
                        credit -= 1.0
                        got = next(work, "end")
                        going = got != "end"
                        if got == "step":
                            break
                    if 3 <= n <= N + 2:
                        read(n - 3)
                    n += 1

            def meet():
                ends = [q.last() for q in (PE, DVE, ACE, POOL)]
                for q in queues:
                    q.after(*ends)

            def chained(*parts):
                for part in parts:
                    yield from part

            def weights(n, has_back, has_front):
                back_layer, front_layer = (n - 1) // B, (n + 1) // B
                return ([(back_layer, w) for w in (W_O, W_FK, W_FR, W_FV)] if has_back else []) + \
                       ([(front_layer, w) for w in (W_K, W_V, W_R, W_G)] if has_front else [])

            def bodies(*which):
                stream = Stream([w for n, _, _, has_back, has_front in which for w in weights(n, has_back, has_front)])
                for n, side, other, has_back, has_front in which:
                    meet()
                    ring, parts, loaded = Ring(bank[5:8]), [], []

                    def start_loads(n=n, other=other, loaded=loaded):
                        loaded.extend(load_front(n + 1, other))

                    if has_back:
                        parts.append(back(n - 1, other, ring, stream, start_loads if has_front else lambda: None))
                    elif has_front:
                        start_loads()
                    if has_front:
                        parts.append(front(other, ring, stream, loaded))
                    if side is None:
                        at_once(chained(*parts))
                    else:
                        recurrence(side, chained(*parts), UNITS * (has_back + has_front) / 2)
                end_of_step()
                fixed.clear()
                w_last[:] = [None, None]

            UNITS = 64
            A, Z = sides
            bodies((-1, None, A, False, True), (0, A, Z, False, True))
            with nc.Fori(0, (NL * B - 2) // 2) as i:
                bodies((2 * i + 1, Z, A, True, True), (2 * i + 2, A, Z, True, True))
            bodies((NL * B - 1, Z, A, True, False), (NL * B, None, Z, True, False))

        with ExitStack() as ctx:
            wq = sb("l3_wq", [P, CT, C], ctx)
            wk = sb("l3_wk", [P, CT, C], ctx)
            wv = sb("l3_wv", [P, CT, C], ctx)
            wo = sb("l3_wo", [P, CT, C], ctx)
            m1 = sb("l3_m1", [P, CT, MLP], ctx)
            vec = sb("l3_vec", [P, 3 * CT + MT], ctx)
            bv = sb("l3_bv", [P, C], ctx)
            bo = sb("l3_bo", [P, C], ctx)
            b2 = sb("l3_b2", [P, C], ctx)
            hT = sb("l3_hT", [P, CT, NK], ctx)
            vt = sb("l3_v", [P, NK // P, C], ctx)
            qf = sb("l3_qf", [P, 2, L], ctx)
            rest = sb("l3_rest", [P, 2, L], ctx)
            parts = sb("l3_parts", [P, 2, 3, L], ctx, BF16)
            mi = sb("l3_mi", [P, L], ctx, I32)
            mb = sb("l3_mb", [P, NK], ctx)
            SR = 3
            stack = sb("l3_stack", [P, SR, 2, L + NK], ctx, BF16)
            nz = sb("l3_nz", [P, 2, NK], ctx)
            xnext = nz[:, :, :].rearrange("p a (m c) -> p (a m) c", c=C)
            pr = sb("l3_p", [P, 2 * LT, NK], ctx)
            pT = sb("l3_pT", [P, LAG3 + 1, L], ctx)
            nmax = sb("l3_nmax", [P, LT * PH], ctx)
            den = sb("l3_den", [P, LT * PH], ctx)
            rden = sb("l3_rden", [P, LT * PH], ctx)
            rdx = sb("l3_rdx", [P, LT, P], ctx)
            rdT = sb("l3_rdT", [P, L], ctx)
            oT = sb("l3_oT", [P, CT, L], ctx)
            att = sb("l3_att", [P, LT, C], ctx)
            nT = oT
            st_flat = stack[:, :, :, :].rearrange("p a b c -> p (a b c)").bitcast(F32)
            m2s = [st_flat[:, a * 2 * C:(a + 1) * 2 * C].rearrange("p (k c) -> p k c", k=2) for a in range(2)]
            ss = sb("l3_ss", [P, LT], ctx)
            scr = sb("l3_scr", [P, 3, LT], ctx)
            h1 = [pr[:, m // 2, (m % 2) * L:(m % 2 + 1) * L] for m in range(MT)]

            SP.after(load(wq[:, :, :], t["l3_wq"]), load(wk[:, :, :], t["l3_wk"], ACE), load(wv[:, :, :], t["l3_wv"]),
                     load(wo[:, :, :], t["l3_wo"], ACE), load(m1[:, :, :], t["l3_m1"]), load(vec[:, :], t["l3_vec"], ACE),
                     load(bv[:, :], t["l3_bv"].partition_broadcast(P)), load(bo[:, :], t["l3_bo"].partition_broadcast(P)),
                     load(b2[:, :], t["l3_b2"].partition_broadcast(P)),
                     load(hT[:, :, 0:L], t["cT"][0]), load(xnext, xs[0]))
            DVE.did(DVE.e.memset(mb[:, L:NK], 0.0))
            end_of_step()

            with nc.Fori(0, B) as b:
                following = (b + 1) % B
                got_m = load(mi[:, :], t["keymask"][b].partition_broadcast(P), ACE)
                got_x = load(att[:, :, :], xs[b])
                ring = Ring(bank)
                for c in range(CT):
                    i, ps, free = ring.take()
                    PE.after(free)
                    for m in range(LT):
                        mm = transpose(ps[:, m * P:(m + 1) * P], xnext[:, m, c * P:(c + 1) * P])
                    ACE.after(PE.did(mm))
                    ring.free[i] = l_done = ACE.did(ACE.e.activation(hT[:, c, L:NK], ps, ACT.Copy))
                DVE.after(got_m)
                e = DVE.did(DVE.e.tensor_single_scalar(mb[:, 0:L], mi[:, :], 0.0, ALU.is_equal))
                DVE.after(e)
                mb_done = DVE.did(DVE.e.tensor_scalar_mul(mb[:, 0:L], mb[:, 0:L], MASKED))
                qf_ring, part_ring = Ring(range(2)), Ring(range(2))
                PE.after(l_done)
                stored_parts = []
                for m in range(CT):
                    for half in (0, 1, None):
                        i, ps, free = ring.take()
                        PE.after(free)
                        w, o = (wq, L) if half is None else (wk, half * L)
                        for k in range(CT):
                            mm = PE.e.matmul(ps, w[:, k, m * P:(m + 1) * P], hT[:, k, o:o + L], start=k == 0, stop=k == CT - 1)
                        a, _, free = qf_ring.take()
                        DVE.after(PE.did(mm), free)
                        if half is None:
                            e = DVE.did(DVE.e.tensor_scalar(qf[:, a, :], ps, vec[:, m:m + 1], 1.0 / PD, ALU.add, ALU.mult))
                            dst = q_parts[:, m * P:(m + 1) * P, :]
                        else:
                            e = DVE.did(DVE.e.tensor_scalar_add(qf[:, a, :], ps, vec[:, CT + m:CT + m + 1]))
                            dst = k3_parts[:, m * P:(m + 1) * P, half * L:(half + 1) * L]
                        ring.free[i] = e
                        p, _, free = part_ring.take()
                        e = qf_ring.free[a] = split3(qf[:, a, :], e, rest[:, a, :], [parts[:, p, n, :] for n in range(3)], free)
                        SP.after(e)
                        part_ring.free[p] = load(dst.rearrange("n p l -> p n l"), parts[:, p, :, :])
                        stored_parts.append(part_ring.free[p])
                st_ring = Ring(range(SR))
                st_last = [None] * SR

                def fetch(h):
                    i, _, free = st_ring.take()
                    m = h // 4
                    SP.after(free, *stored_parts[3 * m:3 * m + 3])
                    d = slice(h * PD, (h + 1) * PD)
                    pairs = []
                    for st, (qn, kn) in enumerate((((0, 0, 0), (0, 1, 2)), ((1, 1, 2), (0, 1, 0)))):
                        for slot in range(3):
                            rows = slice(slot * PD, (slot + 1) * PD)
                            pairs.append((stack[rows, i, st, 0:L], q_parts[qn[slot], d, :]))
                            pairs.append((stack[rows, i, st, L:], k3_parts[kn[slot], d, :]))
                    st_last[i] = load_all(pairs, again=st_last[i])
                    item[("st", h)] = (i, st_last[i])
                item = {}
                for s in range(NK // P):
                    i, ps, free = ring.take()
                    PE.after(free)
                    for k in range(CT):
                        mm = PE.e.matmul(ps, hT[:, k, s * P:(s + 1) * P], wv[:, k, :], start=k == 0, stop=k == CT - 1)
                    DVE.after(PE.did(mm))
                    ring.free[i] = v_done = DVE.did(DVE.e.tensor_tensor(vt[:, s, :], ps, bv[:, :], ALU.add))
                for m in range(LT):
                    DVE.after(got_x)
                    at_done = DVE.did(DVE.e.tensor_tensor(att[:, m, :], att[:, m, :], bo[:, :], ALU.add))
                PE.after(v_done)
                DVE.after(mb_done)

                s_ring = Ring([psum[:, 0:2 * BANK], psum[:, 2 * BANK:4 * BANK]])
                t_ring, o_ring = Ring(bank[4:7]), Ring(bank[7:8])
                for r in (s_ring, t_ring, o_ring):
                    r.free = [v_done] * len(r.bufs)
                nz_ring, pr_ring, pT_ring = Ring(range(2)), Ring(range(2 * LT)), Ring(range(LAG3 + 1))
                oT_done = []
                rd_free = [None]
                KT = NK // P

                def scores(h, lt):
                    n = h * LT + lt
                    si, got = item[("st", h)]
                    i, ps, free = s_ring.take()
                    PE.after(free, got)
                    for half in range(2):
                        for st in range(2):
                            mm = PE.e.matmul(ps[:, half * L:(half + 1) * L], stack[0:3 * PD, si, st, lt * P:(lt + 1) * P],
                                             stack[0:3 * PD, si, st, L + half * L:L + (half + 1) * L],
                                             start=st == 0, stop=st == 1)
                    mm = PE.did(mm)
                    if lt == LT - 1:
                        st_ring.free[si] = mm
                    a, _, freed = nz_ring.take()
                    DVE.after(mm, freed)
                    z = s_ring.free[i] = DVE.did(DVE.e.tensor_tensor_reduce(
                        out=nz[:, a, :], in0=ps, in1=mb[:, :], scale=-1.0, scalar=3.0e38,
                        op0=ALU.add, op1=ALU.min, accum_out=nmax[:, n:n + 1]))
                    i, _, freed = pr_ring.take()
                    ACE.after(z, freed)
                    e = nz_ring.free[a] = ACE.did(ACE.e.activation(pr[:, i, :], nz[:, a, :], ACT.Exp, scale=-1.0,
                                                                   bias=nmax[:, n:n + 1], accum_out=den[:, n:n + 1]))
                    item[(h, lt)] = (i, e)

                def turn(h, s):
                    j, ps, free = t_ring.take()
                    PE.after(free)
                    for lt in range(LT):
                        i, e = item[(h, lt)]
                        PE.after(e)
                        mm = transpose(ps[:, lt * P:(lt + 1) * P], pr[:, i, s * P:(s + 1) * P])
                    mm = PE.did(mm)
                    if s == KT - 1:
                        for lt in range(LT):
                            i, e = item.pop((h, lt))
                            pr_ring.free[i] = mm
                        if h % 4 == 3:
                            spread_sums(h // 4, e)
                    k, _, freed = pT_ring.take()
                    if s % 2:
                        DVE.after(mm, freed)
                        e = DVE.did(DVE.e.tensor_copy(pT[:, k, :], ps))
                    else:
                        ACE.after(mm, freed)
                        e = ACE.did(ACE.e.activation(pT[:, k, :], ps, ACT.Copy))
                    t_ring.free[j] = e
                    item[("pT", h, s)] = (k, e)

                def mix(h, s):
                    k, e = item.pop(("pT", h, s))
                    c, r = divmod(h, 4)
                    if r == 0 and s == 0:
                        item["o"] = o_ring.take()
                        PE.after(item["o"][2])
                    oi, ops, _ = item["o"]
                    PE.after(e)
                    mm = PE.e.matmul(ops[PD * r:PD * (r + 1), :], vt[:, s, h * PD:(h + 1) * PD], pT[:, k, :],
                                     start=s == 0, stop=s == KT - 1)
                    pT_ring.free[k] = mm = PE.did(mm)
                    if r == 3 and s == KT - 1:
                        normalise(c, oi, ops, mm)

                def spread_sums(c, summed):
                    sl = slice(c * 4 * LT, (c + 1) * 4 * LT)
                    DVE.after(summed, rd_free[0])
                    e = DVE.did(DVE.e.reciprocal(rden[:, sl], den[:, sl]))
                    DVE.after(e)
                    e = DVE.did(DVE.e.tensor_copy(
                        rdx[:, :, :].rearrange("p l (h d) -> p l h d", h=4),
                        rden[:, sl].rearrange("p (h l) -> p l h", l=LT).unsqueeze(3).broadcast_to([P, LT, 4, PD])))
                    item["rdx"] = e

                def normalise(c, oi, ops, mm):
                    i, ps, free = t_ring.take()
                    PE.after(item["rdx"], free)
                    for lt in range(LT):
                        m2_ = PE.e.matmul(ps[:, lt * P:(lt + 1) * P], rdx[:, lt, :], ident[:, :], start=True, stop=True)
                    rd_free[0] = PE.did(m2_)
                    ACE.after(rd_free[0], oT_done[-1] if oT_done else None)
                    e = t_ring.free[i] = ACE.did(ACE.e.activation(rdT[:, :], ps, ACT.Copy))
                    DVE.after(e, mm)
                    e = o_ring.free[oi] = DVE.did(DVE.e.tensor_tensor(oT[:, c, :], ops, rdT[:, :], ALU.mult))
                    oT_done.append(e)

                fetch(0)
                fetch(1)
                for step in range((PH + 1) * KT + 1 + LAG3):
                    turn_at, mix_at = step - KT - 1, step - KT - 1 - LAG3
                    if step % KT == 0 and step // KT + 2 < PH:
                        fetch(step // KT + 2)
                    if 0 <= turn_at < PH * KT:
                        turn(*divmod(turn_at, KT))
                    if step < PH * KT and step % 2 == 0:
                        h, s = divmod(step, KT)
                        scores(h, s // 2)
                    if mix_at >= 0:
                        mix(*divmod(mix_at, KT))

                PE.after(*oT_done)
                for lt in range(LT):
                    i, ps, free = t_ring.take()
                    PE.after(free)
                    for c in range(CT):
                        mm = PE.e.matmul(ps, oT[:, c, lt * P:(lt + 1) * P], wo[:, c, :], start=c == 0, stop=c == CT - 1)
                    DVE.after(PE.did(mm), at_done)
                    e = t_ring.free[i] = DVE.did(DVE.e.tensor_tensor(att[:, lt, :], ps, att[:, lt, :], ALU.add))
                    ACE.after(e)
                    ACE.after(ACE.did(ACE.e.activation(qf[:, 0, :], att[:, lt, :], ACT.Square, accum_out=ss[:, lt:lt + 1])))

                DVE.after(ACE.last())
                e = at_once(rsqrt(ss[:, :], [scr[:, i, :] for i in range(3)], 1e-6, 1.0 / C))
                DVE.after(e)
                ring = Ring(bank)
                PE.after(DVE.last(), ACE.last())
                for m in range(LT):
                    an_done = DVE.did(DVE.e.tensor_scalar_mul(att[:, m, :], att[:, m, :], ss[:, m:m + 1]))
                PE.after(an_done)
                for c in range(CT):
                    i, ps, free = ring.take()
                    PE.after(free)
                    for m in range(LT):
                        mm = transpose(ps[:, m * P:(m + 1) * P], att[:, m, c * P:(c + 1) * P])
                    DVE.after(PE.did(mm))
                    ring.free[i] = n_done = DVE.did(DVE.e.tensor_scalar_mul(nT[:, c, :], ps, vec[:, 2 * CT + c:2 * CT + c + 1]))
                SP.after(PE.last(), ACE.last(), DVE.last())
                got_next = [load(hT[:, :, 0:L], t["cT"][following]), load(xnext, xs[following])]
                SP.after(PE.last())
                got_x = load(att[:, :, :], xs[b])
                DVE.after(got_x)
                for m in range(LT):
                    r_done = DVE.did(DVE.e.tensor_tensor(att[:, m, :], att[:, m, :], b2[:, :], ALU.add))
                PE.after(n_done)
                h_done = []
                for m in range(MT):
                    i, ps, free = ring.take()
                    PE.after(free)
                    for k in range(CT):
                        mm = PE.e.matmul(ps, m1[:, k, m * P:(m + 1) * P], nT[:, k, :], start=k == 0, stop=k == CT - 1)
                    ACE.after(PE.did(mm))
                    ring.free[i] = e = ACE.did(ACE.e.activation(h1[m], ps, ACT.Gelu_apprx_tanh,
                                                                bias=vec[:, 3 * CT + m:3 * CT + m + 1]))
                    h_done.append(e)
                m2_free, m2_last = [None, None], [None, None]
                SP.after(*oT_done)
                for q in range(MT // 2):
                    a = q % 2
                    SP.after(m2_free[a])
                    m2_last[a] = load_all([(m2s[a], t["l3_m2"][q])], again=m2_last[a])
                    PE.after(m2_last[a], h_done[2 * q + 1])
                    if q == 0:
                        PE.after(*h_done[-8:])
                    for m in range(LT):
                        for k in range(2):
                            mm = PE.e.matmul(bank[m], h1[2 * q + k][:, m * P:(m + 1) * P], m2s[a][:, k, :],
                                             start=q == 0 and k == 0, stop=q == MT // 2 - 1 and k == 1)
                    m2_free[a] = PE.did(mm)
                DVE.after(PE.last(), r_done)
                for m in range(LT):
                    e = DVE.did(DVE.e.tensor_tensor(att[:, m, :], bank[m], att[:, m, :], ALU.add))
                SP.after(e)
                SP.e.dma_start(t["out"][b], att[:, :, :]).then_inc(store_sem, 16)
                SP.after(*got_next)
                end_of_step(stored=16)


def lay_out(inputs):
    import numpy as np
    a = {k: np.asarray(v) for k, v in inputs.items()}

    def w_tiles(w):
        return w.reshape(-1, P, w.shape[1]).transpose(1, 0, 2)

    def cols(v):
        return v.reshape(-1, P).T

    def tokens(x):
        return x.reshape(B, LT, P, -1).transpose(0, 2, 1, 3)

    def chans(x):
        return x.transpose(0, 2, 1).reshape(B, CT, P, L).transpose(0, 2, 1, 3)

    x, ctx = a["x"], a["ctx_2048"]
    o = {"x": tokens(x), "xT": chans(x), "cT": chans(ctx), "mask": tokens(a["mask_Bx1xSxS2_ff0"][:, 0]),
         "keymask": a["mask_BxS2_ik0"]}
    p = "L0_xattn_"
    o["l0_wq"], o["l0_wv"], o["l0_wo"] = (w_tiles(a[p + n]) for n in ("Wq", "Wv", "Wo"))
    o["l0_wk"], o["l0_bk"], o["l0_bq"] = w_tiles(a[p + "Wk"]), cols(a[p + "bk"]), cols(a[p + "bq"])
    for n in ("bv", "bo", "gamma", "beta"):
        o["l0_" + n] = a[p + n]

    both = {"w1": [], "w2": [], "dw1": [], "dw2": [], "w": [], "vec": []}
    for layer, order in ((1, (0, 1, 2, 3, 4)), (2, (1, 0, 2, 3, 4))):
        p = f"L{layer}_xattn_"
        ffn = p + ("f" if layer == 1 else "ffn_")
        if layer == 1:
            maa = [a[p + "maa_" + n] for n in "wkvrg"]
        else:
            maa = [a[p + "maa_stack"][f] for f in order]
        order = list(order)
        both["w1"].append(w_tiles(a[p + "maa_w1"].reshape(C, NF, DM)[:, order].reshape(C, NF * DM)))
        w2 = np.zeros((P, NF, C), np.float32)
        for f in range(NF):
            w2[DM * f % P:DM * f % P + DM, f] = a[p + "maa_w2"][order[f]]
        both["w2"].append(w2)
        both["dw1"].append(w_tiles(a[p + "decay_w1"]))
        both["dw2"].append(np.concatenate([a[p + "decay_w2"], np.zeros((P - DD, C), np.float32)]))
        both["w"].append(np.stack([w_tiles(a[n].T) for n in (p + "Wr", p + "Wk", p + "Wv", p + "Wg", p + "Wo",
                                                            ffn + "Wk", ffn + "Wr", ffn + "Wv")]))
        v = [a[p + "ln1_w"], a[p + "ln1_b"], a[p + "maa_x"], *maa, a[p + "time_decay"], a[p + "faaaa"].reshape(C),
             a[p + "gn_w"], a[p + "gn_b"], a[p + "ln2_w"], a[p + "ln2_b"], a[ffn + "maa_k"], a[ffn + "maa_r"]]
        both["vec"].append(np.stack([cols(u) for u in v], axis=1))
    for n, v in both.items():
        o["rw_" + n] = np.stack(v)
    o["prev"] = ctx[:, 0:2].reshape(B, 2, CT, P).transpose(0, 3, 1, 2)
    o["s0"] = ctx[:, 2:2 + RS].reshape(B, CT, P, RS).transpose(0, 2, 1, 3)

    p = "L3_xattn_"
    kv = a[p + "kv_w"].reshape(C, C, 2)
    kvb = a[p + "kv_b"].reshape(C, 2)
    o["l3_wq"], o["l3_wo"], o["l3_m1"] = (w_tiles(a[p + n]) for n in ("q_w", "out_w", "mlp_w1"))
    o["l3_wk"], o["l3_wv"] = w_tiles(kv[:, :, 0]), w_tiles(kv[:, :, 1])
    o["l3_m2"] = a[p + "mlp_w2"].reshape(MT // 2, 2, P, C).transpose(0, 2, 1, 3)
    o["l3_vec"] = np.concatenate([cols(a[p + "q_b"]), cols(kvb[:, 0]), cols(a[p + "postnorm_w"]), cols(a[p + "mlp_b1"])], axis=1)
    o["l3_bv"], o["l3_bo"], o["l3_b2"] = kvb[:, 1], a[p + "out_b"], a[p + "mlp_b2"]
    return {k: np.ascontiguousarray(v) for k, v in o.items()}


def kernel(**inputs):
    import concourse.bacc as bacc
    from concourse.bass_utils import run_bass_kernel_spmd

    nc = bacc.Bacc("TRN2", target_bir_lowering=False, num_devices=1)
    arrays = lay_out(inputs)
    t = {n: nc.dram_tensor("in_" + n, v.shape, mybir.dt.from_np(v.dtype), kind="ExternalInput").ap()
         for n, v in arrays.items()}
    t["out"] = nc.dram_tensor("out", (B, P, LT, C), F32, kind="ExternalOutput").ap()
    program(nc, t)
    r = run_bass_kernel_spmd(nc, [{"in_" + n: v for n, v in arrays.items()}], core_ids=[0])
    return r.results[0]["out"].transpose(0, 2, 1, 3).reshape(B, L, C)
```
